# Optimizing a Trainium2 kernel written in Bass

```python
import numpy as np
import jax
import jax.numpy as jnp

def _softmax(x, axis=-1):
    return jax.nn.softmax(x, axis=axis)

def _gelu(x):
    return jax.nn.gelu(x, approximate=True)

def _silu(x):
    return jax.nn.silu(x)

def _sigmoid(x):
    return jax.nn.sigmoid(x)

def _layernorm(x, axis=-1, eps=1e-05):
    m = jnp.mean(x, axis=axis, keepdims=True)
    v = jnp.var(x, axis=axis, keepdims=True)
    return (x - m) / jnp.sqrt(v + eps)

def _scatter_add(tgt, idx, src, axis=0):
    return tgt.at[idx].add(src)

def _segment_sum(src, seg, n):
    return jax.ops.segment_sum(src, seg, n)
kernel_name = 'mk_gnn_ffn_d1_gnn_r8_714051'

def setup_inputs(seed: int=0):
    np.random.seed(seed)
    _w = jnp.asarray

    def _rec_inputs():
        import jax
        import jax.numpy as jnp
        _gk = jax.random.key(seed)
        x = -6.415e-05 + 1 * jax.random.normal(jax.random.fold_in(_gk, 1), (1250, 512), jnp.float32)
        src = jax.random.randint(jax.random.fold_in(_gk, 2), (20000,), 0, 1250, jnp.int32)
        dst = jnp.minimum((1250 * jax.random.uniform(jax.random.fold_in(_gk, 3), (20000,)) ** 2.0).astype(jnp.int32), 9999)
        _o = jnp.argsort(dst, stable=True)
        src = src[_o]
        dst = dst[_o]
        edge_attr_128 = -0.00010739 + 0.99994 * jax.random.normal(jax.random.fold_in(_gk, 11), (20000, 128), jnp.float32)
        return (x, src, dst, edge_attr_128)
    x, src, dst, edge_attr_128 = _rec_inputs()

    def _L0_gnn_setup():
        import jax, jax.numpy as jnp
        import numpy as np
        N_NODES = 2500
        N_EDGES = 12500
        IN = 512
        HID = 512
        OUT = 512
        EF = 128
        NH = 16
        HEAD = OUT // NH

        def _ln(x):
            mu = jnp.mean(x, axis=-1, keepdims=True)
            var = jnp.var(x, axis=-1, keepdims=True)
            return (x - mu) / jnp.sqrt(var + 1e-05)

        def _mlp(x, W1, b1, g, be, W2, b2):
            hdn = x @ W1 + b1
            hdn = _ln(hdn) * g + be
            hdn = jax.nn.relu(hdn)
            return hdn @ W2 + b2
        key = jax.random.key(seed)
        ks = jax.random.split(key, 16)

        def w(k, i, o):
            return jax.random.normal(k, (i, o), jnp.float32) / np.float32(np.sqrt(i))
        inp = {'h': jax.random.normal(ks[0], (N_NODES, IN), jnp.float32), 'edge_feat': jax.random.normal(ks[1], (N_EDGES, EF), jnp.float32), 'edge_index': jax.random.randint(ks[2], (2, N_EDGES), 0, N_NODES, jnp.int32)}
        inp['hk_W1'] = w(ks[3], IN + EF, HID)
        inp['hk_b1'] = jnp.zeros((HID,), jnp.float32)
        inp['hk_g'] = jnp.ones((HID,), jnp.float32)
        inp['hk_be'] = jnp.zeros((HID,), jnp.float32)
        inp['hk_W2'] = w(ks[4], HID, OUT)
        inp['hk_b2'] = jnp.zeros((OUT,), jnp.float32)
        inp['hv_W1'] = w(ks[5], IN + EF, HID)
        inp['hv_b1'] = jnp.zeros((HID,), jnp.float32)
        inp['hv_g'] = jnp.ones((HID,), jnp.float32)
        inp['hv_be'] = jnp.zeros((HID,), jnp.float32)
        inp['hv_W2'] = w(ks[6], HID, OUT)
        inp['hv_b2'] = jnp.zeros((OUT,), jnp.float32)
        inp['hq_W1'] = w(ks[7], IN, HID)
        inp['hq_b1'] = jnp.zeros((HID,), jnp.float32)
        inp['hq_g'] = jnp.ones((HID,), jnp.float32)
        inp['hq_be'] = jnp.zeros((HID,), jnp.float32)
        inp['hq_W2'] = w(ks[8], HID, OUT)
        inp['hq_b2'] = jnp.zeros((OUT,), jnp.float32)
        inp['no_W1'] = w(ks[9], 2 * HID, HID)
        inp['no_b1'] = jnp.zeros((HID,), jnp.float32)
        inp['no_g'] = jnp.ones((HID,), jnp.float32)
        inp['no_be'] = jnp.zeros((HID,), jnp.float32)
        inp['no_W2'] = w(ks[10], HID, HID)
        inp['no_b2'] = jnp.zeros((HID,), jnp.float32)
        return inp
    _L0_gnn_all = _L0_gnn_setup()
    _L0_gnn_in = {k: v for k, v in _L0_gnn_all.items() if k in ('hk_W1', 'hk_b1', 'hk_g', 'hk_be', 'hk_W2', 'hk_b2', 'hv_W1', 'hv_b1', 'hv_g', 'hv_be', 'hv_W2', 'hv_b2', 'hq_W1', 'hq_b1', 'hq_g', 'hq_be', 'hq_W2', 'hq_b2', 'no_W1', 'no_b1', 'no_g', 'no_be', 'no_W2', 'no_b2')}
    del _L0_gnn_all

    def _L0_ffn_setup():
        import jax, jax.numpy as jnp
        import numpy as np
        B, S, D, F, E = (4, 256, 512, 256, 8)
        key = jax.random.key(seed)
        k = jax.random.split(key, 5)
        x = jax.random.normal(k[0], (B, S, D), dtype=jnp.float32)
        Ws = jax.random.normal(k[1], (D, E), dtype=jnp.float32) * 0.02
        bs = jnp.zeros((E,), dtype=jnp.float32)
        W1 = jax.random.normal(k[2], (E, D, F), dtype=jnp.float32) * 0.02
        b1 = jnp.zeros((E, F), dtype=jnp.float32)
        W2 = jax.random.normal(k[3], (E, F, D), dtype=jnp.float32) * 0.02
        b2 = jnp.zeros((E, D), dtype=jnp.float32)
        return {'x': x, 'Ws': Ws, 'bs': bs, 'W1': W1, 'b1': b1, 'W2': W2, 'b2': b2}
    _L0_ffn_all = _L0_ffn_setup()
    _L0_ffn_in = {k: v for k, v in _L0_ffn_all.items() if k in ('Ws', 'bs', 'W1', 'b1', 'W2', 'b2')}
    del _L0_ffn_all
    return {'x': x, 'src': src, 'dst': dst, 'edge_attr_128': edge_attr_128, 'L0_gnn_hk_W1': _L0_gnn_in['hk_W1'], 'L0_gnn_hk_b1': _L0_gnn_in['hk_b1'], 'L0_gnn_hk_g': _L0_gnn_in['hk_g'], 'L0_gnn_hk_be': _L0_gnn_in['hk_be'], 'L0_gnn_hk_W2': _L0_gnn_in['hk_W2'], 'L0_gnn_hk_b2': _L0_gnn_in['hk_b2'], 'L0_gnn_hv_W1': _L0_gnn_in['hv_W1'], 'L0_gnn_hv_b1': _L0_gnn_in['hv_b1'], 'L0_gnn_hv_g': _L0_gnn_in['hv_g'], 'L0_gnn_hv_be': _L0_gnn_in['hv_be'], 'L0_gnn_hv_W2': _L0_gnn_in['hv_W2'], 'L0_gnn_hv_b2': _L0_gnn_in['hv_b2'], 'L0_gnn_hq_W1': _L0_gnn_in['hq_W1'], 'L0_gnn_hq_b1': _L0_gnn_in['hq_b1'], 'L0_gnn_hq_g': _L0_gnn_in['hq_g'], 'L0_gnn_hq_be': _L0_gnn_in['hq_be'], 'L0_gnn_hq_W2': _L0_gnn_in['hq_W2'], 'L0_gnn_hq_b2': _L0_gnn_in['hq_b2'], 'L0_gnn_no_W1': _L0_gnn_in['no_W1'], 'L0_gnn_no_b1': _L0_gnn_in['no_b1'], 'L0_gnn_no_g': _L0_gnn_in['no_g'], 'L0_gnn_no_be': _L0_gnn_in['no_be'], 'L0_gnn_no_W2': _L0_gnn_in['no_W2'], 'L0_gnn_no_b2': _L0_gnn_in['no_b2'], 'L0_ffn_Ws': _L0_ffn_in['Ws'], 'L0_ffn_bs': _L0_ffn_in['bs'], 'L0_ffn_W1': _L0_ffn_in['W1'], 'L0_ffn_b1': _L0_ffn_in['b1'], 'L0_ffn_W2': _L0_ffn_in['W2'], 'L0_ffn_b2': _L0_ffn_in['b2']}

def reference(x, src, dst, edge_attr_128, L0_gnn_hk_W1, L0_gnn_hk_b1, L0_gnn_hk_g, L0_gnn_hk_be, L0_gnn_hk_W2, L0_gnn_hk_b2, L0_gnn_hv_W1, L0_gnn_hv_b1, L0_gnn_hv_g, L0_gnn_hv_be, L0_gnn_hv_W2, L0_gnn_hv_b2, L0_gnn_hq_W1, L0_gnn_hq_b1, L0_gnn_hq_g, L0_gnn_hq_be, L0_gnn_hq_W2, L0_gnn_hq_b2, L0_gnn_no_W1, L0_gnn_no_b1, L0_gnn_no_g, L0_gnn_no_be, L0_gnn_no_W2, L0_gnn_no_b2, L0_ffn_Ws, L0_ffn_bs, L0_ffn_W1, L0_ffn_b1, L0_ffn_W2, L0_ffn_b2):
    import jax
    import jax.numpy as jnp

    def _L0_gnn_ref(h, edge_feat, edge_index, hk_W1, hk_b1, hk_g, hk_be, hk_W2, hk_b2, hv_W1, hv_b1, hv_g, hv_be, hv_W2, hv_b2, hq_W1, hq_b1, hq_g, hq_be, hq_W2, hq_b2, no_W1, no_b1, no_g, no_be, no_W2, no_b2):
        import jax, jax.numpy as jnp
        import numpy as np
        N_NODES = 2500
        N_EDGES = 12500
        IN = 512
        HID = 512
        OUT = 512
        EF = 128
        NH = 16
        HEAD = OUT // NH

        def _ln(x):
            mu = jnp.mean(x, axis=-1, keepdims=True)
            var = jnp.var(x, axis=-1, keepdims=True)
            return (x - mu) / jnp.sqrt(var + 1e-05)

        def _mlp(x, W1, b1, g, be, W2, b2):
            hdn = x @ W1 + b1
            hdn = _ln(hdn) * g + be
            hdn = jax.nn.relu(hdn)
            return hdn @ W2 + b2
        N = h.shape[0]
        src, dst = (edge_index[0], edge_index[1])
        kv_in = jnp.concatenate([h[src], edge_feat], axis=-1)
        k = _mlp(kv_in, hk_W1, hk_b1, hk_g, hk_be, hk_W2, hk_b2).reshape(-1, NH, HEAD)
        v = _mlp(kv_in, hv_W1, hv_b1, hv_g, hv_be, hv_W2, hv_b2).reshape(-1, NH, HEAD)
        q = _mlp(h, hq_W1, hq_b1, hq_g, hq_be, hq_W2, hq_b2).reshape(-1, NH, HEAD)
        logits = jnp.sum(q[dst] * k, axis=-1) / np.float32(np.sqrt(HEAD))
        mx = jax.ops.segment_max(logits, dst, num_segments=N)
        ex = jnp.exp(logits - mx[dst])
        den = jax.ops.segment_sum(ex, dst, num_segments=N)
        alpha = ex / den[dst]
        m = alpha[..., None] * v
        out = jax.ops.segment_sum(m, dst, num_segments=N).reshape(N, OUT)
        out = _mlp(jnp.concatenate([out, h], axis=-1), no_W1, no_b1, no_g, no_be, no_W2, no_b2)
        return out + h

    def _L0_ffn_ref(x, Ws, bs, W1, b1, W2, b2):
        import jax, jax.numpy as jnp
        import numpy as np
        B, S, D, F, E = (4, 256, 512, 256, 8)
        Bb, Ss, Dd = x.shape
        xt = x.reshape(-1, Dd)
        logits = xt @ Ws + bs
        probs = jax.nn.softmax(logits, axis=-1)
        prob_max = jnp.max(probs, axis=-1)
        routes = jnp.argmax(probs, axis=-1)
        onehot = jax.nn.one_hot(routes, W1.shape[0], dtype=xt.dtype)

        def expert_ffn(w1, bb1, w2, bb2):
            h = jax.nn.gelu(xt @ w1 + bb1, approximate=False)
            return h @ w2 + bb2
        y = jax.vmap(expert_ffn)(W1, b1, W2, b2)
        out = jnp.einsum('te,etd->td', onehot, y)
        out = out * prob_max[:, None]
        return out.reshape(Bb, Ss, Dd)
    edge_index = jnp.stack([src, dst])
    x = x + _L0_gnn_ref(_layernorm(x, axis=-1), edge_attr_128, edge_index, L0_gnn_hk_W1, L0_gnn_hk_b1, L0_gnn_hk_g, L0_gnn_hk_be, L0_gnn_hk_W2, L0_gnn_hk_b2, L0_gnn_hv_W1, L0_gnn_hv_b1, L0_gnn_hv_g, L0_gnn_hv_be, L0_gnn_hv_W2, L0_gnn_hv_b2, L0_gnn_hq_W1, L0_gnn_hq_b1, L0_gnn_hq_g, L0_gnn_hq_be, L0_gnn_hq_W2, L0_gnn_hq_b2, L0_gnn_no_W1, L0_gnn_no_b1, L0_gnn_no_g, L0_gnn_no_be, L0_gnn_no_W2, L0_gnn_no_b2)
    x = x + _L0_ffn_ref(_layernorm(x, axis=-1)[None], L0_ffn_Ws, L0_ffn_bs, L0_ffn_W1, L0_ffn_b1, L0_ffn_W2, L0_ffn_b2)[0]
    return x

_drawn_inputs = setup_inputs


def setup_inputs(seed=0):
    import zlib

    import numpy as np

    out = dict(_drawn_inputs(seed))
    spreads = {'L0_gnn_hk_b1': (0.0, 0.8),
     'L0_gnn_hk_g': (1.0, 0.6),
     'L0_gnn_hk_be': (0.0, 0.8),
     'L0_gnn_hk_b2': (0.0, 0.8),
     'L0_gnn_hv_b1': (0.0, 0.498),
     'L0_gnn_hv_g': (1.0, 0.572),
     'L0_gnn_hv_be': (0.0, 0.526),
     'L0_gnn_hv_b2': (0.0, 0.267),
     'L0_gnn_hq_b1': (0.0, 0.8),
     'L0_gnn_hq_g': (1.0, 0.6),
     'L0_gnn_hq_be': (0.0, 0.8),
     'L0_gnn_hq_b2': (0.0, 0.8),
     'L0_gnn_no_b1': (0.0, 0.1),
     'L0_gnn_no_g': (1.0, 0.2),
     'L0_gnn_no_be': (0.0, 0.1),
     'L0_gnn_no_b2': (0.0, 0.1),
     'L0_ffn_bs': (0.0, 0.8),
     'L0_ffn_b1': (0.0, 0.8),
     'L0_ffn_b2': (0.0, 0.743)}
    factors = {'L0_gnn_hq_W1': 2.948, 'L0_ffn_Ws': 4.279, 'L0_ffn_W1': 6.676, 'L0_ffn_W2': 6.212}
    for name, (base, spread) in spreads.items():
        noise = np.random.default_rng([zlib.crc32(name.encode()), seed]).standard_normal(out[name].shape)
        drawn = base * np.exp(spread * noise) if base else spread * noise
        out[name] = jnp.asarray(drawn.astype(out[name].dtype))
    for name, factor in factors.items():
        out[name] = (out[name] * factor).astype(out[name].dtype)
    return out
```

```python
from contextlib import ExitStack

import concourse.bass as bass
from concourse import mybir

ALU = mybir.AluOpType
ACT = mybir.ActivationFunctionType
AX = mybir.AxisListType
F32 = mybir.dt.float32
I32 = mybir.dt.int32

P = 128
NODES, D = 1250, 512
KC = D // P
NODE_ROWS = 125
NODE_TILES = NODES // NODE_ROWS
EDGES, EF = 20000, 128
EDGE_ROWS = 125
PADS = P - EDGE_ROWS
EDGE_TILES = EDGES // EDGE_ROWS
SUPER = 4
SUPERS = EDGE_TILES // SUPER
PLACES = EDGE_TILES * P
SPAN = PLACES // P
HEADS = 16
HEAD = D // HEADS
HALF = EDGE_TILES // 2
EXPERTS, FF = 8, 256
FC = FF // P
EPS = 1e-5
NEG = -1.0e38

T_P, T_SQ, TABLE_W = D, D + EF, D + EF + 4
Q_W = D + HEADS
L_W = HEADS + 4
SUM_W = D + HEADS
SUM_ROWS = 11 * P
SUM_TABLES = 4

assert NODE_TILES * NODE_ROWS == NODES and EDGE_TILES * EDGE_ROWS == EDGES and SUPERS * SUPER == EDGE_TILES
assert SUM_ROWS >= NODES + P


class Chain:

    def __init__(self, eng, sem, base=0):
        self.eng, self.sem, self.base, self.n = eng, sem, base, 0

    def __call__(self, instruction):
        self.n += 1
        instruction.then_inc(self.sem, 1)
        self.eng.wait_ge(self.sem, self.base + self.n)


class Memory:

    def __init__(self, nc, ctx, prefix):
        self.nc, self.ctx, self.prefix = nc, ctx, prefix

    def sb(self, name, shape, dtype=F32):
        return self.ctx.enter_context(self.nc.sbuf_tensor(f"{self.prefix}_{name}", shape, dtype))

    def ps(self, name, shape=(P, D)):
        return self.ctx.enter_context(self.nc.psum_tensor(f"{self.prefix}_{name}", list(shape), F32))

    def sem(self, name):
        return self.ctx.enter_context(self.nc.semaphore(f"{self.prefix}_{name}"))


def row_bc(vector):
    return vector.partition_broadcast(P)


def col(vector):
    return vector.rearrange("(c p) -> p c", p=P)


def reciprocal_root(dve, link, var, root, out, tmp):
    link(dve.reciprocal(out, root))
    link(dve.tensor_tensor(tmp, out, out, ALU.mult))
    link(dve.tensor_tensor(tmp, tmp, var, ALU.mult))
    link(dve.tensor_scalar(tmp, tmp, -0.5, 1.5, ALU.mult, ALU.add))
    link(dve.tensor_tensor(out, out, tmp, ALU.mult))


RECIPROCAL_ROOT_LINKS = 5


def wait_here(eng, passed):
    eng.sem_inc(passed, 1)


def prepare_weights(nc, w, keep, dram):
    with ExitStack() as ctx:
        m = Memory(nc, ctx, "prep")
        cT_h = m.sb("cT_h", [P, 2, KC, D])
        cT_e = m.sb("cT_e", [P, 2, KC, EF])
        mean = m.sb("mean", [P, 3, 5])
        b_mean = m.sb("b_mean", [P, 3])
        b_col = m.sb("b_col", [P, 2, KC])
        rows_i = m.sb("rows_i", [HALF, 2, 2, EDGE_ROWS], I32)
        rows = m.sb("rows", [HALF, 2, 2, P])
        pad_i = m.sb("pad_i", [HALF, 2, P], I32)
        zero = m.sb("zero", [P, SUM_W])
        earlier = m.sb("earlier", [P, P])
        drow = m.sb("drow", [P, 2, 16, P])
        same = m.sb("same", [P, 16, P])
        in_rank = m.sb("in_rank", [P, EDGE_TILES])
        flag = m.sb("flag", [P, EDGE_TILES])
        fill = m.sb("fill", [P, EDGE_TILES])
        fill_i = m.sb("fill_i", [P, EDGE_TILES], I32)
        pT = [m.ps(f"pT{i}") for i in range(2)]
        pE = [m.ps(f"pE{i}") for i in range(2)]
        pQ = m.ps("pQ")
        pG = m.ps("pG")
        pI = m.ps("pI")

        loaded = [m.sem(f"loaded_{x}") for x in "kvq"]
        small = m.sem("small_loaded")
        idx_loaded = m.sem("idx_loaded")
        consts = m.sem("consts")
        pool_own = m.sem("pool_own")
        dve_own = m.sem("dve_own")
        centred = m.sem("centred")
        turned = m.sem("turned")
        turned_sb = m.sem("turned_sb")
        products = m.sem("products")
        products_sb = m.sem("products_sb")
        rows_ready = m.sem("rows_ready")
        rows_turned = m.sem("rows_turned")
        stored = m.sem("stored")
        zeroed = m.sem("zeroed")
        drow_in = [m.sem(f"drow_in{i}") for i in range(2)]
        drow_used = m.sem("drow_used")
        dst_table = m.sem("dst_table")
        nets = [("k", 5), ("v", 5), ("q", 4)]
        GROUPS = EDGE_TILES // 16

        block = ctx.enter_context(nc.Block())

        @block.sync
        def _(sp):
            for n, (x, tiles) in enumerate(nets):
                sp.dma_start(keep.w1[x][:, :, :], w[f"h{x}_W1"].rearrange("(r p) n -> p r n", p=P)).then_inc(loaded[n], 16)
            sp.dma_start(keep.x[:, :, :], w["x"].rearrange("(t p) n -> p t n", p=NODE_ROWS)).then_inc(keep.x_loaded, 16)
            sp.wait_ge(rows_ready, 2)
            for half in range(2):
                sp.dma_start(dram.dst_rows[half * HALF:(half + 1) * HALF, :], rows[:, half, 1, :]).then_inc(stored, 16)
            sp.wait_ge(stored, 32)
            for g in range(GROUPS):
                if g >= 2:
                    sp.wait_ge(drow_used, g - 1)
                src = dram.dst_rows[16 * g:16 * g + 16, :].rearrange("t p -> (t p)").partition_broadcast(P)
                sp.dma_start(drow[:, g % 2, :, :].rearrange("p t e -> p (t e)"), src).then_inc(drow_in[g % 2], 16)
            sp.wait_ge(zeroed, SUM_TABLES * 16)

        @block.scalar
        def _(act):
            for half in range(2):
                for i, name in enumerate(("src", "dst")):
                    act.dma_start(rows_i[:, half, i, :],
                                  w[name].rearrange("(h t p) -> h t p", h=2, p=EDGE_ROWS)[half]).then_inc(idx_loaded, 16)
            for x, _ in nets:
                act.dma_start(keep.b1[x][:, :], row_bc(w[f"h{x}_b1"])).then_inc(small, 16)
                act.dma_start(keep.be[x][:, :], col(w[f"h{x}_be"]), allow_slow_non_contiguous=True).then_inc(small, 16)
            for n, (x, _) in enumerate(nets[:2]):
                act.dma_start(keep.g[x][:, :], row_bc(w[f"h{x}_g"])).then_inc(small, 16)
                act.dma_start(b_col[:, n, :], col(w[f"h{x}_b1"]), allow_slow_non_contiguous=True).then_inc(small, 16)
            act.dma_start(keep.g_col_q[:, :], col(w["hq_g"]), allow_slow_non_contiguous=True).then_inc(small, 16)
            act.dma_start(keep.b2q[:, :], row_bc(w["hq_b2"])).then_inc(small, 16)
            act.dma_start(keep.b2k[:, :], row_bc(w["hk_b2"])).then_inc(small, 16)
            act.wait_ge(consts, 1)
            for t in range(SUM_TABLES):
                act.dma_start(dram.sums[t].rearrange("(p r) f -> p r f", r=SUM_ROWS // P),
                              zero[:, :].unsqueeze(1).to_broadcast([P, SUM_ROWS // P, SUM_W])).then_inc(zeroed, 16)
            for n in range(2):
                for c in range(KC):
                    k = n * KC + c
                    act.wait_ge(turned, k + 1)
                    act.activation(cT_h[:, n, c, :], pT[k % 2][:, :], ACT.Copy).then_inc(turned_sb, 1)
                    act.activation(cT_e[:, n, c, :], pE[k % 2][:, 0:EF], ACT.Copy).then_inc(turned_sb, 1)
                act.wait_ge(products, n + 1)
                act.activation(keep.w_p[:, n, :, :], pQ[:, :].rearrange("p (r n) -> p r n", r=KC), ACT.Copy, scale=2.0)\
                   .then_inc(products_sb, 1)
                act.activation(keep.gram[:, n, :], pG[:, 0:EF], ACT.Copy).then_inc(products_sb, 1)
                act.activation(keep.b_p[:, n, :], pG[:, EF:2 * EF], ACT.Copy, scale=2.0).then_inc(products_sb, 1)

        @block.gpsimd
        def _(pool):
            pool.memset(zero[:, :], 0.0).then_inc(consts, 1)
            pool.memset(keep.ident[:, :], 0.0).then_inc(pool_own, 1)
            pool.memset(earlier[:, :], 1.0).then_inc(pool_own, 1)
            pool.wait_ge(pool_own, 2)
            pool.affine_select(out=keep.ident[:, :], in_=keep.ident[:, :], compare_op=ALU.not_equal, fill=1.0,
                               base=0, pattern=[[-1, P]], channel_multiplier=1).then_inc(consts, 1)
            pool.affine_select(out=earlier[:, :], in_=earlier[:, :], compare_op=ALU.is_gt, fill=0.0,
                               base=0, pattern=[[-1, P]], channel_multiplier=1).then_inc(consts, 1)
            for half in range(2):
                pool.iota(pad_i[:, half, :], [[1, P]], base=NODES - EDGE_ROWS + PADS * HALF * half,
                          channel_multiplier=PADS).then_inc(consts, 1)
            pool.iota(keep.place_i[:, :], [[PADS, EDGE_TILES]], base=EDGES - EDGE_ROWS, channel_multiplier=1).then_inc(pool_own, 1)
            pool.wait_ge(pool_own, 3)
            pool.iota(keep.place_i[0:EDGE_ROWS, :], [[EDGE_ROWS, EDGE_TILES]], base=0, channel_multiplier=1).then_inc(pool_own, 1)
            pool.iota(fill_i[:, :], [[0, EDGE_TILES]], base=NODES, channel_multiplier=1).then_inc(consts, 1)

        @block.vector
        def _(dve):
            link = Chain(dve, dve_own)
            dve.wait_ge(consts, 6)
            dve.wait_ge(idx_loaded, 64)
            link(dve.memset(rows[:, :, 0, :], 0.0))
            link(dve.tensor_copy(rows[:, :, 1, :], pad_i[:, :, :]))
            for i in range(2):
                dve.tensor_copy(rows[:, :, i, 0:EDGE_ROWS], rows_i[:, :, i, :]).then_inc(rows_ready, 1)
            dve.wait_ge(small, 13 * 16)
            for n, (x, tiles) in enumerate(nets):
                dve.wait_ge(loaded[n], 16)
                w1 = keep.w1[x]
                link(dve.tensor_reduce(mean[:, n, 0:tiles], w1[:, :, :], AX.X, ALU.add))
                link(dve.tensor_scalar(mean[:, n, 0:tiles], mean[:, n, 0:tiles], -1.0 / D, None, ALU.mult))
                for r in range(tiles):
                    link(dve.tensor_scalar(w1[:, r, :], w1[:, r, :], mean[:, n, r:r + 1], None, ALU.add))
                link(dve.tensor_reduce(b_mean[:, n:n + 1], keep.b1[x][:, :], AX.X, ALU.add))
                link(dve.tensor_scalar(b_mean[:, n:n + 1], b_mean[:, n:n + 1], -1.0 / D, None, ALU.mult))
                link(dve.tensor_scalar(keep.b1[x][:, :], keep.b1[x][:, :], b_mean[:, n:n + 1], None, ALU.add))
                if n < 2:
                    link(dve.tensor_scalar(b_col[:, n, :], b_col[:, n, :], b_mean[:, n:n + 1], None, ALU.add))
                    dve.tensor_tensor(keep.w1e[x][:, :], w1[:, 4, :], keep.g[x][:, :], ALU.mult).then_inc(centred, 1)
            dve.wait_ge(rows_turned, 1)
            turned_rows = pI[:, 0:4 * HALF].rearrange("p (i h t) -> p i h t", i=2, h=2)
            link(dve.tensor_copy(keep.src_i[:, :].rearrange("p (h t) -> p h t", h=2), turned_rows[:, 0, :, :]))
            link(dve.tensor_copy(keep.dst_f[:, :].rearrange("p (h t) -> p h t", h=2), turned_rows[:, 1, :, :]))
            link(dve.tensor_scalar(flag[:, :], keep.dst_f[:, :], float(NODES), None, ALU.is_lt))
            link(dve.tensor_tensor(fill[:, :], flag[:, :], keep.dst_f[:, :], ALU.mult))
            link(dve.tensor_copy(keep.dst_i[:, :], fill[:, :]))
            for g in range(GROUPS):
                dve.wait_ge(drow_in[g % 2], 16 * (g // 2 + 1))
                mine = keep.dst_f[:, 16 * g:16 * g + 16].unsqueeze(2).to_broadcast([P, 16, P])
                mm = dve.tensor_tensor(same[:, :, :], drow[:, g % 2, :, :], mine, ALU.is_equal)
                mm.then_inc(drow_used, 1)
                dve.wait_ge(drow_used, g + 1)
                link(dve.tensor_tensor(same[:, :, :], same[:, :, :],
                                       earlier[:, :].unsqueeze(1).to_broadcast([P, 16, P]), ALU.mult))
                link(dve.tensor_reduce(in_rank[:, 16 * g:16 * g + 16], same[:, :, :], AX.X, ALU.add))
            link(dve.tensor_scalar(fill[:, :], in_rank[:, :], 0.0, None, ALU.is_equal))
            link(dve.tensor_tensor(flag[:, :], flag[:, :], fill[:, :], ALU.mult))
            link(dve.tensor_copy(fill[:, :], fill_i[:, :]))
            link(dve.tensor_tensor(in_rank[:, :], keep.dst_f[:, :], fill[:, :], ALU.subtract))
            link(dve.tensor_tensor(in_rank[:, :], in_rank[:, :], flag[:, :], ALU.mult))
            link(dve.tensor_tensor(in_rank[:, :], in_rank[:, :], fill[:, :], ALU.add))
            link(dve.tensor_copy(keep.sum_i[:, :], in_rank[:, :]))

        @block.tensor
        def _(pe):
            pe.wait_ge(consts, 6)
            pe.wait_ge(rows_ready, 2)
            for i in range(2):
                for half in range(2):
                    k = 2 * i + half
                    mm = pe.transpose(pI[:, k * HALF:(k + 1) * HALF], rows[:, half, i, :], keep.ident[0:HALF, 0:HALF])
            mm.then_inc(rows_turned, 1)
            for n in range(2):
                x = nets[n][0]
                pe.wait_ge(centred, n + 1)
                for c in range(KC):
                    k = n * KC + c
                    if k >= 2:
                        pe.wait_ge(turned_sb, 2 * (k - 1))
                    for r in range(KC):
                        pe.transpose(pT[k % 2][:, r * P:(r + 1) * P], keep.w1[x][:, r, c * P:(c + 1) * P], keep.ident[:, :])
                    pe.transpose(pE[k % 2][:, 0:EF], keep.w1[x][:, 4, c * P:(c + 1) * P], keep.ident[:, :]).then_inc(turned, 1)
                pe.wait_ge(turned_sb, 2 * KC * (n + 1))
                if n:
                    pe.wait_ge(products_sb, 3)
                for r in range(KC):
                    for c in range(KC):
                        pe.matmul(pQ[:, r * EF:(r + 1) * EF], cT_h[:, n, c, r * P:(r + 1) * P], cT_e[:, n, c, :],
                                  start=(c == 0), stop=(c == KC - 1))
                for c in range(KC):
                    pe.matmul(pG[:, 0:EF], cT_e[:, n, c, :], cT_e[:, n, c, :], start=(c == 0), stop=(c == KC - 1))
                for c in range(KC):
                    mm = pe.matmul(pG[:, EF:2 * EF], b_col[:, n, c:c + 1].to_broadcast([P, P]), cT_e[:, n, c, :],
                                   start=(c == 0), stop=(c == KC - 1))
                mm.then_inc(products, 1)


def node_tables(nc, w, keep, dram):
    with ExitStack() as ctx:
        m = Memory(nc, ctx, "node")
        R = NODE_ROWS
        w2q = m.sb("w2q", [P, KC, D])
        stats = m.sb("stats", [R, 6])
        mv = m.sb("mv", [R, 2])
        var = m.sb("var", [R, 2])
        root = m.sb("root", [R, 2])
        rstd = m.sb("rstd", [R, 2])
        tmp = m.sb("tmp", [R, 2])
        h = m.sb("h", [R, D])
        hT = m.sb("hT", [P, KC, R])
        first = m.sb("first", [R, 3, D])
        square = m.sb("square", [R, 3, D])
        sumsq = m.sb("sumsq", [R, 3])
        row = m.sb("row", [R, 2, TABLE_W])
        q_norm = m.sb("q_norm", [R, D])
        qT = m.sb("qT", [P, KC, R])
        q_row = m.sb("q_row", [R, Q_W])
        q_bias = m.sb("q_bias", [R, D])
        pH = m.ps("pH")
        pF = [m.ps(f"pF{i}") for i in range(3)]
        pP = m.ps("pP")
        pT = m.ps("pT")
        pQ = m.ps("pQ")

        w2_loaded = m.sem("w2_loaded")
        own = m.sem("dve_own")
        var_ready = m.sem("var_ready")
        root_ready = m.sem("root_ready")
        h_ready = m.sem("h_ready")
        h_turned = m.sem("h_turned")
        hT_ready = m.sem("hT_ready")
        first_done = m.sem("first_done")
        first_sb = m.sem("first_sb")
        squared = m.sem("squared")
        rows_ready = m.sem("rows_ready")
        rows_stored = m.sem("rows_stored")
        q_normed = m.sem("q_normed")
        q_turned = m.sem("q_turned")
        qT_ready = m.sem("qT_ready")
        q_done = m.sem("q_done")
        q_ready = m.sem("q_ready")
        q_stored = m.sem("q_stored")
        kept = m.sem("hT_kept")
        LINKS = 2 * RECIPROCAL_ROOT_LINKS + 11

        block = ctx.enter_context(nc.Block())

        @block.sync
        def _(sp):
            sp.dma_start(w2q[:, :, :], w["hq_W2"].rearrange("(r p) n -> p r n", p=P)).then_inc(w2_loaded, 16)
            with sp.Fori(0, NODE_TILES) as i:
                rows = bass.ds(i * R, R)
                sp.wait_ge(rows_ready, i + 1)
                for n in range(2):
                    sp.dma_start(dram.table[n][rows, :], row[:, n, :]).then_inc(rows_stored, 16)
                sp.wait_ge(q_ready, i + 1)
                sp.dma_start(dram.query[rows, :], q_row[:, :]).then_inc(q_stored, 16)
            sp.wait_ge(rows_stored, NODE_TILES * 32)
            sp.wait_ge(q_stored, NODE_TILES * 16)

        @block.vector
        def _(dve):
            dve.memset(row[:, :, :], 0.0).then_inc(own, 1)
            dve.wait_ge(own, 1)
            dve.wait_ge(keep.x_loaded, 16)
            with dve.Fori(0, NODE_TILES) as i:
                link = Chain(dve, own, i * LINKS + 1)
                x = keep.x[:, bass.ds(i, 1), :].rearrange("p a n -> p (a n)")
                link(dve.bn_stats(stats[:, :], x))
                wait_here(dve, keep.dve_passed)
                link(dve.bn_aggr(mv[:, :], stats[:, :]))
                dve.tensor_scalar(var[:, 0:1], mv[:, 1:2], EPS, None, ALU.add).then_inc(var_ready, 1)
                dve.wait_ge(root_ready, 2 * i + 1)
                reciprocal_root(dve, link, var[:, 0:1], root[:, 0:1], rstd[:, 0:1], tmp[:, 0:1])
                dve.wait_ge(kept, 2 * i)
                dve.tensor_scalar(h[:, :], x, mv[:, 0:1], rstd[:, 0:1], ALU.subtract, ALU.mult).then_inc(h_ready, 1)
                dve.wait_ge(first_done, i + 1)
                dve.tensor_tensor(first[:, 2, :], pF[2][0:R, :], keep.b1["q"][0:R, :], ALU.add).then_inc(first_sb, 1)
                for n, net in enumerate("kv"):
                    dve.tensor_tensor(first[:, n, :], pF[n][0:R, :], keep.b1[net][0:R, :], ALU.add).then_inc(first_sb, 1)
                dve.wait_ge(squared, 3 * i + 1)
                dve.tensor_scalar(var[:, 1:2], sumsq[:, 2:3], EPS, None, ALU.add).then_inc(var_ready, 1)
                dve.wait_ge(root_ready, 2 * i + 2)
                reciprocal_root(dve, link, var[:, 1:2], root[:, 1:2], rstd[:, 1:2], tmp[:, 1:2])
                dve.tensor_scalar(q_norm[:, :], first[:, 2, :], rstd[:, 1:2], None, ALU.mult).then_inc(q_normed, 1)
                dve.wait_ge(first_sb, 3 * i + 3)
                dve.wait_ge(rows_stored, i * 32)
                dve.wait_ge(squared, 3 * i + 3)
                for n, net in enumerate("kv"):
                    link(dve.tensor_tensor(row[:, n, 0:D], first[:, n, :], keep.g[net][0:R, :], ALU.mult))
                    link(dve.tensor_tensor(row[:, n, T_P:T_P + EF], pP[0:R, n * EF:(n + 1) * EF], keep.b_p[0:R, n, :], ALU.add))
                    link(dve.tensor_scalar(row[:, n, T_SQ:T_SQ + 1], sumsq[:, n:n + 1], EPS, None, ALU.add))
                dve.sem_inc(rows_ready, 1)
                dve.wait_ge(q_done, i + 1)
                dve.wait_ge(q_stored, i * 16)
                link(dve.tensor_tensor(q_row[:, 0:D], pQ[0:R, :], keep.b2q[0:R, :], ALU.add))
                link(dve.tensor_tensor(q_bias[:, :], q_row[:, 0:D], keep.b2k[0:R, :], ALU.mult))
                link(dve.tensor_reduce(q_row[:, D:Q_W], q_bias[:, :].rearrange("p (h d) -> p h d", h=HEADS), AX.X, ALU.add))
                dve.sem_inc(q_ready, 1)
                assert link.n == LINKS

        @block.scalar
        def _(act):
            with act.Fori(0, NODE_TILES) as i:
                act.wait_ge(var_ready, 2 * i + 1)
                act.activation(root[:, 0:1], var[:, 0:1], ACT.Sqrt).then_inc(root_ready, 1)
                act.wait_ge(h_turned, i + 1)
                act.wait_ge(kept, 2 * i)
                act.activation(hT[:, :, :], pH[:, 0:KC * R].rearrange("p (c r) -> p c r", c=KC), ACT.Copy).then_inc(hT_ready, 1)
                for k, n in enumerate((2, 0, 1)):
                    act.wait_ge(first_sb, 3 * i + k + 1)
                    act.activation(square[:, n, :], first[:, n, :], ACT.Square, scale=D ** -0.5,
                                   accum_out=sumsq[:, n:n + 1]).then_inc(squared, 1)
                    if n == 2:
                        act.wait_ge(var_ready, 2 * i + 2)
                        act.activation(root[:, 1:2], var[:, 1:2], ACT.Sqrt).then_inc(root_ready, 1)
                act.wait_ge(q_turned, i + 1)
                for c in range(KC):
                    act.activation(qT[:, c, :], pT[:, c * R:(c + 1) * R], ACT.Relu, bias=keep.be["q"][:, c:c + 1],
                                   scale=keep.g_col_q[:, c:c + 1]).then_inc(qT_ready, 1)

        @block.gpsimd
        def _(pool):
            with pool.Fori(0, NODE_TILES) as i:
                pool.wait_ge(h_ready, i + 1)
                wait_here(pool, keep.pool_passed)
                pool.tensor_copy(keep.h[:, bass.ds(i, 1), :].rearrange("p a n -> p (a n)"), h[:, :]).then_inc(kept, 1)
                pool.wait_ge(hT_ready, i + 1)
                wait_here(pool, keep.pool_passed)
                pool.tensor_copy(keep.hT[:, :, bass.ds(i * R, R)], hT[:, :, :]).then_inc(kept, 1)

        @block.tensor
        def _(pe):
            pe.wait_ge(w2_loaded, 16)
            with pe.Fori(0, NODE_TILES) as i:
                pe.wait_ge(h_ready, i + 1)
                for c in range(KC):
                    mm = pe.transpose(pH[:, c * R:(c + 1) * R], h[:, c * P:(c + 1) * P], keep.ident[0:R, 0:R])
                mm.then_inc(h_turned, 1)
                pe.wait_ge(hT_ready, i + 1)
                pe.wait_ge(own, i * LINKS)
                for n, net in ((2, "q"), (0, "k"), (1, "v")):
                    for c in range(KC):
                        mm = pe.matmul(pF[n][0:R, :], hT[:, c, :], keep.w1[net][:, c, :], start=(c == 0), stop=(c == KC - 1))
                for n in range(2):
                    for c in range(KC):
                        mm = pe.matmul(pP[0:R, n * EF:(n + 1) * EF], hT[:, c, :], keep.w_p[:, n, c, :],
                                       start=(c == 0), stop=(c == KC - 1))
                mm.then_inc(first_done, 1)
                pe.wait_ge(q_normed, i + 1)
                for c in range(KC):
                    mm = pe.transpose(pT[:, c * R:(c + 1) * R], q_norm[:, c * P:(c + 1) * P], keep.ident[0:R, 0:R])
                mm.then_inc(q_turned, 1)
                pe.wait_ge(qT_ready, KC * (i + 1))
                for c in range(KC):
                    mm = pe.matmul(pQ[0:R, :], qT[:, c, :], w2q[:, c, :], start=(c == 0), stop=(c == KC - 1))
                mm.then_inc(q_done, 1)


def edge_phase(nc, w, keep, dram, values):
    net = "v" if values else "k"
    n_net = int(values)
    side_w = HEADS if values else Q_W
    with ExitStack() as ctx:
        m = Memory(nc, ctx, f"edge_{net}")
        w2 = m.sb("w2", [P, KC, D])
        ef = [m.sb(f"ef{s}", [P, SUPER, EF]) for s in range(2)]
        table = [m.sb(f"table{s}", [P, SUPER, TABLE_W]) for s in range(2)]
        side = [m.sb(f"side{s}", [P, SUPER, side_w]) for s in range(2)]
        src_at = [m.sb(f"src_at{s}", [P, SUPER], I32) for s in range(2)]
        side_at = [m.sb(f"side_at{s}", [P, SUPER], I32) for s in range(2)]
        out_at = [m.sb(f"out_at{s}", [P, SUPER], I32) for s in range(2)]
        efT = m.sb("efT", [EF, SUPER * P])
        efT_n = m.sb("efT_n", [EF, SUPER * P])
        diag = m.sb("diag", [P, SUPER, P])
        hidT = m.sb("hidT", [P, KC, SUPER * P])
        cross = m.sb("cross", [P, SUPER, EF])
        var = m.sb("var", [P, SUPER])
        root = m.sb("root", [P, SUPER])
        rstd = m.sb("rstd", [P, SUPER])
        tmp = m.sb("tmp", [P, SUPER])
        if values:
            drow = [m.sb(f"drow{s}", [P, SUPER, P]) for s in range(2)]
            dcol = [m.sb(f"dcol{s}", [P, SUPER]) for s in range(2)]
            equal = [m.sb(f"equal{s}", [P, SUPER, P]) for s in range(2)]
            weighted = [m.sb(f"weighted{s}", [P, SUM_W]) for s in range(2)]
            out = [m.sb(f"out{s}", [P, SUPER, SUM_W]) for s in range(2)]
        else:
            product = m.sb("product", [P, D])
            logit = m.sb("logit", [P, HEADS])
            out = [m.sb(f"out{s}", [P, SUPER, L_W]) for s in range(2)]

        pT = m.ps("pT")
        pG = m.ps("pG")
        pH = [m.ps(f"pH{b}") for b in range(2)]
        pL = [m.ps(f"pL{b}") for b in range(2)]
        if values:
            pS = m.ps("pS")
            pD = m.ps("pD")
            drow_in = [m.sem(f"drow_in{s}") for s in range(2)]
            weighted_ready = m.sem("weighted_ready")
            sum_done = m.sem("sum_done")
            sum_copied = m.sem("sum_copied")

        w2_loaded = m.sem("w2_loaded")
        cleared = m.sem("cleared")
        ef_in = [m.sem(f"ef_in{s}") for s in range(2)]
        table_in = [m.sem(f"table_in{s}") for s in range(2)]
        side_in = [m.sem(f"side_in{s}") for s in range(2)]
        pool_own = m.sem("pool_own")
        own = m.sem("dve_own")
        efT_turned = m.sem("efT_turned")
        efT_ready = m.sem("efT_ready")
        gram_done = m.sem("gram_done")
        var_ready = m.sem("var_ready")
        root_ready = m.sem("root_ready")
        diag_ready = m.sem("diag_ready")
        efT_n_turned = m.sem("efT_n_turned")
        efT_n_ready = m.sem("efT_n_ready")
        hid_done = m.sem("hid_done")
        hid_ready = m.sem("hid_ready")
        second_done = m.sem("second_done")
        second_used = m.sem("second_used")
        front_done = m.sem("front_done")
        out_ready = m.sem("out_ready")
        out_done = [m.sem(f"out_done{t}") for t in range(SUPER)]

        PAIRS = SUPERS // 2

        def following(i, s):
            return (i, 1) if s == 0 else (i + 1, 0)

        def rolled(eng, body):
            with eng.Fori(0, PAIRS - 1) as i:
                for s in range(2):
                    body(i, s, following(i, s))
            body(PAIRS - 1, 0, (PAIRS - 1, 1))
            body(PAIRS - 1, 1, None)

        block = ctx.enter_context(nc.Block())

        @block.sync
        def _(sp):
            sp.dma_start(w2[:, :, :], w[f"h{net}_W2"].rearrange("(r p) n -> p r n", p=P)).then_inc(w2_loaded, 16)
            sp.wait_ge(cleared, 2)
            with sp.Fori(0, PAIRS) as i:
                for s in range(2):
                    j = 2 * i + s
                    sp.wait_ge(efT_n_turned, 2 * i)
                    sp.dma_start(ef[s][0:EDGE_ROWS, :, :],
                                 w["edge_attr_128"][bass.ds(j * (SUPER * EDGE_ROWS), SUPER * EDGE_ROWS), :]
                                 .rearrange("(t p) f -> p t f", t=SUPER)).then_inc(ef_in[s], 16)
                    if values:
                        sp.wait_ge(front_done, 2 * i)
                        sp.dma_start(drow[s][:, :, :].rearrange("p t e -> p (t e)"),
                                     dram.dst_rows[bass.ds(j * SUPER, SUPER), :].rearrange("t p -> (t p)").partition_broadcast(P))\
                          .then_inc(drow_in[s], 16)
            for t in range(SUPER):
                sp.wait_ge(out_done[t], 16 * SUPERS)

        @block.gpsimd
        def _(pool):
            for s in range(2):
                pool.memset(ef[s][:, :, :], 0.0).then_inc(cleared, 1)

            def gather(i, s):
                j = 2 * i + s
                cols = bass.ds(j * SUPER, SUPER)
                pool.tensor_copy(src_at[s][:, :], keep.src_i[:, cols]).then_inc(pool_own, 1)
                pool.tensor_copy(side_at[s][:, :], (keep.place_i if values else keep.dst_i)[:, cols]).then_inc(pool_own, 1)
                pool.tensor_copy(out_at[s][:, :], (keep.sum_i if values else keep.place_i)[:, cols]).then_inc(pool_own, 1)
                pool.wait_ge(pool_own, 3 * j + 3)
                wait_here(pool, keep.pool_passed)
                for t in range(SUPER):
                    pool.indirect_dma_start(out=table[s][:, t, :], out_offset=None, in_=dram.table[n_net],
                                            in_offset=bass.IndirectOffsetOnAxis(ap=src_at[s][:, t:t + 1], axis=0))\
                        .then_inc(table_in[s], 16)
                for t in range(SUPER):
                    pool.indirect_dma_start(out=side[s][:, t, :], out_offset=None, in_=dram.expo if values else dram.query,
                                            in_offset=bass.IndirectOffsetOnAxis(ap=side_at[s][:, t:t + 1], axis=0))\
                        .then_inc(side_in[s], 16)

            def body(i, s, nxt):
                j = 2 * i + s
                if nxt:
                    pool.wait_ge(hid_done, KC * j)
                    pool.wait_ge(second_used, SUPER * j)
                    for t in range(SUPER):
                        pool.wait_ge(out_done[t], 16 * j)
                    wait_here(pool, keep.pool_passed)
                    gather(*nxt)
                for t in range(SUPER):
                    pool.wait_ge(out_ready, SUPER * j + t + 1)
                    if values:
                        pool.wait_ge(out_done[t], 16 * j)
                    wait_here(pool, keep.pool_passed)
                    where = bass.IndirectOffsetOnAxis(ap=out_at[s][:, t:t + 1], axis=0)
                    if values:
                        pool.indirect_dma_start(out=dram.sums[t], out_offset=where, in_=out[s][:, t, :], in_offset=None,
                                                compute_op=ALU.add).then_inc(out_done[t], 16)
                    else:
                        pool.indirect_dma_start(out=dram.logits, out_offset=where, in_=out[s][:, t, :],
                                                in_offset=None).then_inc(out_done[t], 16)

            gather(0, 0)
            rolled(pool, body)

        @block.scalar
        def _(act):
            def copy_efT(i, s):
                j = 2 * i + s
                act.wait_ge(efT_turned, j + 1)
                act.wait_ge(gram_done, j)
                act.activation(efT[:, :], pT[:, :], ACT.Copy).then_inc(efT_ready, 1)

            def square_root(i, s):
                act.wait_ge(var_ready, 2 * i + s + 1)
                act.activation(root[:, :], var[:, :], ACT.Sqrt).then_inc(root_ready, 1)

            def copy_efT_n(i, s):
                act.wait_ge(efT_n_turned, 2 * i + s + 1)
                act.activation(efT_n[:, :], pT[:, :], ACT.Copy).then_inc(efT_n_ready, 1)

            def copy_sum(i, s, t):
                j = 2 * i + s
                act.wait_ge(sum_done, SUPER * j + t + 1)
                act.wait_ge(out_done[t], 32 * i)
                act.activation(out[s][:, t, 0:D], pS[:, :], ACT.Copy).then_inc(sum_copied, 1)
                act.activation(out[s][:, t, D:SUM_W], pD[:, 0:HEADS], ACT.Copy).then_inc(sum_copied, 1)
                act.wait_ge(sum_copied, 2 * (SUPER * j + t + 1))
                act.sem_inc(out_ready, 1)

            def body(i, s, nxt):
                j = 2 * i + s
                for c in range(KC):
                    act.wait_ge(hid_done, KC * j + c + 1)
                    act.activation(hidT[:, c, :], pH[c % 2][:, :], ACT.Relu, bias=keep.be[net][:, c:c + 1])\
                       .then_inc(hid_ready, 1)
                    if c == 1 and nxt:
                        copy_efT(*nxt)
                if nxt:
                    square_root(*nxt)
                if values:
                    copy_sum(i, s, 0)
                    copy_sum(i, s, 1)
                if nxt:
                    copy_efT_n(*nxt)
                if values:
                    copy_sum(i, s, 2)
                    copy_sum(i, s, 3)

            copy_efT(0, 0)
            square_root(0, 0)
            copy_efT_n(0, 0)
            rolled(act, body)

        @block.vector
        def _(dve):
            FRONT = 4 + RECIPROCAL_ROOT_LINKS + (1 if values else 0)
            TILE = 0 if values else 3
            LINKS = FRONT + SUPER * TILE

            def front(i, s, link, others):
                j = 2 * i + s
                dve.wait_ge(gram_done, j + 1)
                dve.wait_ge(table_in[s], 64 * (i + 1))
                dve.wait_ge(ef_in[s], 16 * (i + 1))
                link(dve.tensor_tensor(cross[:, :, :], pG[:, :].rearrange("p (t f) -> p t f", t=SUPER),
                                       table[s][:, :, T_P:T_P + EF], ALU.add))
                link(dve.tensor_tensor(cross[:, :, :], cross[:, :, :], ef[s][:, :, :], ALU.mult))
                link(dve.tensor_reduce(tmp[:, :], cross[:, :, :], AX.X, ALU.add))
                link(dve.scalar_tensor_tensor(out=var[:, :], in0=tmp[:, :], scalar=1.0 / D,
                                              in1=table[s][:, :, T_SQ:T_SQ + 1].rearrange("p t a -> p (t a)"),
                                              op0=ALU.mult, op1=ALU.add))
                dve.tensor_scalar(var[:, :], var[:, :], EPS, None, ALU.max).then_inc(var_ready, 1)
                dve.wait_ge(root_ready, j + 1)
                reciprocal_root(dve, link, var[:, :], root[:, :], rstd[:, :], tmp[:, :])
                dve.wait_ge(hid_done, KC * j)
                for t in range(SUPER):
                    dve.tensor_scalar(diag[:, t, :], keep.ident[:, :], rstd[:, t:t + 1], None, ALU.mult).then_inc(diag_ready, 1)
                if values:
                    link(dve.tensor_copy(dcol[s][:, :], keep.dst_f[:, bass.ds(j * SUPER, SUPER)]))
                    dve.wait_ge(drow_in[s], 16 * (i + 1))
                    for t in range(SUPER):
                        e = dve.tensor_scalar(equal[s][:, t, :], drow[s][:, t, :], dcol[s][:, t:t + 1], None, ALU.is_equal)
                    e.then_inc(front_done, 1)
                else:
                    for t in range(SUPER):
                        dve.wait_ge(out_done[t], 16 * others)
                    dve.tensor_copy(out[s][:, :, HEADS:HEADS + 1].rearrange("p t a -> p (t a)"),
                                    keep.dst_f[:, bass.ds(j * SUPER, SUPER)]).then_inc(front_done, 1)

            def logits(i, s, t, link):
                j = 2 * i + s
                link(dve.tensor_tensor(product[:, :], pL[t % 2][:, :], side[s][:, t, 0:D], ALU.mult))
                dve.sem_inc(second_used, 1)
                link(dve.tensor_reduce(logit[:, :], product[:, :].rearrange("p (h d) -> p h d", h=HEADS), AX.X, ALU.add))
                link(dve.tensor_tensor(out[s][:, t, 0:HEADS], logit[:, :], side[s][:, t, D:Q_W], ALU.add))
                dve.wait_ge(front_done, j + 1)
                dve.sem_inc(out_ready, 1)

            def weigh(i, s, t):
                j = 2 * i + s
                dve.wait_ge(sum_done, SUPER * j + max(t - 1, 0))
                heads = side[s][:, t, :].unsqueeze(2).to_broadcast([P, HEADS, HEAD])
                dve.tensor_tensor(weighted[t % 2][:, 0:D].rearrange("p (h d) -> p h d", h=HEADS),
                                  pL[t % 2][:, :].rearrange("p (h d) -> p h d", h=HEADS), heads, ALU.mult)\
                   .then_inc(second_used, 1)
                dve.tensor_copy(weighted[t % 2][:, D:SUM_W], side[s][:, t, :]).then_inc(weighted_ready, 1)

            def body(i, s, nxt):
                j = 2 * i + s
                link = Chain(dve, own, j * LINKS + FRONT + 1)
                if nxt:
                    front(*nxt, link, j)
                for t in range(SUPER):
                    dve.wait_ge(second_done, SUPER * j + t + 1)
                    if t == 0:
                        dve.wait_ge(side_in[s], 64 * (i + 1))
                    if values:
                        weigh(i, s, t)
                    else:
                        logits(i, s, t, link)
                assert link.n == (LINKS if nxt else LINKS - FRONT)

            if values:
                dve.sem_inc(own, 1)
            else:
                for s in range(2):
                    z = dve.memset(out[s][:, :, :], 0.0)
                z.then_inc(own, 1)
            dve.wait_ge(own, 1)
            front(0, 0, Chain(dve, own, 1), 0)
            rolled(dve, body)

        @block.tensor
        def _(pe):
            def turn_ef(i, s):
                pe.wait_ge(ef_in[s], 16 * (i + 1))
                for t in range(SUPER):
                    mm = pe.transpose(pT[:, t * P:(t + 1) * P], ef[s][:, t, :], keep.ident[:, :])
                mm.then_inc(efT_turned, 1)

            def gram(i, s):
                pe.wait_ge(efT_ready, 2 * i + s + 1)
                for t in range(SUPER):
                    mm = pe.matmul(pG[:, t * EF:(t + 1) * EF], efT[:, t * P:(t + 1) * P], keep.gram[:, n_net, :],
                                   start=True, stop=True)
                mm.then_inc(gram_done, 1)

            def turn_ef_n(i, s):
                pe.wait_ge(diag_ready, SUPER * (2 * i + s + 1))
                for t in range(SUPER):
                    mm = pe.matmul(pT[:, t * P:(t + 1) * P], ef[s][:, t, :], diag[:, t, :], start=True, stop=True)
                mm.then_inc(efT_n_turned, 1)

            def first_layer(i, s, c):
                j = 2 * i + s
                if c == 0:
                    pe.wait_ge(efT_n_ready, j + 1)
                    pe.wait_ge(table_in[s], 64 * (i + 1))
                if c >= 2:
                    pe.wait_ge(hid_ready, KC * j + c - 1)
                feats = slice(c * P, (c + 1) * P)
                pe.matmul(pH[c % 2][:, :], keep.w1e[net][:, feats], efT_n[:, :], start=True, stop=False)
                for t in range(SUPER):
                    mm = pe.matmul(pH[c % 2][:, t * P:(t + 1) * P], table[s][:, t, feats], diag[:, t, :],
                                   start=False, stop=(t == SUPER - 1))
                mm.then_inc(hid_done, 1)

            def second_layer(i, s, t):
                j = 2 * i + s
                if t == 0:
                    pe.wait_ge(hid_ready, KC * (j + 1))
                if t != 1:
                    pe.wait_ge(second_used, SUPER * j + max(t - 1, 0))
                for c in range(KC):
                    mm = pe.matmul(pL[t % 2][:, :], hidT[:, c, t * P:(t + 1) * P], w2[:, c, :],
                                   start=(c == 0), stop=(c == KC - 1))
                mm.then_inc(second_done, 1)

            def add_rows(i, s, t):
                j = 2 * i + s
                if t == 0:
                    pe.wait_ge(front_done, j + 1)
                pe.wait_ge(weighted_ready, SUPER * j + t + 1)
                pe.wait_ge(sum_copied, 2 * (SUPER * j + t))
                pe.matmul(pS[:, :], equal[s][:, t, :], weighted[t % 2][:, 0:D], start=True, stop=True)
                pe.matmul(pD[:, 0:HEADS], equal[s][:, t, :], weighted[t % 2][:, D:SUM_W], start=True, stop=True)\
                  .then_inc(sum_done, 1)

            def body(i, s, nxt):
                for c in range(KC):
                    first_layer(i, s, c)
                    if c == 1 and nxt:
                        turn_ef(*nxt)
                if nxt:
                    gram(*nxt)
                for t in range(SUPER):
                    second_layer(i, s, t)
                    if values and t:
                        add_rows(i, s, t - 1)
                    if t == 2 and nxt:
                        turn_ef_n(*nxt)
                if values:
                    add_rows(i, s, SUPER - 1)

            pe.wait_ge(w2_loaded, 16)
            turn_ef(0, 0)
            gram(0, 0)
            turn_ef_n(0, 0)
            rolled(pe, body)


def segment_softmax(nc, keep, dram):
    with ExitStack() as ctx:
        m = Memory(nc, ctx, "soft")
        place = m.sb("place", [P, SPAN, L_W])
        dest = m.sb("dest", [P, SPAN])
        apart = m.sb("apart", [P, SPAN])
        ahead = m.sb("ahead", [P, SPAN])
        lead = m.sb("lead", [P, SPAN])
        trail = m.sb("trail", [P, SPAN])
        fwd = m.sb("fwd", [P, HEADS, SPAN])
        best = m.sb("best", [P, HEADS, SPAN])
        expo = m.sb("expo", [P, SPAN, HEADS])
        ends = m.sb("ends", [P, 4, HEADS])
        endsT = m.sb("endsT", [HEADS, 4, P])
        whole = m.sb("whole", [HEADS, P])
        joined = m.sb("joined", [HEADS, P])
        joined_b = m.sb("joined_b", [HEADS, P])
        through = m.sb("through", [HEADS, P])
        carry = m.sb("carry", [HEADS, 2, P])
        scanned = m.sb("scanned", [HEADS, 2, P])
        carry_in = m.sb("carry_in", [P, 2, HEADS])
        pA = m.ps("pA")
        pB = m.ps("pB")
        loaded = m.sem("loaded")
        own = m.sem("own")
        ends_ready = m.sem("ends_ready")
        turned = m.sem("turned")
        carry_ready = m.sem("carry_ready")
        carried = m.sem("carried")
        less = m.sem("less")
        expo_ready = m.sem("expo_ready")
        stored = m.sem("stored")
        block = ctx.enter_context(nc.Block())

        @block.sync
        def _(sp):
            sp.dma_start(place[:, :, :], dram.logits.rearrange("(p j) f -> p j f", p=P)).then_inc(loaded, 16)
            sp.wait_ge(expo_ready, 1)
            sp.dma_start(dram.expo.rearrange("(p j) f -> p j f", p=P), expo[:, :, :]).then_inc(stored, 16)
            sp.wait_ge(stored, 16)

        @block.scalar
        def _(act):
            act.wait_ge(less, 1)
            act.activation(expo[:, :, :], expo[:, :, :], ACT.Exp, scale=HEAD ** -0.5).then_inc(expo_ready, 1)

        @block.vector
        def _(dve):
            link = Chain(dve, own)
            dve.wait_ge(loaded, 16)
            link(dve.tensor_copy(dest[:, :].unsqueeze(2), place[:, :, HEADS:HEADS + 1]))
            link(dve.memset(apart[:, :], NEG))
            link(dve.memset(ahead[:, :], NEG))
            link(dve.tensor_tensor(apart[:, 1:SPAN], dest[:, 1:SPAN], dest[:, 0:SPAN - 1], ALU.not_equal))
            link(dve.tensor_scalar(apart[:, 1:SPAN], apart[:, 1:SPAN], NEG, None, ALU.mult))
            link(dve.tensor_copy(ahead[:, 0:SPAN - 1], apart[:, 1:SPAN]))
            link(dve.tensor_scalar(lead[:, :], dest[:, :], dest[:, 0:1], NEG, ALU.not_equal, ALU.mult))
            link(dve.tensor_scalar(trail[:, :], dest[:, :], dest[:, SPAN - 1:SPAN], NEG, ALU.not_equal, ALU.mult))
            for h in range(HEADS):
                s = dve.tensor_tensor_scan(fwd[:, h, :], apart[:, :], place[:, :, h:h + 1].rearrange("p j a -> p (j a)"),
                                           NEG, ALU.add, ALU.max)
            link(s)
            for h in range(HEADS):
                s = dve.tensor_tensor_scan(best[:, h, ::-1], ahead[:, ::-1], fwd[:, h, ::-1], NEG, ALU.add, ALU.max)
            link(s)
            link(dve.tensor_copy(ends[:, 0, :].unsqueeze(2), best[:, :, 0:1]))
            link(dve.tensor_copy(ends[:, 1, :].unsqueeze(2), best[:, :, SPAN - 1:SPAN]))
            link(dve.tensor_copy(ends[:, 2, :], dest[:, 0:1].to_broadcast([P, HEADS])))
            dve.tensor_copy(ends[:, 3, :], dest[:, SPAN - 1:SPAN].to_broadcast([P, HEADS])).then_inc(ends_ready, 1)
            dve.wait_ge(turned, 1)
            link(dve.tensor_copy(endsT[:, :, :].rearrange("h k p -> h (k p)"), pA[0:HEADS, :]))
            first, last = endsT[:, 2, :], endsT[:, 3, :]
            link(dve.memset(joined[:, :], NEG))
            link(dve.memset(joined_b[:, :], NEG))
            link(dve.tensor_tensor(whole[:, :], first, last, ALU.not_equal))
            link(dve.tensor_scalar(whole[:, :], whole[:, :], NEG, None, ALU.mult))
            link(dve.tensor_tensor(joined[:, 1:P], first[:, 1:P], last[:, 0:P - 1], ALU.not_equal))
            link(dve.tensor_scalar(joined[:, 1:P], joined[:, 1:P], NEG, None, ALU.mult))
            link(dve.tensor_copy(joined_b[:, 0:P - 1], joined[:, 1:P]))
            link(dve.memset(carry[:, :, :], NEG))
            link(dve.tensor_tensor(through[:, :], whole[:, :], joined[:, :], ALU.min))
            link(dve.tensor_tensor_scan(scanned[:, 0, :], through[:, :], endsT[:, 1, :], NEG, ALU.add, ALU.max))
            link(dve.tensor_tensor(through[:, :], whole[:, :], joined_b[:, :], ALU.min))
            link(dve.tensor_tensor_scan(scanned[:, 1, ::-1], through[:, ::-1], endsT[:, 0, ::-1], NEG, ALU.add, ALU.max))
            link(dve.tensor_tensor(carry[:, 0, 1:P], scanned[:, 0, 0:P - 1], joined[:, 1:P], ALU.add))
            dve.tensor_tensor(carry[:, 1, 0:P - 1], scanned[:, 1, 1:P], joined_b[:, 0:P - 1], ALU.add).then_inc(carry_ready, 1)
            dve.wait_ge(carried, 1)
            link(dve.tensor_copy(carry_in[:, :, :].rearrange("p k h -> p (k h)"), pB[:, 0:2 * HEADS]))
            for k, mask in enumerate((lead, trail)):
                for h in range(HEADS):
                    s = dve.scalar_tensor_tensor(out=best[:, h, :], in0=mask[:, :], scalar=carry_in[:, k, h:h + 1],
                                                 in1=best[:, h, :], op0=ALU.add, op1=ALU.max)
                link(s)
            dve.tensor_tensor(expo[:, :, :], place[:, :, 0:HEADS], best[:, :, :].rearrange("p h j -> p j h"), ALU.subtract)\
               .then_inc(less, 1)

        @block.tensor
        def _(pe):
            pe.wait_ge(ends_ready, 1)
            for k in range(4):
                mm = pe.transpose(pA[0:HEADS, k * P:(k + 1) * P], ends[:, k, :], keep.ident[:, :])
            mm.then_inc(turned, 1)
            pe.wait_ge(carry_ready, 1)
            for k in range(2):
                mm = pe.transpose(pB[:, k * HEADS:(k + 1) * HEADS], carry[:, k, :], keep.ident[0:HEADS, 0:HEADS])
            mm.then_inc(carried, 1)


def node_output(nc, w, keep, dram):
    with ExitStack() as ctx:
        m = Memory(nc, ctx, "outp")
        R = NODE_ROWS
        w1 = m.sb("w1", [P, 2 * KC, D])
        w2 = m.sb("w2", [P, KC, D])
        ws = m.sb("ws", [P, KC, EXPERTS])
        bs = m.sb("bs", [P, EXPERTS])
        b1 = m.sb("b1", [P, D])
        b2 = m.sb("b2", [P, D])
        b2v = m.sb("b2v", [P, D])
        g_col = m.sb("g_col", [P, KC])
        be_col = m.sb("be_col", [P, KC])
        eb2 = m.sb("eb2", [EXPERTS, D])
        order_i = m.sb("order_i", [P, EXPERTS], I32)
        order = m.sb("order", [P, EXPERTS])
        w_mean = m.sb("w_mean", [P, 2 * KC])
        b_mean = m.sb("b_mean", [P, 1])
        sums = m.sb("sums", [R, SUM_TABLES, SUM_W])
        some = m.sb("some", [R, HEADS])
        att = m.sb("att", [R, D])
        bias_v = m.sb("bias_v", [R, D])
        attT = m.sb("attT", [P, KC, R])
        hT = m.sb("hT", [P, KC, R])
        first = m.sb("first", [R, D])
        square = m.sb("square", [R, D])
        sumsq = m.sb("sumsq", [R, 1])
        var = m.sb("var", [R, 2])
        root = m.sb("root", [R, 2])
        rstd = m.sb("rstd", [R, 2])
        tmp = m.sb("tmp", [R, 2])
        normed = m.sb("normed", [R, D])
        normT = m.sb("normT", [P, KC, R])
        x1 = m.sb("x1", [R, D])
        stats = m.sb("stats", [R, 6])
        mv = m.sb("mv", [R, 2])
        z = m.sb("z", [R, D])
        zT = m.sb("zT", [P, KC, R])
        scores = m.sb("scores", [R, EXPERTS])
        top = m.sb("top", [R, 1])
        neg_top = m.sb("neg_top", [R, 1])
        chosen = m.sb("chosen", [R, EXPERTS])
        expo = m.sb("expo", [R, EXPERTS])
        total = m.sb("total", [R, 1])
        coef = m.sb("coef", [R, EXPERTS])
        coefT = m.sb("coefT", [EXPERTS, R])
        pA = m.ps("pA")
        pF = m.ps("pF")
        pN = m.ps("pN")
        pY = m.ps("pY")
        pZ = m.ps("pZ")
        pR = m.ps("pR")
        pC = m.ps("pC")
        pB = m.ps("pB")

        loaded = m.sem("loaded")
        ready = m.sem("weights_ready")
        order_ready = m.sem("order_ready")
        own = m.sem("own")
        sums_in = m.sem("sums_in")
        sums_used = m.sem("sums_used")
        att_ready = m.sem("att_ready")
        att_turned = m.sem("att_turned")
        attT_ready = m.sem("attT_ready")
        hT_ready = m.sem("hT_ready")
        first_done = m.sem("first_done")
        first_ready = m.sem("first_ready")
        squared = m.sem("squared")
        var_ready = m.sem("var_ready")
        root_ready = m.sem("root_ready")
        normed_ready = m.sem("normed_ready")
        norm_turned = m.sem("norm_turned")
        normT_ready = m.sem("normT_ready")
        second_done = m.sem("second_done")
        z_ready = m.sem("z_ready")
        z_turned = m.sem("z_turned")
        zT_ready = m.sem("zT_ready")
        zT_kept = m.sem("zT_kept")
        routed = m.sem("routed")
        top_ready = m.sem("top_ready")
        expo_ready = m.sem("expo_ready")
        coef_ready = m.sem("coef_ready")
        coef_turned = m.sem("coef_turned")
        coefT_ready = m.sem("coefT_ready")
        bias_done = m.sem("bias_done")
        SETUP = 2 + 2 * KC + 3 + 1
        LINKS = 2 * RECIPROCAL_ROOT_LINKS + 23
        block = ctx.enter_context(nc.Block())

        @block.sync
        def _(sp):
            def load(to, of):
                sp.dma_start(to, of, allow_slow_non_contiguous=True).then_inc(loaded, 16)

            load(w1[:, :, :], w["no_W1"].rearrange("(r p) n -> p r n", p=P))
            load(w2[:, :, :], w["no_W2"].rearrange("(r p) n -> p r n", p=P))
            load(ws[:, :, :], w["Ws"].rearrange("(r p) n -> p r n", p=P))
            load(bs[:, :], row_bc(w["bs"]))
            load(b1[:, :], row_bc(w["no_b1"]))
            load(b2[:, :], row_bc(w["no_b2"]))
            load(b2v[:, :], row_bc(w["hv_b2"]))
            load(g_col[:, :], col(w["no_g"]))
            load(be_col[:, :], col(w["no_be"]))
            load(eb2[:, :], w["b2"])
            with sp.Fori(0, NODE_TILES) as i:
                sp.wait_ge(sums_used, i)
                for t in range(SUM_TABLES):
                    sp.dma_start(sums[:, t, :], dram.sums[t][bass.ds(i * R, R), :]).then_inc(sums_in, 16)

        @block.gpsimd
        def _(pool):
            pool.iota(order_i[:, :], [[-1, EXPERTS]], base=EXPERTS, channel_multiplier=0).then_inc(order_ready, 1)
            with pool.Fori(0, NODE_TILES) as i:
                pool.wait_ge(first_done, i)
                wait_here(pool, keep.pool_passed)
                pool.tensor_copy(hT[:, :, :], keep.hT[:, :, bass.ds(i * R, R)]).then_inc(hT_ready, 1)
                pool.wait_ge(zT_ready, i + 1)
                wait_here(pool, keep.pool_passed)
                pool.tensor_copy(keep.hT[:, :, bass.ds(i * R, R)], zT[:, :, :]).then_inc(zT_kept, 1)

        @block.vector
        def _(dve):
            link = Chain(dve, own)
            dve.wait_ge(order_ready, 1)
            link(dve.tensor_copy(order[:, :], order_i[:, :]))
            dve.wait_ge(loaded, 160)
            link(dve.tensor_reduce(w_mean[:, :], w1[:, :, :], AX.X, ALU.add))
            link(dve.tensor_scalar(w_mean[:, :], w_mean[:, :], -1.0 / D, None, ALU.mult))
            for r in range(2 * KC):
                link(dve.tensor_scalar(w1[:, r, :], w1[:, r, :], w_mean[:, r:r + 1], None, ALU.add))
            link(dve.tensor_reduce(b_mean[:, :], b1[:, :], AX.X, ALU.add))
            link(dve.tensor_scalar(b_mean[:, :], b_mean[:, :], -1.0 / D, None, ALU.mult))
            link(dve.tensor_scalar(b1[:, :], b1[:, :], b_mean[:, :], None, ALU.add))
            assert link.n == SETUP
            dve.sem_inc(ready, 1)
            with dve.Fori(0, NODE_TILES) as i:
                link = Chain(dve, own, i * LINKS + SETUP)
                tile = bass.ds(i, 1)
                x = keep.x[:, tile, :].rearrange("p a n -> p (a n)")
                dve.wait_ge(sums_in, SUM_TABLES * 16 * (i + 1))
                for t in range(1, SUM_TABLES):
                    link(dve.tensor_tensor(sums[:, 0, :], sums[:, 0, :], sums[:, t, :], ALU.add))
                den = sums[:, 0, D:SUM_W]
                link(dve.tensor_scalar(some[:, :], den, 0.0, None, ALU.is_gt))
                link(dve.tensor_scalar(den, den, 1e-30, None, ALU.max))
                link(dve.reciprocal(den, den))
                dve.wait_ge(att_turned, i)
                link(dve.tensor_tensor(att[:, :].rearrange("p (h d) -> p h d", h=HEADS),
                                       sums[:, 0, 0:D].rearrange("p (h d) -> p h d", h=HEADS),
                                       den.unsqueeze(2).to_broadcast([R, HEADS, HEAD]), ALU.mult))
                dve.sem_inc(sums_used, 1)
                link(dve.tensor_tensor(bias_v[:, :].rearrange("p (h d) -> p h d", h=HEADS),
                                       b2v[0:R, :].rearrange("p (h d) -> p h d", h=HEADS),
                                       some[:, :].unsqueeze(2).to_broadcast([R, HEADS, HEAD]), ALU.mult))
                dve.tensor_tensor(att[:, :], att[:, :], bias_v[:, :], ALU.add).then_inc(att_ready, 1)
                dve.wait_ge(first_done, i + 1)
                dve.tensor_tensor(first[:, :], pF[0:R, :], b1[0:R, :], ALU.add).then_inc(first_ready, 1)
                dve.wait_ge(squared, i + 1)
                dve.tensor_scalar(var[:, 0:1], sumsq[:, :], EPS, None, ALU.add).then_inc(var_ready, 1)
                dve.wait_ge(root_ready, 2 * i + 1)
                reciprocal_root(dve, link, var[:, 0:1], root[:, 0:1], rstd[:, 0:1], tmp[:, 0:1])
                dve.tensor_scalar(normed[:, :], first[:, :], rstd[:, 0:1], None, ALU.mult).then_inc(normed_ready, 1)
                dve.wait_ge(second_done, i + 1)
                link(dve.tensor_tensor(x1[:, :], pY[0:R, :], b2[0:R, :], ALU.add))
                link(dve.tensor_tensor(x1[:, :], x1[:, :], keep.h[:, tile, :].rearrange("p a n -> p (a n)"), ALU.add))
                link(dve.tensor_tensor(x1[:, :], x1[:, :], x, ALU.add))
                link(dve.bn_stats(stats[:, :], x1[:, :]))
                wait_here(dve, keep.dve_passed)
                link(dve.bn_aggr(mv[:, :], stats[:, :]))
                dve.tensor_scalar(var[:, 1:2], mv[:, 1:2], EPS, None, ALU.add).then_inc(var_ready, 1)
                dve.wait_ge(root_ready, 2 * i + 2)
                reciprocal_root(dve, link, var[:, 1:2], root[:, 1:2], rstd[:, 1:2], tmp[:, 1:2])
                dve.tensor_scalar(z[:, :], x1[:, :], mv[:, 0:1], rstd[:, 1:2], ALU.subtract, ALU.mult).then_inc(z_ready, 1)
                dve.wait_ge(routed, i + 1)
                link(dve.tensor_tensor(scores[:, :], pR[0:R, 0:EXPERTS], bs[0:R, :], ALU.add))
                link(dve.tensor_reduce(top[:, :], scores[:, :], AX.X, ALU.max))
                dve.tensor_scalar(neg_top[:, :], top[:, :], -1.0, None, ALU.mult).then_inc(top_ready, 1)
                link(dve.scalar_tensor_tensor(out=chosen[:, :], in0=scores[:, :], scalar=top[:, 0:1], in1=order[0:R, :],
                                              op0=ALU.is_equal, op1=ALU.mult))
                link(dve.tensor_reduce(top[:, :], chosen[:, :], AX.X, ALU.max))
                link(dve.tensor_scalar(chosen[:, :], chosen[:, :], top[:, 0:1], None, ALU.is_equal))
                dve.wait_ge(expo_ready, i + 1)
                link(dve.reciprocal(total[:, :], total[:, :]))
                link(dve.tensor_scalar(coef[:, :], chosen[:, :], total[:, 0:1], None, ALU.mult))
                dve.sem_inc(coef_ready, 1)
                link(dve.tensor_copy(keep.coef[:, :, tile], coef[:, :].unsqueeze(2)))
                dve.wait_ge(coef_turned, i + 1)
                link(dve.tensor_copy(coefT[:, :], pC[0:EXPERTS, 0:R]))
                dve.sem_inc(coefT_ready, 1)
                dve.wait_ge(bias_done, i + 1)
                link(dve.tensor_tensor(x, x1[:, :], pB[0:R, :], ALU.add))
                assert link.n == LINKS, link.n

        @block.scalar
        def _(act):
            with act.Fori(0, NODE_TILES) as i:
                act.wait_ge(att_turned, i + 1)
                act.activation(attT[:, :, :], pA[:, 0:KC * R].rearrange("p (c r) -> p c r", c=KC), ACT.Copy)\
                   .then_inc(attT_ready, 1)
                act.wait_ge(first_ready, i + 1)
                act.activation(square[:, :], first[:, :], ACT.Square, scale=D ** -0.5, accum_out=sumsq[:, :])\
                   .then_inc(squared, 1)
                act.wait_ge(var_ready, 2 * i + 1)
                act.activation(root[:, 0:1], var[:, 0:1], ACT.Sqrt).then_inc(root_ready, 1)
                act.wait_ge(norm_turned, i + 1)
                for c in range(KC):
                    act.activation(normT[:, c, :], pN[:, c * R:(c + 1) * R], ACT.Relu, bias=be_col[:, c:c + 1],
                                   scale=g_col[:, c:c + 1]).then_inc(normT_ready, 1)
                act.wait_ge(var_ready, 2 * i + 2)
                act.activation(root[:, 1:2], var[:, 1:2], ACT.Sqrt).then_inc(root_ready, 1)
                act.wait_ge(z_turned, i + 1)
                act.wait_ge(zT_kept, i)
                act.activation(zT[:, :, :], pZ[:, 0:KC * R].rearrange("p (c r) -> p c r", c=KC), ACT.Copy)\
                   .then_inc(zT_ready, 1)
                act.wait_ge(top_ready, i + 1)
                act.activation(expo[:, :], scores[:, :], ACT.Exp, bias=neg_top[:, 0:1], accum_out=total[:, :])\
                   .then_inc(expo_ready, 1)

        @block.tensor
        def _(pe):
            def turn(to, of):
                for c in range(KC):
                    mm = pe.transpose(to[:, c * R:(c + 1) * R], of[:, c * P:(c + 1) * P], keep.ident[0:R, 0:R])
                return mm

            pe.wait_ge(ready, 1)
            with pe.Fori(0, NODE_TILES) as i:
                pe.wait_ge(att_ready, i + 1)
                turn(pA, att).then_inc(att_turned, 1)
                pe.wait_ge(hT_ready, i + 1)
                for c in range(KC):
                    pe.matmul(pF[0:R, :], hT[:, c, :], w1[:, KC + c, :], start=(c == 0), stop=False)
                pe.wait_ge(attT_ready, i + 1)
                for c in range(KC):
                    mm = pe.matmul(pF[0:R, :], attT[:, c, :], w1[:, c, :], start=False, stop=(c == KC - 1))
                mm.then_inc(first_done, 1)
                pe.wait_ge(normed_ready, i + 1)
                turn(pN, normed).then_inc(norm_turned, 1)
                pe.wait_ge(normT_ready, KC * (i + 1))
                for c in range(KC):
                    mm = pe.matmul(pY[0:R, :], normT[:, c, :], w2[:, c, :], start=(c == 0), stop=(c == KC - 1))
                mm.then_inc(second_done, 1)
                pe.wait_ge(z_ready, i + 1)
                turn(pZ, z).then_inc(z_turned, 1)
                pe.wait_ge(zT_ready, i + 1)
                for c in range(KC):
                    mm = pe.matmul(pR[0:R, 0:EXPERTS], zT[:, c, :], ws[:, c, :], start=(c == 0), stop=(c == KC - 1))
                mm.then_inc(routed, 1)
                pe.wait_ge(coef_ready, i + 1)
                pe.transpose(pC[0:EXPERTS, 0:R], coef[:, :], keep.ident[0:R, 0:R]).then_inc(coef_turned, 1)
                pe.wait_ge(coefT_ready, i + 1)
                pe.matmul(pB[0:R, :], coefT[:, :], eb2[:, :], start=True, stop=True).then_inc(bias_done, 1)


def experts(nc, w, keep, out):
    with ExitStack() as ctx:
        m = Memory(nc, ctx, "ffn")
        R = NODE_ROWS
        GROUPS = [(0, 4), (4, 4), (8, 2)]
        w1 = [m.sb(f"w1_{s}", [P, KC, FF]) for s in range(2)]
        w2 = [m.sb(f"w2_{s}", [P, FC, D]) for s in range(2)]
        b1 = [m.sb(f"b1_{s}", [P, FC]) for s in range(2)]
        coef = [m.sb(f"coef{s}", [R, NODE_TILES]) for s in range(2)]
        hid = [m.sb(f"hid{b}", [P, FC, 4 * R]) for b in range(2)]
        pH = [m.ps(f"pH{b}") for b in range(2)]
        pY = [m.ps(f"pY{b}") for b in range(3)]
        w_in = [m.sem(f"w_in{s}") for s in range(2)]
        coef_ready = m.sem("coef_ready")
        hid_done = m.sem("hid_done")
        hid_ready = m.sem("hid_ready")
        out_done = m.sem("out_done")
        added = m.sem("added")
        stored = m.sem("stored")
        NG = len(GROUPS)
        block = ctx.enter_context(nc.Block())

        @block.sync
        def _(sp):
            with sp.Fori(0, EXPERTS // 2) as i:
                for s in range(2):
                    e = bass.ds(2 * i + s, 1)
                    sp.wait_ge(out_done, 2 * i * NODE_TILES)
                    sp.dma_start(w1[s][:, :, :], w["W1"][e, :, :].rearrange("a (r p) n -> p (a r) n", p=P)).then_inc(w_in[s], 16)
                    sp.dma_start(w2[s][:, :, :], w["W2"][e, :, :].rearrange("a (r p) n -> p (a r) n", p=P)).then_inc(w_in[s], 16)
                    sp.dma_start(b1[s][:, :], w["b1"][e, :].rearrange("a (c p) -> p (a c)", p=P),
                                 allow_slow_non_contiguous=True).then_inc(w_in[s], 16)
            sp.wait_ge(added, EXPERTS * NODE_TILES)
            sp.dma_start(out.rearrange("(t p) n -> p t n", p=R), keep.x[:, :, :]).then_inc(stored, 16)
            sp.wait_ge(stored, 16)

        @block.scalar
        def _(act):
            with act.Fori(0, EXPERTS // 2) as i:
                for s in range(2):
                    for g, (t0, n) in enumerate(GROUPS):
                        k = (2 * i + s) * NG + g
                        if g == 2:
                            act.wait_ge(out_done, (2 * i + s) * NODE_TILES + 4)
                        else:
                            act.wait_ge(out_done, (2 * i + s) * NODE_TILES)
                        for f in range(FC):
                            act.wait_ge(hid_done, k * FC + f + 1)
                            act.activation(hid[g % 2][:, f, 0:n * R], pH[f][:, 0:n * R], ACT.Gelu, bias=b1[s][:, f:f + 1])\
                               .then_inc(hid_ready, 1)

        @block.vector
        def _(dve):
            with dve.Fori(0, EXPERTS // 2) as i:
                for s in range(2):
                    e = 2 * i + s
                    dve.tensor_copy(coef[s][:, :].unsqueeze(1), keep.coef[:, bass.ds(e, 1), :]).then_inc(coef_ready, 1)
                    dve.wait_ge(coef_ready, e + 1)
                    dve.wait_ge(added, e * NODE_TILES)
                    for t in range(NODE_TILES):
                        dve.wait_ge(out_done, e * NODE_TILES + t + 1)
                        dve.scalar_tensor_tensor(out=keep.x[:, t, :], in0=pY[t % 3][0:R, :], scalar=coef[s][:, t:t + 1],
                                                 in1=keep.x[:, t, :], op0=ALU.mult, op1=ALU.add).then_inc(added, 1)

        @block.tensor
        def _(pe):
            with pe.Fori(0, EXPERTS // 2) as i:
                for s in range(2):
                    e = 2 * i + s
                    pe.wait_ge(w_in[s], 48 * (i + 1))

                    def hidden(g):
                        t0, n = GROUPS[g]
                        for f in range(FC):
                            pe.wait_ge(hid_ready, (e * NG + g) * FC)
                            for c in range(KC):
                                mm = pe.matmul(pH[f][:, 0:n * R], w1[s][:, c, f * P:(f + 1) * P],
                                               keep.hT[:, c, t0 * R:(t0 + n) * R], start=(c == 0), stop=(c == KC - 1))
                            mm.then_inc(hid_done, 1)

                    def output(g):
                        t0, n = GROUPS[g]
                        pe.wait_ge(hid_ready, (e * NG + g + 1) * FC)
                        for t in range(t0, t0 + n):
                            pe.wait_ge(added, e * NODE_TILES + max(t - 2, 0))
                            for f in range(FC):
                                mm = pe.matmul(pY[t % 3][0:R, :], hid[g % 2][:, f, (t - t0) * R:(t - t0 + 1) * R],
                                               w2[s][:, f, :], start=(f == 0), stop=(f == FC - 1))
                            mm.then_inc(out_done, 1)

                    for g in range(NG):
                        hidden(g)
                        output(g)


class Tables:

    def __init__(self, nc):
        def table(name, shape):
            return nc.dram_tensor(name, shape, F32, kind="Internal").ap()

        self.dst_rows = table("dst_rows", [EDGE_TILES, P])
        self.table = [table(f"first_layer_{x}", [NODES, TABLE_W]) for x in "kv"]
        self.query = table("query", [NODES, Q_W])
        self.logits = table("logits", [PLACES, L_W])
        self.expo = table("expo", [PLACES, HEADS])
        self.sums = [table(f"sums{t}", [SUM_ROWS, SUM_W]) for t in range(SUM_TABLES)]


class Keep:

    def __init__(self, m):
        self.ident = m.sb("ident", [P, P])
        self.x = m.sb("x", [NODE_ROWS, NODE_TILES, D])
        self.h = m.sb("h", [NODE_ROWS, NODE_TILES, D])
        self.hT = m.sb("hT", [P, KC, NODES])
        self.coef = m.sb("coef", [NODE_ROWS, EXPERTS, NODE_TILES])
        self.src_i = m.sb("src_i", [P, EDGE_TILES], I32)
        self.dst_i = m.sb("dst_i", [P, EDGE_TILES], I32)
        self.dst_f = m.sb("dst_f", [P, EDGE_TILES])
        self.sum_i = m.sb("sum_i", [P, EDGE_TILES], I32)
        self.place_i = m.sb("place_i", [P, EDGE_TILES], I32)
        self.w1e = {x: m.sb(f"w1e_{x}", [P, D]) for x in "kv"}
        self.gram = m.sb("gram", [P, 2, EF])
        self.be = {x: m.sb(f"be_{x}", [P, KC]) for x in "kvq"}
        self.x_loaded = m.sem("x_loaded")
        self.pool_passed = m.sem("pool_passed")
        self.dve_passed = m.sem("dve_passed")

    def for_nodes(self, m):
        self.w1 = {x: m.sb(f"w1_{x}", [P, 4 if x == "q" else 5, D]) for x in "kvq"}
        self.b1 = {x: m.sb(f"b1_{x}", [P, D]) for x in "kvq"}
        self.g = {x: m.sb(f"g_{x}", [P, D]) for x in "kv"}
        self.g_col_q = m.sb("g_col_q", [P, KC])
        self.b2q = m.sb("b2q", [P, D])
        self.b2k = m.sb("b2k", [P, D])
        self.w_p = m.sb("w_p", [P, 2, KC, EF])
        self.b_p = m.sb("b_p", [P, 2, EF])


def build(nc, w, out):
    dram = Tables(nc)
    with ExitStack() as ctx:
        keep = Keep(Memory(nc, ctx, "keep"))
        with ExitStack() as early:
            keep.for_nodes(Memory(nc, early, "early"))
            prepare_weights(nc, w, keep, dram)
            node_tables(nc, w, keep, dram)
        edge_phase(nc, w, keep, dram, values=False)
        segment_softmax(nc, keep, dram)
        edge_phase(nc, w, keep, dram, values=True)
        node_output(nc, w, keep, dram)
        experts(nc, w, keep, out)


_GNN = [f"{x}_{y}" for x in ("hk", "hv", "hq", "no") for y in ("W1", "b1", "g", "be", "W2", "b2")]
_FFN = ["Ws", "bs", "W1", "b1", "W2", "b2"]
_NAMES = {"x": "x", "src": "src", "dst": "dst", "edge_attr_128": "edge_attr_128",
          **{f"L0_gnn_{x}": x for x in _GNN}, **{f"L0_ffn_{x}": x for x in _FFN}}


def kernel(**inputs):
    import numpy as _np
    import concourse.bacc as _bacc
    from concourse import mybir as _mybir
    from concourse.bass_utils import run_bass_kernel_spmd as _run

    nc = _bacc.Bacc("TRN2", target_bir_lowering=False, num_devices=1)
    arrays, w = {}, {}
    for name, short in _NAMES.items():
        a = _np.ascontiguousarray(inputs[name])
        arrays[f"in_{name}"] = a
        w[short] = nc.dram_tensor(f"in_{name}", a.shape, _mybir.dt.from_np(a.dtype), kind="ExternalInput").ap()
    out = nc.dram_tensor("out_0", (NODES, D), _mybir.dt.float32, kind="ExternalOutput").ap()
    build(nc, w, out)
    r = _run(nc, [arrays], core_ids=[0])
    return r.results[0]["out_0"]
```

```python
from contextlib import ExitStack

import concourse.bass as bass
from concourse import mybir

ALU = mybir.AluOpType
ACT = mybir.ActivationFunctionType
AX = mybir.AxisListType
F32 = mybir.dt.float32
F32R = mybir.dt.float32r
I32 = mybir.dt.int32

P = 128
NODES, D = 1250, 512
KC = D // P
NODE_ROWS = 125
NODE_TILES = NODES // NODE_ROWS
EDGES, EF = 20000, 128
EDGE_ROWS = 125
PADS = P - EDGE_ROWS
EDGE_TILES = EDGES // EDGE_ROWS
SUPER = 4
SUPERS = EDGE_TILES // SUPER
PLACES = EDGE_TILES * P
SPAN = PLACES // P
HEADS = 16
HEAD = D // HEADS
HALF = EDGE_TILES // 2
EXPERTS, FF = 8, 256
FC = FF // P
EPS = 1e-5
NEG = -1.0e38

Q_W = D + HEADS
L_W = HEADS + 4
SUM_W = D + HEADS
SUM_ROWS = 11 * P
SUM_TABLES = 4

assert NODE_TILES * NODE_ROWS == NODES and EDGE_TILES * EDGE_ROWS == EDGES and SUPERS * SUPER == EDGE_TILES
assert SUM_ROWS >= NODES + P


class Chain:

    def __init__(self, eng, sem, base=0):
        self.eng, self.sem, self.base, self.n = eng, sem, base, 0

    def __call__(self, instruction):
        self.n += 1
        instruction.then_inc(self.sem, 1)
        self.eng.wait_ge(self.sem, self.base + self.n)


class Memory:

    def __init__(self, nc, ctx, prefix):
        self.nc, self.ctx, self.prefix, self.sems = nc, ctx, prefix, []
        ctx.callback(self.release)

    def release(self):
        if self.sems:
            self.nc.clear_and_free_semaphores(self.sems)
            self.nc.all_engine_barrier()

    def sb(self, name, shape, dtype=F32):
        return self.ctx.enter_context(self.nc.sbuf_tensor(f"{self.prefix}_{name}", shape, dtype))

    def ps(self, name, shape=(P, D)):
        return self.ctx.enter_context(self.nc.psum_tensor(f"{self.prefix}_{name}", list(shape), F32))

    def sem(self, name):
        self.sems.append(self.nc.alloc_semaphore(name=f"{self.prefix}_{name}"))
        return self.sems[-1]


def row_bc(vector):
    return vector.partition_broadcast(P)


def col(vector):
    return vector.rearrange("(c p) -> p c", p=P)


def reciprocal_root(dve, link, var, root, out, tmp):
    link(dve.reciprocal(out, root))
    link(dve.tensor_tensor(tmp, out, out, ALU.mult))
    link(dve.tensor_tensor(tmp, tmp, var, ALU.mult))
    link(dve.tensor_scalar(tmp, tmp, -0.5, 1.5, ALU.mult, ALU.add))
    link(dve.tensor_tensor(out, out, tmp, ALU.mult))


RECIPROCAL_ROOT_LINKS = 5


def wait_here(eng, passed):
    eng.sem_inc(passed, 1)


def prepare_weights(nc, w, keep, dram):
    with ExitStack() as ctx:
        m = Memory(nc, ctx, "prep")
        mean = m.sb("mean", [P, 3, 5])
        b_mean = m.sb("b_mean", [P, 3])
        rows_i = m.sb("rows_i", [HALF, 2, 2, EDGE_ROWS], I32)
        rows = m.sb("rows", [HALF, 2, 2, P])
        pad_i = m.sb("pad_i", [HALF, 2, P], I32)
        zero = m.sb("zero", [P, SUM_W])
        earlier = m.sb("earlier", [P, P])
        drow = m.sb("drow", [P, 2, 16, P])
        same = m.sb("same", [P, 16, P])
        lead = m.sb("lead", [P, EDGE_TILES])
        flag = m.sb("flag", [P, EDGE_TILES])
        fill = m.sb("fill", [P, EDGE_TILES])
        fill_i = m.sb("fill_i", [P, EDGE_TILES], I32)
        pI = m.ps("pI")

        loaded = [m.sem(f"loaded_{x}") for x in "kvq"]
        small = m.sem("small_loaded")
        idx_loaded = m.sem("idx_loaded")
        consts = m.sem("consts")
        pool_own = m.sem("pool_own")
        dve_own = m.sem("dve_own")
        rows_ready = m.sem("rows_ready")
        rows_turned = m.sem("rows_turned")
        stored = m.sem("stored")
        zeroed = m.sem("zeroed")
        drow_in = [m.sem(f"drow_in{i}") for i in range(2)]
        drow_used = m.sem("drow_used")
        dst_table = m.sem("dst_table")
        nets = [("k", 5), ("v", 5), ("q", 4)]
        GROUPS = EDGE_TILES // 16

        block = ctx.enter_context(nc.Block())

        @block.sync
        def _(sp):
            for n, (x, tiles) in enumerate(nets):
                sp.dma_start(keep.w1[x][:, :, :], w[f"h{x}_W1"].rearrange("(r p) n -> p r n", p=P)).then_inc(loaded[n], 16)
            sp.dma_start(keep.x[:, :, :], w["x"].rearrange("(t p) n -> p t n", p=NODE_ROWS)).then_inc(keep.x_loaded, 16)
            sp.wait_ge(rows_ready, 2)
            for half in range(2):
                sp.dma_start(dram.dst_rows[half * HALF:(half + 1) * HALF, :], rows[:, half, 1, :]).then_inc(stored, 16)
            sp.wait_ge(stored, 32)
            for g in range(GROUPS):
                if g >= 2:
                    sp.wait_ge(drow_used, g - 1)
                src = dram.dst_rows[16 * g:16 * g + 16, :].rearrange("t p -> (t p)").partition_broadcast(P)
                sp.dma_start(drow[:, g % 2, :, :].rearrange("p t e -> p (t e)"), src).then_inc(drow_in[g % 2], 16)
            sp.wait_ge(zeroed, SUM_TABLES * 16)

        @block.scalar
        def _(act):
            for half in range(2):
                for i, name in enumerate(("src", "dst")):
                    act.dma_start(rows_i[:, half, i, :],
                                  w[name].rearrange("(h t p) -> h t p", h=2, p=EDGE_ROWS)[half]).then_inc(idx_loaded, 16)
            for x, _ in nets:
                act.dma_start(keep.b1[x][:, :], row_bc(w[f"h{x}_b1"])).then_inc(small, 16)
            act.dma_start(keep.be_q[:, :], col(w["hq_be"]), allow_slow_non_contiguous=True).then_inc(small, 16)
            act.dma_start(keep.g_col_q[:, :], col(w["hq_g"]), allow_slow_non_contiguous=True).then_inc(small, 16)
            act.dma_start(keep.b2q[:, :], row_bc(w["hq_b2"])).then_inc(small, 16)
            act.dma_start(keep.b2k[:, :], row_bc(w["hk_b2"])).then_inc(small, 16)
            act.wait_ge(consts, 1)
            for t in range(SUM_TABLES):
                act.dma_start(dram.sums[t].rearrange("(p r) f -> p r f", r=SUM_ROWS // P),
                              zero[:, :].unsqueeze(1).to_broadcast([P, SUM_ROWS // P, SUM_W])).then_inc(zeroed, 16)

        @block.gpsimd
        def _(pool):
            pool.memset(zero[:, :], 0.0).then_inc(consts, 1)
            pool.memset(keep.ident[:, :], 0.0).then_inc(pool_own, 1)
            pool.memset(earlier[:, :], 1.0).then_inc(pool_own, 1)
            pool.wait_ge(pool_own, 2)
            pool.affine_select(out=keep.ident[:, :], in_=keep.ident[:, :], compare_op=ALU.not_equal, fill=1.0,
                               base=0, pattern=[[-1, P]], channel_multiplier=1).then_inc(consts, 1)
            pool.affine_select(out=earlier[:, :], in_=earlier[:, :], compare_op=ALU.is_gt, fill=0.0,
                               base=0, pattern=[[-1, P]], channel_multiplier=1).then_inc(consts, 1)
            for half in range(2):
                pool.iota(pad_i[:, half, :], [[1, P]], base=NODES - EDGE_ROWS + PADS * HALF * half,
                          channel_multiplier=PADS).then_inc(consts, 1)
            pool.iota(keep.place_i[:, :], [[PADS, EDGE_TILES]], base=EDGES - EDGE_ROWS, channel_multiplier=1).then_inc(consts, 1)
            pool.iota(fill_i[:, :], [[0, EDGE_TILES]], base=NODES, channel_multiplier=1).then_inc(consts, 1)

        @block.vector
        def _(dve):
            link = Chain(dve, dve_own)
            dve.wait_ge(consts, 7)
            dve.wait_ge(idx_loaded, 64)
            link(dve.memset(rows[:, :, 0, :], 0.0))
            link(dve.tensor_copy(rows[:, :, 1, :], pad_i[:, :, :]))
            for i in range(2):
                dve.tensor_copy(rows[:, :, i, 0:EDGE_ROWS], rows_i[:, :, i, :]).then_inc(rows_ready, 1)
            dve.wait_ge(small, 7 * 16)
            for n, (x, tiles) in enumerate(nets):
                dve.wait_ge(loaded[n], 16)
                w1 = keep.w1[x]
                link(dve.tensor_reduce(mean[:, n, 0:tiles], w1[:, :, :], AX.X, ALU.add))
                link(dve.tensor_scalar(mean[:, n, 0:tiles], mean[:, n, 0:tiles], -1.0 / D, None, ALU.mult))
                for r in range(tiles):
                    to = keep.w1e[x][:, :] if r == KC else w1[:, r, :]
                    link(dve.tensor_scalar(to, w1[:, r, :], mean[:, n, r:r + 1], None, ALU.add))
                link(dve.tensor_reduce(b_mean[:, n:n + 1], keep.b1[x][:, :], AX.X, ALU.add))
                link(dve.tensor_scalar(b_mean[:, n:n + 1], b_mean[:, n:n + 1], -1.0 / D, None, ALU.mult))
                link(dve.tensor_scalar(keep.b1[x][:, :], keep.b1[x][:, :], b_mean[:, n:n + 1], None, ALU.add))
            dve.wait_ge(rows_turned, 1)
            turned_rows = pI[:, 0:4 * HALF].rearrange("p (i h t) -> p i h t", i=2, h=2)
            link(dve.tensor_copy(keep.src_i[:, :].rearrange("p (h t) -> p h t", h=2), turned_rows[:, 0, :, :]))
            link(dve.tensor_copy(keep.dst_f[:, :].rearrange("p (h t) -> p h t", h=2), turned_rows[:, 1, :, :]))
            link(dve.tensor_scalar(flag[:, :], keep.dst_f[:, :], float(NODES), None, ALU.is_lt))
            link(dve.tensor_tensor(fill[:, :], flag[:, :], keep.dst_f[:, :], ALU.mult))
            link(dve.tensor_copy(keep.dst_i[:, :], fill[:, :]))
            for g in range(GROUPS):
                dve.wait_ge(drow_in[g % 2], 16 * (g // 2 + 1))
                mine = keep.dst_f[:, 16 * g:16 * g + 16].unsqueeze(2).to_broadcast([P, 16, P])
                mm = dve.tensor_tensor(same[:, :, :], drow[:, g % 2, :, :], mine, ALU.is_equal)
                mm.then_inc(drow_used, 1)
                dve.wait_ge(drow_used, g + 1)
                link(dve.tensor_tensor(same[:, :, :], same[:, :, :],
                                       earlier[:, :].unsqueeze(1).to_broadcast([P, 16, P]), ALU.mult))
                link(dve.tensor_reduce(keep.in_rank[:, 16 * g:16 * g + 16], same[:, :, :], AX.X, ALU.add))
            link(dve.tensor_scalar(fill[:, :], keep.in_rank[:, :], 0.0, None, ALU.is_equal))
            link(dve.tensor_tensor(flag[:, :], flag[:, :], fill[:, :], ALU.mult))
            link(dve.tensor_copy(fill[:, :], fill_i[:, :]))
            link(dve.tensor_tensor(lead[:, :], keep.dst_f[:, :], fill[:, :], ALU.subtract))
            link(dve.tensor_tensor(lead[:, :], lead[:, :], flag[:, :], ALU.mult))
            link(dve.tensor_tensor(lead[:, :], lead[:, :], fill[:, :], ALU.add))
            link(dve.tensor_copy(keep.sum_i[:, :], lead[:, :]))

        @block.tensor
        def _(pe):
            pe.wait_ge(consts, 7)
            pe.wait_ge(rows_ready, 2)
            for i in range(2):
                for half in range(2):
                    k = 2 * i + half
                    mm = pe.transpose(pI[:, k * HALF:(k + 1) * HALF], rows[:, half, i, :], keep.ident[0:HALF, 0:HALF])
            mm.then_inc(rows_turned, 1)


def node_tables(nc, w, keep, dram):
    with ExitStack() as ctx:
        m = Memory(nc, ctx, "node")
        R = NODE_ROWS
        T = NODE_TILES
        w2q = m.sb("w2q", [P, KC, D])
        stats = m.sb("stats", [R, T, 6])
        mv = m.sb("mv", [R, T, 2])
        var = m.sb("var", [R, T])
        root = m.sb("root", [R, T])
        rstd = m.sb("rstd", [R, T])
        tmp = m.sb("tmp", [R, T])
        var_q = m.sb("var_q", [R, 1])
        root_q = m.sb("root_q", [R, 1])
        rstd_q = m.sb("rstd_q", [R, 1])
        tmp_q = m.sb("tmp_q", [R, 1])
        h = [m.sb(f"h{b}", [R, D]) for b in range(2)]
        first = m.sb("first", [R, D])
        square = m.sb("square", [R, D])
        sumsq = m.sb("sumsq", [R, 1])
        row = [m.sb(f"row{b}", [R, 2, D]) for b in range(2)]
        q_norm = m.sb("q_norm", [R, D])
        qT = m.sb("qT", [P, KC, R])
        q_row = [m.sb(f"q_row{b}", [R, Q_W]) for b in range(2)]
        q_bias = m.sb("q_bias", [R, D])
        pH = m.ps("pH")
        pF = {net: m.ps(f"pF_{net}") for net in "kvq"}
        pT = m.ps("pT")
        pQ = m.ps("pQ")

        w2_loaded = m.sem("w2_loaded")
        own = m.sem("dve_own")
        var_ready = m.sem("var_ready")
        root_ready = m.sem("root_ready")
        h_ready = m.sem("h_ready")
        h_stored = [m.sem(f"h_stored{b}") for b in range(2)]
        h_turned = m.sem("h_turned")
        hT_ready = m.sem("hT_ready")
        done = {net: m.sem(f"first_done_{net}") for net in "kvq"}
        taken = {net: m.sem(f"first_taken_{net}") for net in "kvq"}
        squared = m.sem("squared")
        normed = m.sem("normed")
        var_q_ready = m.sem("var_q_ready")
        root_q_ready = m.sem("root_q_ready")
        rows_stored = [m.sem(f"rows_stored{b}") for b in range(2)]
        q_turned = m.sem("q_turned")
        qT_ready = m.sem("qT_ready")
        q_done = m.sem("q_done")
        q_taken = m.sem("q_taken")
        q_ready = m.sem("q_ready")
        q_stored = [m.sem(f"q_stored{b}") for b in range(2)]

        block = ctx.enter_context(nc.Block())

        @block.sync
        def _(sp):
            sp.dma_start(w2q[:, :, :], w["hq_W2"].rearrange("(r p) n -> p r n", p=P)).then_inc(w2_loaded, 16)

            def store_query(n):
                sp.wait_ge(q_ready, n + 1)
                sp.dma_start(dram.query[n * R:(n + 1) * R, :], q_row[n % 2][:, :]).then_inc(q_stored[n % 2], 16)

            for n in range(T):
                rows = slice(n * R, (n + 1) * R)
                sp.wait_ge(h_ready, n + 1)
                sp.dma_start(dram.h[rows, :], h[n % 2][:, :]).then_inc(h_stored[n % 2], 16)
                if n:
                    store_query(n - 1)
                for k, net in enumerate("kv"):
                    sp.wait_ge(taken[net], n + 1)
                    sp.dma_start(dram.table[k][rows, :], row[n % 2][:, k, :]).then_inc(rows_stored[n % 2], 16)
            store_query(T - 1)
            for b in range(2):
                sp.wait_ge(h_stored[b], T // 2 * 16)
                sp.wait_ge(rows_stored[b], T // 2 * 32)
                sp.wait_ge(q_stored[b], T // 2 * 16)

        @block.vector
        def _(dve):
            link = Chain(dve, own)
            dve.wait_ge(keep.x_loaded, 16)
            for n in range(T):
                x = dve.bn_stats(stats[:, n, :], keep.x[:, n, :])
            link(x)
            for n in range(T):
                x = dve.bn_aggr(mv[:, n, :], stats[:, n, :])
            link(x)
            dve.tensor_scalar(var[:, :], mv[:, :, 1], EPS, None, ALU.add).then_inc(var_ready, 1)
            dve.wait_ge(root_ready, 1)
            reciprocal_root(dve, link, var[:, :], root[:, :], rstd[:, :], tmp[:, :])

            def normalise(n):
                if n >= 2:
                    dve.wait_ge(h_turned, n - 1)
                    dve.wait_ge(h_stored[n % 2], 16 * (n // 2))
                dve.tensor_scalar(h[n % 2][:, :], keep.x[:, n, :], mv[:, n, 0:1], rstd[:, n:n + 1], ALU.subtract, ALU.mult)\
                   .then_inc(h_ready, 1)

            def take_query(n):
                dve.wait_ge(done["q"], n + 1)
                if n:
                    dve.wait_ge(normed, n)
                dve.tensor_tensor(first[:, :], pF["q"][0:R, :], keep.b1["q"][0:R, :], ALU.add).then_inc(taken["q"], 1)

            def take_row(n, net):
                dve.wait_ge(done[net], n + 1)
                if n >= 2:
                    dve.wait_ge(rows_stored[n % 2], 32 * (n // 2))
                dve.tensor_tensor(row[n % 2][:, "kv".index(net), :], pF[net][0:R, :], keep.b1[net][0:R, :], ALU.add)\
                   .then_inc(taken[net], 1)

            def normalise_query(n):
                dve.wait_ge(squared, n + 1)
                dve.tensor_scalar(var_q[:, :], sumsq[:, :], EPS, None, ALU.add).then_inc(var_q_ready, 1)
                dve.wait_ge(root_q_ready, n + 1)
                reciprocal_root(dve, link, var_q[:, :], root_q[:, :], rstd_q[:, :], tmp_q[:, :])
                if n:
                    dve.wait_ge(q_turned, n)
                dve.tensor_scalar(q_norm[:, :], first[:, :], rstd_q[:, 0:1], None, ALU.mult).then_inc(normed, 1)

            def finish_query(n):
                to = q_row[n % 2]
                dve.wait_ge(q_done, n + 1)
                if n >= 2:
                    dve.wait_ge(q_stored[n % 2], 16 * (n // 2))
                link(dve.tensor_tensor(to[:, 0:D], pQ[0:R, :], keep.b2q[0:R, :], ALU.add))
                dve.sem_inc(q_taken, 1)
                link(dve.tensor_tensor(q_bias[:, :], to[:, 0:D], keep.b2k[0:R, :], ALU.mult))
                dve.tensor_reduce(to[:, D:Q_W], q_bias[:, :].rearrange("p (h d) -> p h d", h=HEADS), AX.X, ALU.add)\
                   .then_inc(q_ready, 1)

            normalise(0)
            for n in range(T):
                if n + 1 < T:
                    normalise(n + 1)
                take_query(n)
                normalise_query(n)
                take_row(n, "k")
                if n:
                    finish_query(n - 1)
                take_row(n, "v")
            finish_query(T - 1)

        @block.scalar
        def _(act):
            def copy_hT(n):
                act.wait_ge(h_turned, n + 1)
                act.activation(keep.hT[:, :, n * R:(n + 1) * R], pH[:, 0:KC * R].rearrange("p (c r) -> p c r", c=KC), ACT.Copy)\
                   .then_inc(hT_ready, 1)

            def squares(n):
                act.wait_ge(taken["q"], n + 1)
                if n:
                    act.wait_ge(squared, n)
                    act.wait_ge(var_q_ready, n)
                act.activation(square[:, :], first[:, :], ACT.Square, scale=D ** -0.5, accum_out=sumsq[:, :]).then_inc(squared, 1)

            act.wait_ge(var_ready, 1)
            act.activation(root[:, :], var[:, :], ACT.Sqrt).then_inc(root_ready, 1)
            copy_hT(0)
            for n in range(T):
                squares(n)
                act.wait_ge(var_q_ready, n + 1)
                act.activation(root_q[:, :], var_q[:, :], ACT.Sqrt).then_inc(root_q_ready, 1)
                if n + 1 < T:
                    copy_hT(n + 1)
                act.wait_ge(q_turned, n + 1)
                if n:
                    act.wait_ge(q_done, n)
                for c in range(KC):
                    q = act.activation(qT[:, c, :], pT[:, c * R:(c + 1) * R], ACT.Relu, bias=keep.be_q[:, c:c + 1],
                                       scale=keep.g_col_q[:, c:c + 1])
                q.then_inc(qT_ready, 1)

        @block.tensor
        def _(pe):
            def turn(to, of):
                for c in range(KC):
                    mm = pe.transpose(to[:, c * R:(c + 1) * R], of[:, c * P:(c + 1) * P], keep.ident[0:R, 0:R])
                return mm

            def turn_h(n):
                pe.wait_ge(h_ready, n + 1)
                if n:
                    pe.wait_ge(hT_ready, n)
                turn(pH, h[n % 2]).then_inc(h_turned, 1)

            def first_layer(n, net):
                if n:
                    pe.wait_ge(taken[net], n)
                for c in range(KC):
                    mm = pe.matmul(pF[net][0:R, :], keep.hT[:, c, n * R:(n + 1) * R], keep.w1[net][:, c, :],
                                   start=(c == 0), stop=(c == KC - 1))
                return mm

            def second_layer(n):
                pe.wait_ge(qT_ready, n + 1)
                if n:
                    pe.wait_ge(q_taken, n)
                for c in range(KC):
                    mm = pe.matmul(pQ[0:R, :], qT[:, c, :], w2q[:, c, :], start=(c == 0), stop=(c == KC - 1))
                mm.then_inc(q_done, 1)

            turn_h(0)
            for n in range(T):
                pe.wait_ge(hT_ready, n + 1)
                first_layer(n, "q").then_inc(done["q"], 1)
                first_layer(n, "k").then_inc(done["k"], 1)
                if n:
                    second_layer(n - 1)
                else:
                    pe.wait_ge(w2_loaded, 16)
                first_layer(n, "v").then_inc(done["v"], 1)
                if n + 1 < T:
                    turn_h(n + 1)
                pe.wait_ge(normed, n + 1)
                if n:
                    pe.wait_ge(qT_ready, n)
                turn(pT, q_norm).then_inc(q_turned, 1)
            second_layer(T - 1)


def rank_edges(nc, keep):
    with ExitStack() as ctx:
        m = Memory(nc, ctx, "rank")
        LOW = 32
        HIGH = -(-NODES // LOW)
        BANK = D // LOW
        TURN = 4
        R = EDGE_ROWS
        count_i = m.sb("count_i", [P, HIGH + 1], I32)
        bound = m.sb("bound", [P, HIGH + 1])
        low_no = m.sb("low_no", [P, LOW])
        before = m.sb("before", [HIGH, HIGH])
        reached = m.sb("reached", [P, EDGE_TILES, HIGH + 1])
        high = m.sb("high", [P, EDGE_TILES, HIGH])
        high_no = m.sb("high_no", [P, EDGE_TILES])
        low = m.sb("low", [P, EDGE_TILES, LOW])
        counts = m.sb("counts", [HIGH, LOW, EDGE_TILES])
        upto = m.sb("upto", [HIGH, LOW, EDGE_TILES])
        total = m.sb("total", [HIGH, 1])
        start = m.sb("start", [HIGH, 1])
        turned = [m.sb(f"turned{b}", [HIGH, TURN, R]) for b in range(2)]
        found = m.sb("found", [P, EDGE_TILES])
        base = reached[0:HIGH, :, 0:LOW]
        pC = [m.ps(f"pC{b}") for b in range(2)]
        pT = [m.ps(f"pT{b}") for b in range(2)]
        pL = [m.ps(f"pL{b}") for b in range(2)]
        pS = m.ps("pS")
        own = m.sem("own")
        consts = m.sem("consts")
        pool_own = m.sem("pool_own")
        high_ready = m.sem("high_ready")
        low_ready = m.sem("low_ready")
        counted = m.sem("counted")
        counts_ready = m.sem("counts_ready")
        total_ready = m.sem("total_ready")
        start_done = m.sem("start_done")
        base_ready = m.sem("base_ready")
        turn_done = m.sem("turn_done")
        turn_ready = m.sem("turn_ready")
        looked = m.sem("looked")
        read = m.sem("read")
        block = ctx.enter_context(nc.Block())

        @block.gpsimd
        def _(pool):
            pool.iota(count_i[:, :], [[1, HIGH + 1]], base=0, channel_multiplier=0).then_inc(consts, 1)
            pool.memset(before[:, :], 1.0).then_inc(pool_own, 1)
            pool.wait_ge(pool_own, 1)
            pool.affine_select(out=before[:, :], in_=before[:, :], compare_op=ALU.is_gt, fill=0.0,
                               base=0, pattern=[[1, HIGH]], channel_multiplier=-1).then_inc(consts, 1)

        @block.vector
        def _(dve):
            link = Chain(dve, own)
            dve.wait_ge(consts, 2)
            link(dve.tensor_copy(low_no[:, :], count_i[:, 0:LOW]))
            link(dve.tensor_copy(bound[:, :], count_i[:, :]))
            link(dve.tensor_scalar(bound[:, :], bound[:, :], float(LOW), None, ALU.mult))
            all_dst = keep.dst_f[:, :].unsqueeze(2).to_broadcast([P, EDGE_TILES, HIGH + 1])
            link(dve.tensor_tensor(reached[:, :, :], all_dst, bound[:, :].unsqueeze(1).to_broadcast([P, EDGE_TILES, HIGH + 1]),
                                   ALU.is_ge))
            dve.tensor_tensor(high[:, :, :], reached[:, :, 0:HIGH], reached[:, :, 1:HIGH + 1], ALU.subtract).then_inc(high_ready, 1)
            link(dve.tensor_reduce(high_no[:, :], reached[:, :, 1:HIGH + 1], AX.X, ALU.add))
            link(dve.scalar_tensor_tensor(out=high_no[:, :], in0=high_no[:, :], scalar=-float(LOW), in1=keep.dst_f[:, :],
                                          op0=ALU.mult, op1=ALU.add))
            dve.tensor_tensor(low[:, :, :], high_no[:, :].unsqueeze(2).to_broadcast([P, EDGE_TILES, LOW]),
                              low_no[:, :].unsqueeze(1).to_broadcast([P, EDGE_TILES, LOW]), ALU.is_equal).then_inc(low_ready, 1)
            dve.wait_ge(counts_ready, EDGE_TILES // BANK)
            flat = counts[:, :, :].rearrange("h l t -> h (l t)")
            link(dve.tensor_tensor_scan(upto[:, :, :].rearrange("h l t -> h (l t)"), flat, flat, 0.0, ALU.add, ALU.max))
            dve.tensor_copy(total[:, :], upto[:, LOW - 1, EDGE_TILES - 1:EDGE_TILES]).then_inc(total_ready, 1)
            dve.wait_ge(total_ready, 1)
            link(dve.tensor_tensor(upto[:, :, :], upto[:, :, :], counts[:, :, :], ALU.subtract))
            dve.wait_ge(start_done, 1)
            link(dve.tensor_copy(start[:, :], pS[0:HIGH, 0:1]))
            dve.wait_ge(low_ready, 1)
            dve.tensor_scalar(base, upto[:, :, :].rearrange("h l t -> h t l"), start[:, 0:1], None, ALU.add)\
               .then_inc(base_ready, 1)
            for g in range(EDGE_TILES // BANK):
                tiles = slice(g * BANK, (g + 1) * BANK)
                dve.wait_ge(looked, BANK * (g + 1))
                dve.tensor_tensor(low[0:R, tiles, :], pL[g % 2][0:R, :].rearrange("p (t l) -> p t l", t=BANK),
                                  low[0:R, tiles, :], ALU.mult).then_inc(read, 1)
            dve.wait_ge(read, EDGE_TILES // BANK)
            link(dve.tensor_reduce(found[0:R, :], low[0:R, :, :], AX.X, ALU.add))
            link(dve.tensor_tensor(found[0:R, :], found[0:R, :], keep.in_rank[0:R, :], ALU.add))
            link(dve.tensor_copy(keep.place_i[0:R, :], found[0:R, :]))

        @block.scalar
        def _(act):
            for g in range(EDGE_TILES // BANK):
                act.wait_ge(counted, g + 1)
                act.activation(counts[:, :, g * BANK:(g + 1) * BANK].rearrange("h l t -> h t l"),
                               pC[g % 2][0:HIGH, :].rearrange("h (t l) -> h t l", l=LOW), ACT.Copy).then_inc(counts_ready, 1)
            for k in range(EDGE_TILES // TURN):
                act.wait_ge(turn_done, k + 1)
                if k >= 2:
                    act.wait_ge(looked, TURN * (k - 1))
                act.activation(turned[k % 2][:, :, :].rearrange("h t e -> h (t e)"), pT[k % 2][0:HIGH, 0:TURN * R], ACT.Copy)\
                   .then_inc(turn_ready, 1)

        @block.tensor
        def _(pe):
            pe.wait_ge(low_ready, 1)
            pe.wait_ge(high_ready, 1)
            for g in range(EDGE_TILES // BANK):
                if g >= 2:
                    pe.wait_ge(counts_ready, g - 1)
                for k in range(BANK):
                    t = g * BANK + k
                    mm = pe.matmul(pC[g % 2][0:HIGH, k * LOW:(k + 1) * LOW], high[0:R, t, :], low[0:R, t, :],
                                   start=True, stop=True)
                mm.then_inc(counted, 1)

            def turn(k):
                if k >= 2:
                    pe.wait_ge(turn_ready, k - 1)
                for t in range(TURN):
                    mm = pe.transpose(pT[k % 2][0:HIGH, t * R:(t + 1) * R], high[0:R, k * TURN + t, :], keep.ident[0:R, 0:R])
                mm.then_inc(turn_done, 1)

            turn(0)
            pe.wait_ge(total_ready, 1)
            pe.matmul(pS[0:HIGH, 0:1], before[:, :], total[:, :], start=True, stop=True)\
              .then_inc(start_done, 1)
            pe.wait_ge(base_ready, 1)
            for k in range(EDGE_TILES // TURN):
                if k + 1 < EDGE_TILES // TURN:
                    turn(k + 1)
                pe.wait_ge(turn_ready, k + 1)
                for t in range(TURN):
                    tile = k * TURN + t
                    bank = tile // BANK
                    if tile % BANK == 0 and bank >= 2:
                        pe.wait_ge(read, bank - 1)
                    pe.matmul(pL[bank % 2][0:R, (tile % BANK) * LOW:(tile % BANK + 1) * LOW], turned[k % 2][:, t, :],
                              base[:, tile, :], start=True, stop=True).then_inc(looked, 1)


def awaits(eng, sem, value):
    if not isinstance(value, int) or value > 0:
        eng.wait_ge(sem, value)


def edge_phase(nc, w, keep, dram, values):
    net = "v" if values else "k"
    n_net = int(values)
    side_w = HEADS if values else Q_W
    with ExitStack() as ctx:
        m = Memory(nc, ctx, f"edge_{net}")
        w2_hi = m.sb("w2_hi", [P, KC, D], F32R)
        w2_lo = m.sb("w2_lo", [P, KC, D], F32R)
        w1_hi = m.sb("w1_hi", [P, D], F32R)
        w1_lo = m.sb("w1_lo", [P, D], F32R)
        g_col = m.sb("g_col", [P, KC])
        be_col = m.sb("be_col", [P, KC])
        split_weights(nc, w, keep, net, w2_hi, w2_lo, w1_hi, w1_lo, g_col, be_col)

        ef = [m.sb(f"ef{s}", [P, SUPER, EF]) for s in range(2)]
        table = [m.sb(f"table{s}", [P, SUPER, D]) for s in range(2)]
        side = [m.sb(f"side{s}", [P, SUPER, side_w]) for s in range(2)]
        src_at = [m.sb(f"src_at{s}", [P, SUPER], I32) for s in range(2)]
        side_at = [m.sb(f"side_at{s}", [P, SUPER], I32) for s in range(2)]
        out_at = [m.sb(f"out_at{s}", [P, SUPER], I32) for s in range(2)]
        efT_hi = [m.sb(f"efT_hi{s}", [EF, SUPER * P], F32R) for s in range(2)]
        efT_lo = [m.sb(f"efT_lo{s}", [EF, SUPER * P], F32R) for s in range(2)]
        first = [m.sb(f"first{t}", [P, D]) for t in range(SUPER)]
        square = m.sb("square", [P, D])
        sumsq = [m.sb(f"sumsq{t}", [P, 1]) for t in range(SUPER)]
        root = [m.sb(f"root{t}", [P, 1]) for t in range(SUPER)]
        rstd = [m.sb(f"rstd{t}", [P, 1]) for t in range(SUPER)]
        eps = m.sb("eps", [P, 1])
        var = m.sb("var", [P, 1])
        inverse = m.sb("inverse", [P, 1])
        error = m.sb("error", [P, 1])
        correction = m.sb("correction", [P, 1])
        hid = m.sb("hid", [P, KC, P])
        hid_hi = [m.sb(f"hid_hi{b}", [P, KC, P], F32R) for b in range(2)]
        hid_lo = [m.sb(f"hid_lo{b}", [P, KC, P], F32R) for b in range(2)]
        if values:
            drow = [m.sb(f"drow{s}", [P, SUPER, P]) for s in range(2)]
            dcol = m.sb("dcol", [P, SUPER])
            equal = [m.sb(f"equal{s}", [P, SUPER, P], F32R) for s in range(2)]
            weighted = m.sb("weighted", [P, SUM_W])
            weighted_hi = [m.sb(f"weighted_hi{b}", [P, SUM_W], F32R) for b in range(2)]
            weighted_lo = [m.sb(f"weighted_lo{b}", [P, SUM_W], F32R) for b in range(2)]
            out = [m.sb(f"out{s}", [P, SUPER, SUM_W]) for s in range(2)]
        else:
            product = m.sb("product", [P, D])
            logit = m.sb("logit", [P, HEADS])
            out = [m.sb(f"out{s}", [P, SUPER, L_W]) for s in range(2)]

        pE = m.ps("pE")
        pF = [m.ps(f"pF{b}") for b in range(2)]
        pH = m.ps("pH")
        pL = [m.ps(f"pL{b}") for b in range(2)]
        if values:
            pS = m.ps("pS")
            pD = m.ps("pD")
            drow_in = [m.sem(f"drow_in{s}") for s in range(2)]
            dcol_ready = m.sem("dcol_ready")
            equal_ready = m.sem("equal_ready")
            weighted_ready = m.sem("weighted_ready")
            weighted_hi_ready = m.sem("weighted_hi_ready")
            weighted_lo_ready = m.sem("weighted_lo_ready")
            sum_done = m.sem("sum_done")
            sum_copied = m.sem("sum_copied")
        else:
            dst_written = m.sem("dst_written")
            out_cleared = m.sem("out_cleared")
            heads_added = m.sem("heads_added")
            logits_ready = m.sem("logits_ready")

        cleared = m.sem("cleared")
        ef_in = [m.sem(f"ef_in{s}") for s in range(2)]
        table_in = [m.sem(f"table_in{s}") for s in range(2)]
        side_in = [m.sem(f"side_in{s}") for s in range(2)]
        src_copied = m.sem("src_copied")
        side_copied = m.sem("side_copied")
        out_copied = m.sem("out_copied")
        ef_turned = m.sem("ef_turned")
        efT_hi_ready = m.sem("efT_hi_ready")
        efT_lo_ready = m.sem("efT_lo_ready")
        first_done = m.sem("first_done")
        first_ready = m.sem("first_ready")
        squared = m.sem("squared")
        root_ready = m.sem("root_ready")
        var_ready = m.sem("var_ready")
        inverse_ready = m.sem("inverse_ready")
        error_ready = m.sem("error_ready")
        correction_ready = m.sem("correction_ready")
        rstd_ready = m.sem("rstd_ready")
        normed = m.sem("normed")
        turned = m.sem("turned")
        hid_ready = m.sem("hid_ready")
        hid_hi_ready = m.sem("hid_hi_ready")
        hid_lo_ready = m.sem("hid_lo_ready")
        second_done = m.sem("second_done")
        second_used = m.sem("second_used")
        out_ready = m.sem("out_ready")
        out_done = [m.sem(f"out_done{t}") for t in range(SUPER)]

        PAIRS = SUPERS // 2

        def rolled(eng, start, step, end):
            def pair(i):
                first_pair, last_pair = (isinstance(i, int) and i == k for k in (0, PAIRS - 1))
                for s in range(2):
                    def super_at(n):
                        if first_pair and s + n < 0 or last_pair and s + n > 1:
                            return None
                        return (i + (s + n) // 2, (s + n) % 2)

                    def tile_at(n, t):
                        where = super_at((t + n) // SUPER)
                        return where and (*where, (t + n) % SUPER)

                    start(super_at)
                    for t in range(SUPER):
                        step(t, lambda n: tile_at(n, t), super_at)

            pair(0)
            with eng.Fori(1, PAIRS - 1) as i:
                pair(i)
            pair(PAIRS - 1)
            end()

        def nothing(*_):
            pass

        def each(body, where, *more):
            if where:
                body(*where, *more)

        def number(i, s, t):
            return (2 * i + s) * SUPER + t

        LAST = [(PAIRS - 1, 1, t) for t in range(SUPER)]
        block = ctx.enter_context(nc.Block())

        @block.sync
        def _(sp):
            def load_ef(i, s):
                j = 2 * i + s
                awaits(sp, ef_turned, j - 1)
                sp.dma_start(ef[s][0:EDGE_ROWS, :, :],
                             w["edge_attr_128"][bass.ds(j * (SUPER * EDGE_ROWS), SUPER * EDGE_ROWS), :]
                             .rearrange("(t p) f -> p t f", t=SUPER)).then_inc(ef_in[s], 16)

            def load_drow(i, s):
                j = 2 * i + s
                awaits(sp, equal_ready, SUPER * (j - 1))
                sp.dma_start(drow[s][:, :, :].rearrange("p t e -> p (t e)"),
                             dram.dst_rows[bass.ds(j * SUPER, SUPER), :].rearrange("t p -> (t p)").partition_broadcast(P))\
                  .then_inc(drow_in[s], 16)

            def start(supertile):
                each(load_ef, supertile(2))
                if values:
                    each(load_drow, supertile(2))

            def end():
                for t in range(SUPER):
                    sp.wait_ge(out_done[t], 16 * SUPERS)

            sp.wait_ge(cleared, 3)
            for s in range(2):
                load_ef(0, s)
            if values:
                for s in range(2):
                    load_drow(0, s)
            rolled(sp, start, nothing, end)

        @block.gpsimd
        def _(pool):
            def gather_table(i, s):
                j = 2 * i + s
                awaits(pool, first_ready, SUPER * (j - 1))
                wait_here(pool, keep.pool_passed)
                pool.tensor_copy(src_at[s][:, :], keep.src_i[:, bass.ds(j * SUPER, SUPER)]).then_inc(src_copied, 1)
                pool.wait_ge(src_copied, j + 1)
                wait_here(pool, keep.pool_passed)
                for t in range(SUPER):
                    pool.indirect_dma_start(out=table[s][:, t, :], out_offset=None, in_=dram.table[n_net],
                                            in_offset=bass.IndirectOffsetOnAxis(ap=src_at[s][:, t:t + 1], axis=0))\
                        .then_inc(table_in[s], 16)

            def gather_side(i, s):
                j = 2 * i + s
                awaits(pool, weighted_ready if values else out_ready, SUPER * (j - 1))
                wait_here(pool, keep.pool_passed)
                pool.tensor_copy(side_at[s][:, :], (keep.place_i if values else keep.dst_i)[:, bass.ds(j * SUPER, SUPER)])\
                    .then_inc(side_copied, 1)
                pool.wait_ge(side_copied, j + 1)
                wait_here(pool, keep.pool_passed)
                for t in range(SUPER):
                    pool.indirect_dma_start(out=side[s][:, t, :], out_offset=None, in_=dram.expo if values else dram.query,
                                            in_offset=bass.IndirectOffsetOnAxis(ap=side_at[s][:, t:t + 1], axis=0))\
                        .then_inc(side_in[s], 16)

            def scatter(i, s, t):
                j = 2 * i + s
                if t == 0:
                    for u in range(SUPER):
                        awaits(pool, out_done[u], 16 * (j - 1))
                    wait_here(pool, keep.pool_passed)
                    pool.tensor_copy(out_at[s][:, :], (keep.sum_i if values else keep.place_i)[:, bass.ds(j * SUPER, SUPER)])\
                        .then_inc(out_copied, 1)
                    pool.wait_ge(out_copied, j + 1)
                pool.wait_ge(out_ready, number(i, s, t) + 1)
                awaits(pool, out_done[t], 16 * j)
                wait_here(pool, keep.pool_passed)
                where = bass.IndirectOffsetOnAxis(ap=out_at[s][:, t:t + 1], axis=0)
                if values:
                    pool.indirect_dma_start(out=dram.sums[t], out_offset=where, in_=out[s][:, t, :], in_offset=None,
                                            compute_op=ALU.add).then_inc(out_done[t], 16)
                else:
                    pool.indirect_dma_start(out=dram.logits, out_offset=where, in_=out[s][:, t, :],
                                            in_offset=None).then_inc(out_done[t], 16)

            BEHIND = 3 if values else 1

            def start(supertile):
                if supertile(-1):
                    scatter(*supertile(-1), SUPER - BEHIND)
                each(gather_side, supertile(1))
                each(gather_table, supertile(2))
                for t in range(SUPER - BEHIND + 1, SUPER):
                    if supertile(-1):
                        scatter(*supertile(-1), t)
                for t in range(SUPER - BEHIND):
                    scatter(*supertile(0), t)

            def end():
                for t in range(SUPER - BEHIND, SUPER):
                    scatter(*LAST[t])

            for s in range(2):
                pool.memset(ef[s][:, :, :], 0.0).then_inc(cleared, 1)
            gather_table(0, 0)
            gather_table(0, 1)
            gather_side(0, 0)
            rolled(pool, start, nothing, end)

        @block.scalar
        def _(act):
            def split_efT(i, s):
                act.wait_ge(ef_turned, 2 * i + s + 1)
                act.activation(efT_hi[s][:, :], pE[:, :], ACT.Copy).then_inc(efT_hi_ready, 1)

            def squares(i, s, t):
                n = number(i, s, t)
                act.wait_ge(first_ready, n + 1)
                awaits(act, squared, n)
                awaits(act, rstd_ready, n - SUPER + 1)
                act.activation(square[:, :], first[t][:, :], ACT.Square, scale=D ** -0.5, accum_out=sumsq[t][:, :])\
                   .then_inc(squared, 1)
                act.wait_ge(squared, n + 1)
                act.activation(root[t][:, :], sumsq[t][:, :], ACT.Sqrt, bias=eps[:, 0:1]).then_inc(root_ready, 1)

            def hidden(i, s, t):
                n = number(i, s, t)
                act.wait_ge(turned, n + 1)
                awaits(act, hid_lo_ready, n)
                for c in range(KC):
                    r = act.activation(hid[:, c, :], pH[:, c * P:(c + 1) * P], ACT.Relu, bias=be_col[:, c:c + 1],
                                       scale=g_col[:, c:c + 1])
                r.then_inc(hid_ready, 1)
                act.wait_ge(hid_ready, n + 1)
                awaits(act, second_done, n - 1)
                act.activation(hid_hi[t % 2][:, :, :], hid[:, :, :], ACT.Copy).then_inc(hid_hi_ready, 1)

            def split_weighted(i, s, t):
                n = number(i, s, t)
                act.wait_ge(second_used, n + 1)
                act.wait_ge(weighted_ready, n + 1)
                awaits(act, sum_done, n - 1)
                act.activation(weighted_hi[t % 2][:, :], weighted[:, :], ACT.Copy).then_inc(weighted_hi_ready, 1)

            def copy_sum(i, s, t):
                n = number(i, s, t)
                act.wait_ge(sum_done, n + 1)
                awaits(act, out_done[t], 16 * (2 * i + s - 1))
                act.activation(out[s][:, t, 0:D], pS[:, :], ACT.Copy).then_inc(sum_copied, 1)
                act.activation(out[s][:, t, D:SUM_W], pD[:, 0:HEADS], ACT.Copy).then_inc(sum_copied, 1)
                act.wait_ge(sum_copied, 2 * (n + 1))
                act.sem_inc(out_ready, 1)

            def step(t, tile, supertile):
                if values:
                    each(copy_sum, tile(-3))
                each(hidden, tile(1))
                if values:
                    each(split_weighted, tile(-1))
                each(squares, tile(3))
                if t == 2:
                    each(split_efT, supertile(2))

            def end():
                if values:
                    copy_sum(*LAST[1])
                    split_weighted(*LAST[3])
                    copy_sum(*LAST[2])
                    copy_sum(*LAST[3])

            for s in range(2):
                split_efT(0, s)
            act.wait_ge(cleared, 3)
            for t in range(3):
                squares(0, 0, t)
            hidden(0, 0, 0)
            rolled(act, nothing, step, end)

        @block.vector
        def _(dve):
            def split_efT(i, s):
                j = 2 * i + s
                dve.wait_ge(efT_hi_ready, j + 1)
                dve.tensor_tensor(efT_lo[s][:, :], pE[:, :], efT_hi[s][:, :], ALU.subtract).then_inc(efT_lo_ready, 1)

            def add_table(i, s, t):
                n = number(i, s, t)
                if t == 0:
                    dve.wait_ge(table_in[s], 64 * (i + 1))
                dve.wait_ge(first_done, n + 1)
                awaits(dve, turned, n - SUPER + 1)
                dve.tensor_tensor(first[t][:, :], pF[t % 2][:, :], table[s][:, t, :], ALU.add).then_inc(first_ready, 1)


            def invert(i, s, t):
                n = number(i, s, t)
                dve.wait_ge(root_ready, n + 1)
                awaits(dve, rstd_ready, n)
                dve.tensor_scalar(var[:, :], sumsq[t][:, :], EPS, None, ALU.add).then_inc(var_ready, 1)
                dve.reciprocal(inverse[:, :], root[t][:, :]).then_inc(inverse_ready, 1)

            def newton_product(i, s, t):
                n = number(i, s, t)
                dve.wait_ge(var_ready, n + 1)
                dve.wait_ge(inverse_ready, n + 1)
                dve.scalar_tensor_tensor(out=error[:, :], in0=inverse[:, :], scalar=var[:, 0:1], in1=inverse[:, :],
                                         op0=ALU.mult, op1=ALU.mult).then_inc(error_ready, 1)

            def newton_factor(i, s, t):
                dve.wait_ge(error_ready, number(i, s, t) + 1)
                dve.tensor_scalar(correction[:, :], error[:, :], -0.5, 1.5, ALU.mult, ALU.add).then_inc(correction_ready, 1)

            def correct(i, s, t):
                n = number(i, s, t)
                dve.wait_ge(correction_ready, n + 1)
                awaits(dve, normed, n - SUPER + 1)
                dve.tensor_tensor(rstd[t][:, :], inverse[:, :], correction[:, :], ALU.mult).then_inc(rstd_ready, 1)

            def normalise(i, s, t):
                n = number(i, s, t)
                dve.wait_ge(rstd_ready, n + 1)
                dve.wait_ge(squared, n + 1)
                dve.tensor_scalar(first[t][:, :], first[t][:, :], rstd[t][:, 0:1], None, ALU.mult).then_inc(normed, 1)

            def split_hidden(i, s, t):
                n = number(i, s, t)
                dve.wait_ge(hid_hi_ready, n + 1)
                awaits(dve, second_done, n - 1)
                dve.tensor_tensor(hid_lo[t % 2][:, :, :], hid[:, :, :], hid_hi[t % 2][:, :, :], ALU.subtract)\
                   .then_inc(hid_lo_ready, 1)

            def compare(i, s, t):
                j = 2 * i + s
                if t == 0:
                    awaits(dve, equal_ready, SUPER * j)
                    dve.tensor_copy(dcol[:, :], keep.dst_f[:, bass.ds(j * SUPER, SUPER)]).then_inc(dcol_ready, 1)
                    dve.wait_ge(dcol_ready, j + 1)
                    dve.wait_ge(drow_in[s], 16 * (i + 1))
                awaits(dve, sum_done, number(i, s, t) - 2 * SUPER + 1)
                dve.tensor_scalar(equal[s][:, t, :], drow[s][:, t, :], dcol[:, t:t + 1], None, ALU.is_equal).then_inc(equal_ready, 1)

            def write_destinations(i, s):
                j = 2 * i + s
                for t in range(SUPER):
                    awaits(dve, out_done[t], 16 * (j - 1))
                dve.tensor_copy(out[s][:, :, HEADS:HEADS + 1].rearrange("p t a -> p (t a)"),
                                keep.dst_f[:, bass.ds(j * SUPER, SUPER)]).then_inc(dst_written, 1)


            def multiply_query(i, s, t):
                n = number(i, s, t)
                dve.wait_ge(second_done, n + 1)
                awaits(dve, heads_added, n)
                if t == 0:
                    dve.wait_ge(side_in[s], 64 * (i + 1))
                dve.tensor_tensor(product[:, :], pL[t % 2][:, :], side[s][:, t, 0:D], ALU.mult).then_inc(second_used, 1)

            def add_heads(i, s, t):
                n = number(i, s, t)
                dve.wait_ge(second_used, n + 1)
                awaits(dve, logits_ready, n)
                dve.tensor_reduce(logit[:, :], product[:, :].rearrange("p (h d) -> p h d", h=HEADS), AX.X, ALU.add)\
                   .then_inc(heads_added, 1)

            def add_bias(i, s, t):
                n = number(i, s, t)
                dve.wait_ge(heads_added, n + 1)
                dve.wait_ge(dst_written, 2 * i + s + 1)
                dve.tensor_tensor(out[s][:, t, 0:HEADS], logit[:, :], side[s][:, t, D:Q_W], ALU.add).then_inc(logits_ready, 1)
                dve.wait_ge(logits_ready, n + 1)
                dve.sem_inc(out_ready, 1)


            def weigh(i, s, t):
                n = number(i, s, t)
                dve.wait_ge(second_done, n + 1)
                awaits(dve, weighted_lo_ready, n)
                if t == 0:
                    dve.wait_ge(side_in[s], 64 * (i + 1))
                heads = side[s][:, t, :].unsqueeze(2).to_broadcast([P, HEADS, HEAD])
                dve.tensor_tensor(weighted[:, 0:D].rearrange("p (h d) -> p h d", h=HEADS),
                                  pL[t % 2][:, :].rearrange("p (h d) -> p h d", h=HEADS), heads, ALU.mult)\
                   .then_inc(second_used, 1)
                dve.tensor_copy(weighted[:, D:SUM_W], side[s][:, t, :]).then_inc(weighted_ready, 1)

            def split_weighted(i, s, t):
                n = number(i, s, t)
                dve.wait_ge(weighted_hi_ready, n + 1)
                awaits(dve, sum_done, n - 1)
                dve.tensor_tensor(weighted_lo[t % 2][:, :], weighted[:, :], weighted_hi[t % 2][:, :], ALU.subtract)\
                   .then_inc(weighted_lo_ready, 1)

            def step(t, tile, supertile):
                each(invert, tile(2))
                each(weigh if values else multiply_query, tile(-1))
                each(newton_product, tile(2))
                if not values:
                    each(add_heads, tile(-1))
                each(newton_factor, tile(2))
                each(add_table, tile(3))
                each(correct, tile(2))
                if not values:
                    each(add_bias, tile(-1))
                each(normalise, tile(2))
                each(split_hidden, tile(1))
                if values:
                    each(split_weighted, tile(-1))
                if t == 3:
                    each(split_efT, supertile(2))
                if values:
                    each(compare, tile(SUPER))
                elif t == 2:
                    each(write_destinations, supertile(1))

            def end():
                if values:
                    weigh(*LAST[3])
                    split_weighted(*LAST[3])
                else:
                    for part in (multiply_query, add_heads, add_bias):
                        part(*LAST[3])

            dve.memset(eps[:, :], EPS).then_inc(cleared, 1)
            if not values:
                for s in range(2):
                    dve.memset(out[s][:, :, :], 0.0).then_inc(out_cleared, 1)
                dve.wait_ge(out_cleared, 2)
            for s in range(2):
                split_efT(0, s)
            for t in range(3):
                add_table(0, 0, t)
            for t in range(2):
                for part in (invert, newton_product, newton_factor, correct, normalise):
                    part(0, 0, t)
            split_hidden(0, 0, 0)
            if values:
                for t in range(SUPER):
                    compare(0, 0, t)
            else:
                write_destinations(0, 0)
            rolled(dve, nothing, step, end)

        @block.tensor
        def _(pe):
            def turn_ef(i, s):
                j = 2 * i + s
                pe.wait_ge(ef_in[s], 16 * (i + 1))
                awaits(pe, efT_lo_ready, j)
                for t in range(SUPER):
                    mm = pe.transpose(pE[:, t * P:(t + 1) * P], ef[s][:, t, :], keep.ident[:, :])
                mm.then_inc(ef_turned, 1)

            def first_layer(i, s, t):
                n = number(i, s, t)
                if t == 0:
                    pe.wait_ge(efT_lo_ready, 2 * i + s + 1)
                awaits(pe, first_ready, n - 1)
                edges = slice(t * P, (t + 1) * P)
                pe.matmul(pF[t % 2][:, :], efT_hi[s][:, edges], w1_hi[:, :], start=True, stop=False)
                pe.matmul(pF[t % 2][:, :], efT_hi[s][:, edges], w1_lo[:, :], start=False, stop=False)
                pe.matmul(pF[t % 2][:, :], efT_lo[s][:, edges], w1_hi[:, :], start=False, stop=True).then_inc(first_done, 1)

            def turn(i, s, t):
                n = number(i, s, t)
                pe.wait_ge(normed, n + 1)
                awaits(pe, hid_ready, n)
                for c in range(KC):
                    feats = slice(c * P, (c + 1) * P)
                    mm = pe.transpose(pH[:, feats], first[t][:, feats], keep.ident[:, :])
                mm.then_inc(turned, 1)

            def second_layer(i, s, t):
                n = number(i, s, t)
                pe.wait_ge(hid_lo_ready, n + 1)
                awaits(pe, second_used, n - 1)
                hi, lo, bank = hid_hi[t % 2], hid_lo[t % 2], pL[t % 2]
                for c in range(KC):
                    pe.matmul(bank[:, :], hi[:, c, :], w2_hi[:, c, :], start=(c == 0), stop=False)
                    pe.matmul(bank[:, :], hi[:, c, :], w2_lo[:, c, :], start=False, stop=False)
                    mm = pe.matmul(bank[:, :], lo[:, c, :], w2_hi[:, c, :], start=False, stop=(c == KC - 1))
                mm.then_inc(second_done, 1)

            def add_rows(i, s, t):
                n = number(i, s, t)
                pe.wait_ge(equal_ready, n + 1)
                pe.wait_ge(weighted_lo_ready, n + 1)
                awaits(pe, sum_copied, 2 * n)
                for cols, bank in ((slice(0, D), pS[:, :]), (slice(D, SUM_W), pD[:, 0:HEADS])):
                    pe.matmul(bank, equal[s][:, t, :], weighted_hi[t % 2][:, cols], start=True, stop=False)
                    mm = pe.matmul(bank, equal[s][:, t, :], weighted_lo[t % 2][:, cols], start=False, stop=True)
                mm.then_inc(sum_done, 1)

            def step(t, tile, supertile):
                each(first_layer, tile(3))
                each(turn, tile(1))
                second_layer(*tile(0))
                if values:
                    each(add_rows, tile(-2))
                if t == 1:
                    each(turn_ef, supertile(2))

            def end():
                if values:
                    add_rows(*LAST[2])
                    add_rows(*LAST[3])

            for s in range(2):
                turn_ef(0, s)
            for t in range(3):
                first_layer(0, 0, t)
            turn(0, 0, 0)
            rolled(pe, nothing, step, end)


def split_weights(nc, w, keep, net, w2_hi, w2_lo, w1_hi, w1_lo, g_col, be_col):
    with ExitStack() as ctx:
        m = Memory(nc, ctx, f"split_{net}")
        w2 = m.sb("w2", [P, KC, D])
        loaded = m.sem("loaded")
        own = m.sem("own")
        w2_hi_ready = m.sem("w2_hi_ready")
        block = ctx.enter_context(nc.Block())

        @block.sync
        def _(sp):
            sp.dma_start(w2[:, :, :], w[f"h{net}_W2"].rearrange("(r p) n -> p r n", p=P)).then_inc(loaded, 16)
            sp.dma_start(g_col[:, :], col(w[f"h{net}_g"]), allow_slow_non_contiguous=True).then_inc(loaded, 16)
            sp.dma_start(be_col[:, :], col(w[f"h{net}_be"]), allow_slow_non_contiguous=True).then_inc(loaded, 16)

        @block.scalar
        def _(act):
            act.wait_ge(loaded, 48)
            act.activation(w2_hi[:, :, :], w2[:, :, :], ACT.Copy).then_inc(w2_hi_ready, 1)

        @block.vector
        def _(dve):
            link = Chain(dve, own)
            link(dve.tensor_copy(w1_hi[:, :], keep.w1e[net][:, :]))
            link(dve.tensor_tensor(w1_lo[:, :], keep.w1e[net][:, :], w1_hi[:, :], ALU.subtract))
            dve.wait_ge(w2_hi_ready, 1)
            link(dve.tensor_tensor(w2_lo[:, :, :], w2[:, :, :], w2_hi[:, :, :], ALU.subtract))


def segment_softmax(nc, keep, dram):
    with ExitStack() as ctx:
        m = Memory(nc, ctx, "soft")
        place = m.sb("place", [P, SPAN, L_W])
        dest = m.sb("dest", [P, SPAN])
        apart = m.sb("apart", [P, SPAN])
        ahead = m.sb("ahead", [P, SPAN])
        lead = m.sb("lead", [P, SPAN])
        trail = m.sb("trail", [P, SPAN])
        fwd = m.sb("fwd", [P, HEADS, SPAN])
        best = m.sb("best", [P, HEADS, SPAN])
        expo = m.sb("expo", [P, SPAN, HEADS])
        ends = m.sb("ends", [P, 4, HEADS])
        endsT = m.sb("endsT", [HEADS, 4, P])
        whole = m.sb("whole", [HEADS, P])
        joined = m.sb("joined", [HEADS, P])
        joined_b = m.sb("joined_b", [HEADS, P])
        through = m.sb("through", [HEADS, P])
        carry = m.sb("carry", [HEADS, 2, P])
        scanned = m.sb("scanned", [HEADS, 2, P])
        carry_in = m.sb("carry_in", [P, 2, HEADS])
        pA = m.ps("pA")
        pB = m.ps("pB")
        loaded = m.sem("loaded")
        own = m.sem("own")
        ends_ready = m.sem("ends_ready")
        turned = m.sem("turned")
        carry_ready = m.sem("carry_ready")
        carried = m.sem("carried")
        less = m.sem("less")
        expo_ready = m.sem("expo_ready")
        stored = m.sem("stored")
        block = ctx.enter_context(nc.Block())

        @block.sync
        def _(sp):
            sp.dma_start(place[:, :, :], dram.logits.rearrange("(p j) f -> p j f", p=P)).then_inc(loaded, 16)
            sp.wait_ge(expo_ready, 1)
            sp.dma_start(dram.expo.rearrange("(p j) f -> p j f", p=P), expo[:, :, :]).then_inc(stored, 16)
            sp.wait_ge(stored, 16)

        @block.scalar
        def _(act):
            act.wait_ge(less, 1)
            act.activation(expo[:, :, :], expo[:, :, :], ACT.Exp, scale=HEAD ** -0.5).then_inc(expo_ready, 1)

        @block.vector
        def _(dve):
            link = Chain(dve, own)
            dve.wait_ge(loaded, 16)
            link(dve.tensor_copy(dest[:, :].unsqueeze(2), place[:, :, HEADS:HEADS + 1]))
            link(dve.memset(apart[:, :], NEG))
            link(dve.memset(ahead[:, :], NEG))
            link(dve.tensor_tensor(apart[:, 1:SPAN], dest[:, 1:SPAN], dest[:, 0:SPAN - 1], ALU.not_equal))
            link(dve.tensor_scalar(apart[:, 1:SPAN], apart[:, 1:SPAN], NEG, None, ALU.mult))
            link(dve.tensor_copy(ahead[:, 0:SPAN - 1], apart[:, 1:SPAN]))
            link(dve.tensor_scalar(lead[:, :], dest[:, :], dest[:, 0:1], NEG, ALU.not_equal, ALU.mult))
            link(dve.tensor_scalar(trail[:, :], dest[:, :], dest[:, SPAN - 1:SPAN], NEG, ALU.not_equal, ALU.mult))
            for h in range(HEADS):
                s = dve.tensor_tensor_scan(fwd[:, h, :], apart[:, :], place[:, :, h:h + 1].rearrange("p j a -> p (j a)"),
                                           NEG, ALU.add, ALU.max)
            link(s)
            for h in range(HEADS):
                s = dve.tensor_tensor_scan(best[:, h, ::-1], ahead[:, ::-1], fwd[:, h, ::-1], NEG, ALU.add, ALU.max)
            link(s)
            link(dve.tensor_copy(ends[:, 0, :].unsqueeze(2), best[:, :, 0:1]))
            link(dve.tensor_copy(ends[:, 1, :].unsqueeze(2), best[:, :, SPAN - 1:SPAN]))
            link(dve.tensor_copy(ends[:, 2, :], dest[:, 0:1].to_broadcast([P, HEADS])))
            dve.tensor_copy(ends[:, 3, :], dest[:, SPAN - 1:SPAN].to_broadcast([P, HEADS])).then_inc(ends_ready, 1)
            dve.wait_ge(turned, 1)
            link(dve.tensor_copy(endsT[:, :, :].rearrange("h k p -> h (k p)"), pA[0:HEADS, :]))
            first, last = endsT[:, 2, :], endsT[:, 3, :]
            link(dve.memset(joined[:, :], NEG))
            link(dve.memset(joined_b[:, :], NEG))
            link(dve.tensor_tensor(whole[:, :], first, last, ALU.not_equal))
            link(dve.tensor_scalar(whole[:, :], whole[:, :], NEG, None, ALU.mult))
            link(dve.tensor_tensor(joined[:, 1:P], first[:, 1:P], last[:, 0:P - 1], ALU.not_equal))
            link(dve.tensor_scalar(joined[:, 1:P], joined[:, 1:P], NEG, None, ALU.mult))
            link(dve.tensor_copy(joined_b[:, 0:P - 1], joined[:, 1:P]))
            link(dve.memset(carry[:, :, :], NEG))
            link(dve.tensor_tensor(through[:, :], whole[:, :], joined[:, :], ALU.min))
            link(dve.tensor_tensor_scan(scanned[:, 0, :], through[:, :], endsT[:, 1, :], NEG, ALU.add, ALU.max))
            link(dve.tensor_tensor(through[:, :], whole[:, :], joined_b[:, :], ALU.min))
            link(dve.tensor_tensor_scan(scanned[:, 1, ::-1], through[:, ::-1], endsT[:, 0, ::-1], NEG, ALU.add, ALU.max))
            link(dve.tensor_tensor(carry[:, 0, 1:P], scanned[:, 0, 0:P - 1], joined[:, 1:P], ALU.add))
            dve.tensor_tensor(carry[:, 1, 0:P - 1], scanned[:, 1, 1:P], joined_b[:, 0:P - 1], ALU.add).then_inc(carry_ready, 1)
            dve.wait_ge(carried, 1)
            link(dve.tensor_copy(carry_in[:, :, :].rearrange("p k h -> p (k h)"), pB[:, 0:2 * HEADS]))
            for k, mask in enumerate((lead, trail)):
                for h in range(HEADS):
                    s = dve.scalar_tensor_tensor(out=best[:, h, :], in0=mask[:, :], scalar=carry_in[:, k, h:h + 1],
                                                 in1=best[:, h, :], op0=ALU.add, op1=ALU.max)
                link(s)
            dve.tensor_tensor(expo[:, :, :], place[:, :, 0:HEADS], best[:, :, :].rearrange("p h j -> p j h"), ALU.subtract)\
               .then_inc(less, 1)

        @block.tensor
        def _(pe):
            pe.wait_ge(ends_ready, 1)
            for k in range(4):
                mm = pe.transpose(pA[0:HEADS, k * P:(k + 1) * P], ends[:, k, :], keep.ident[:, :])
            mm.then_inc(turned, 1)
            pe.wait_ge(carry_ready, 1)
            for k in range(2):
                mm = pe.transpose(pB[:, k * HEADS:(k + 1) * HEADS], carry[:, k, :], keep.ident[0:HEADS, 0:HEADS])
            mm.then_inc(carried, 1)


def node_output(nc, w, keep, dram):
    with ExitStack() as ctx:
        m = Memory(nc, ctx, "outp")
        R = NODE_ROWS
        T = NODE_TILES
        w1 = m.sb("w1", [P, 2 * KC, D])
        w2 = m.sb("w2", [P, KC, D])
        ws = m.sb("ws", [P, KC, EXPERTS])
        bs = m.sb("bs", [P, EXPERTS])
        b1 = m.sb("b1", [P, D])
        b2 = m.sb("b2", [P, D])
        b2v = m.sb("b2v", [P, D])
        g_col = m.sb("g_col", [P, KC])
        be_col = m.sb("be_col", [P, KC])
        eb2 = m.sb("eb2", [EXPERTS, D])
        order_i = m.sb("order_i", [P, EXPERTS], I32)
        order = m.sb("order", [P, EXPERTS])
        w_mean = m.sb("w_mean", [P, 2 * KC])
        b_mean = m.sb("b_mean", [P, 1])
        sums = [m.sb(f"sums{b}", [R, SUM_TABLES, SUM_W]) for b in range(2)]
        h = [m.sb(f"h{b}", [R, D]) for b in range(2)]
        some = m.sb("some", [R, HEADS])
        att = [m.sb(f"att{b}", [R, D]) for b in range(2)]
        bias_v = m.sb("bias_v", [R, D])
        attT = m.sb("attT", [P, KC, R])
        first = m.sb("first", [R, D])
        square = m.sb("square", [R, D])
        sumsq = m.sb("sumsq", [R, 1])
        var = m.sb("var", [R, 2])
        root = m.sb("root", [R, 2])
        rstd = m.sb("rstd", [R, 2])
        tmp = m.sb("tmp", [R, 2])
        normed = m.sb("normed", [R, D])
        normT = m.sb("normT", [P, KC, R])
        x1 = [m.sb(f"x1_{b}", [R, D]) for b in range(2)]
        stats = m.sb("stats", [R, 6])
        mv = m.sb("mv", [R, 2])
        z = m.sb("z", [R, D])
        scores = m.sb("scores", [R, EXPERTS])
        top = m.sb("top", [R, 1])
        neg_top = m.sb("neg_top", [R, 1])
        chosen = m.sb("chosen", [R, EXPERTS])
        expo = m.sb("expo", [R, EXPERTS])
        total = m.sb("total", [R, 1])
        coef = m.sb("coef", [R, EXPERTS])
        coefT = m.sb("coefT", [EXPERTS, R])
        pT = [m.ps(f"pT{b}") for b in range(2)]
        pF = [m.ps(f"pF{b}") for b in range(2)]
        pY = m.ps("pY")
        pR = m.ps("pR")
        pB = m.ps("pB")

        att_loaded = m.sem("att_weights_loaded")
        loaded = m.sem("loaded")
        ready = m.sem("weights_ready")
        order_ready = m.sem("order_ready")
        own = m.sem("own")
        sums_in = [m.sem(f"sums_in{b}") for b in range(2)]
        sums_used = m.sem("sums_used")
        h_in = [m.sem(f"h_in{b}") for b in range(2)]
        h_used = m.sem("h_used")
        att_ready = m.sem("att_ready")
        turn_done = m.sem("turn_done")
        turn_copied = m.sem("turn_copied")
        first_done = m.sem("first_done")
        first_ready = m.sem("first_ready")
        squared = m.sem("squared")
        var_ready = m.sem("var_ready")
        root_ready = m.sem("root_ready")
        normed_ready = m.sem("normed_ready")
        second_done = m.sem("second_done")
        second_taken = m.sem("second_taken")
        z_ready = m.sem("z_ready")
        routed = m.sem("routed")
        top_ready = m.sem("top_ready")
        expo_ready = m.sem("expo_ready")
        coef_ready = m.sem("coef_ready")
        coef_turned = m.sem("coef_turned")
        coefT_ready = m.sem("coefT_ready")
        bias_done = m.sem("bias_done")
        bias_taken = m.sem("bias_taken")

        turns = [("att", 0)]
        for n in range(T + 1):
            turns += [(what, k) for what, k in (("z", n - 1), ("norm", n), ("att", n + 1))
                      if 0 <= k < T and (what != "norm" or n < T)]
        turn_no = {what: k for k, what in enumerate(turns)}
        block = ctx.enter_context(nc.Block())

        @block.sync
        def _(sp):
            def load_sums(n):
                b = n % 2
                if n >= 2:
                    sp.wait_ge(sums_used, n - 1)
                rows = slice(n * R, (n + 1) * R)
                for t in range(SUM_TABLES):
                    sp.dma_start(sums[b][:, t, :], dram.sums[t][rows, :]).then_inc(sums_in[b], 16)
                if n >= 2:
                    sp.wait_ge(h_used, n - 1)
                sp.dma_start(h[b][:, :], dram.h[rows, :]).then_inc(h_in[b], 16)

            def load(to, of, sem=loaded):
                sp.dma_start(to, of, allow_slow_non_contiguous=True).then_inc(sem, 16)

            load(w1[:, :, :], w["no_W1"].rearrange("(r p) n -> p r n", p=P), att_loaded)
            load(b1[:, :], row_bc(w["no_b1"]), att_loaded)
            load(b2v[:, :], row_bc(w["hv_b2"]), att_loaded)
            load_sums(0)
            load_sums(1)
            load(w2[:, :, :], w["no_W2"].rearrange("(r p) n -> p r n", p=P))
            load(ws[:, :, :], w["Ws"].rearrange("(r p) n -> p r n", p=P))
            load(bs[:, :], row_bc(w["bs"]))
            load(b2[:, :], row_bc(w["no_b2"]))
            load(g_col[:, :], col(w["no_g"]))
            load(be_col[:, :], col(w["no_be"]))
            load(eb2[:, :], w["b2"])
            for n in range(2, T):
                load_sums(n)

        @block.gpsimd
        def _(pool):
            pool.iota(order_i[:, :], [[-1, EXPERTS]], base=EXPERTS, channel_multiplier=0).then_inc(order_ready, 1)

        @block.vector
        def _(dve):
            link = Chain(dve, own)
            dve.wait_ge(order_ready, 1)
            link(dve.tensor_copy(order[:, :], order_i[:, :]))
            dve.wait_ge(att_loaded, 48)
            link(dve.tensor_reduce(w_mean[:, :], w1[:, :, :], AX.X, ALU.add))
            link(dve.tensor_scalar(w_mean[:, :], w_mean[:, :], -1.0 / D, None, ALU.mult))
            for r in range(2 * KC):
                dve.tensor_scalar(w1[:, r, :], w1[:, r, :], w_mean[:, r:r + 1], None, ALU.add).then_inc(ready, 1)
            link(dve.tensor_reduce(b_mean[:, :], b1[:, :], AX.X, ALU.add))
            link(dve.tensor_scalar(b_mean[:, :], b_mean[:, :], -1.0 / D, None, ALU.mult))
            link(dve.tensor_scalar(b1[:, :], b1[:, :], b_mean[:, :], None, ALU.add))

            def attention(n):
                s, to = sums[n % 2], att[n % 2]
                dve.wait_ge(sums_in[n % 2], SUM_TABLES * 16 * (n // 2 + 1))
                for t in range(1, SUM_TABLES):
                    link(dve.tensor_tensor(s[:, 0, :], s[:, 0, :], s[:, t, :], ALU.add))
                den = s[:, 0, D:SUM_W]
                link(dve.tensor_scalar(some[:, :], den, 0.0, None, ALU.is_gt))
                link(dve.tensor_scalar(den, den, 1e-30, None, ALU.max))
                link(dve.reciprocal(den, den))
                if n >= 2:
                    dve.wait_ge(turn_done, turn_no["att", n - 2] + 1)
                link(dve.tensor_tensor(to[:, :].rearrange("p (h d) -> p h d", h=HEADS),
                                       s[:, 0, 0:D].rearrange("p (h d) -> p h d", h=HEADS),
                                       den.unsqueeze(2).to_broadcast([R, HEADS, HEAD]), ALU.mult))
                dve.sem_inc(sums_used, 1)
                link(dve.tensor_tensor(bias_v[:, :].rearrange("p (h d) -> p h d", h=HEADS),
                                       b2v[0:R, :].rearrange("p (h d) -> p h d", h=HEADS),
                                       some[:, :].unsqueeze(2).to_broadcast([R, HEADS, HEAD]), ALU.mult))
                dve.tensor_tensor(to[:, :], to[:, :], bias_v[:, :], ALU.add).then_inc(att_ready, 1)

            def normalise_first(n):
                dve.wait_ge(first_done, n + 1)
                dve.tensor_tensor(first[:, :], pF[n % 2][0:R, :], b1[0:R, :], ALU.add).then_inc(first_ready, 1)
                dve.wait_ge(squared, n + 1)
                dve.tensor_scalar(var[:, 0:1], sumsq[:, :], EPS, None, ALU.add).then_inc(var_ready, 1)
                dve.wait_ge(root_ready, 2 * n + 1)
                reciprocal_root(dve, link, var[:, 0:1], root[:, 0:1], rstd[:, 0:1], tmp[:, 0:1])
                if n:
                    dve.wait_ge(turn_done, turn_no["norm", n - 1] + 1)
                link(dve.tensor_scalar(normed[:, :], first[:, :], rstd[:, 0:1], None, ALU.mult))
                dve.sem_inc(normed_ready, 1)

            def residuals(n):
                to = x1[n % 2]
                dve.wait_ge(second_done, n + 1)
                link(dve.tensor_tensor(to[:, :], pY[0:R, :], b2[0:R, :], ALU.add))
                dve.sem_inc(second_taken, 1)
                dve.wait_ge(h_in[n % 2], 16 * (n // 2 + 1))
                link(dve.tensor_tensor(to[:, :], to[:, :], h[n % 2][:, :], ALU.add))
                dve.sem_inc(h_used, 1)
                link(dve.tensor_tensor(to[:, :], to[:, :], keep.x[:, n, :], ALU.add))
                link(dve.bn_stats(stats[:, :], to[:, :]))
                link(dve.bn_aggr(mv[:, :], stats[:, :]))
                dve.tensor_scalar(var[:, 1:2], mv[:, 1:2], EPS, None, ALU.add).then_inc(var_ready, 1)
                dve.wait_ge(root_ready, 2 * n + 2)
                reciprocal_root(dve, link, var[:, 1:2], root[:, 1:2], rstd[:, 1:2], tmp[:, 1:2])
                if n:
                    dve.wait_ge(turn_done, turn_no["z", n - 1] + 1)
                dve.tensor_scalar(z[:, :], to[:, :], mv[:, 0:1], rstd[:, 1:2], ALU.subtract, ALU.mult).then_inc(z_ready, 1)

            def route(n):
                dve.wait_ge(routed, n + 1)
                if n:
                    dve.wait_ge(coef_turned, n)
                link(dve.tensor_tensor(scores[:, :], pR[0:R, 0:EXPERTS], bs[0:R, :], ALU.add))
                link(dve.tensor_reduce(top[:, :], scores[:, :], AX.X, ALU.max))
                dve.tensor_scalar(neg_top[:, :], top[:, :], -1.0, None, ALU.mult).then_inc(top_ready, 1)
                link(dve.scalar_tensor_tensor(out=chosen[:, :], in0=scores[:, :], scalar=top[:, 0:1], in1=order[0:R, :],
                                              op0=ALU.is_equal, op1=ALU.mult))
                link(dve.tensor_reduce(top[:, :], chosen[:, :], AX.X, ALU.max))
                link(dve.tensor_scalar(chosen[:, :], chosen[:, :], top[:, 0:1], None, ALU.is_equal))
                dve.wait_ge(expo_ready, n + 1)
                link(dve.reciprocal(total[:, :], total[:, :]))
                link(dve.tensor_scalar(coef[:, :], chosen[:, :], total[:, 0:1], None, ALU.mult))
                dve.sem_inc(coef_ready, 1)
                link(dve.tensor_copy(keep.coef[:, :, n:n + 1], coef[:, :].unsqueeze(2)))

            def copy_coefT(n):
                dve.wait_ge(coef_turned, n + 1)
                if n:
                    dve.wait_ge(bias_done, n)
                dve.tensor_copy(coefT[:, :], pR[0:EXPERTS, 0:R]).then_inc(coefT_ready, 1)

            def add_bias(n):
                dve.wait_ge(bias_done, n + 1)
                dve.tensor_tensor(keep.x[:, n, :], x1[n % 2][:, :], pB[0:R, :], ALU.add).then_inc(bias_taken, 1)

            attention(0)
            attention(1)
            dve.wait_ge(loaded, 7 * 16)
            for n in range(T + 1):
                if n < T:
                    normalise_first(n)
                if n:
                    route(n - 1)
                if n + 2 < T:
                    attention(n + 2)
                if n:
                    copy_coefT(n - 1)
                if n < T:
                    residuals(n)
                if n:
                    add_bias(n - 1)

        @block.scalar
        def _(act):
            def tile_of(what, n):
                act.wait_ge(turn_done, turn_no[what, n] + 1)
                return pT[turn_no[what, n] % 2]

            def copy_att(n):
                bank = tile_of("att", n)
                if n:
                    act.wait_ge(first_done, n)
                act.activation(attT[:, :, :], bank[:, 0:KC * R].rearrange("p (c r) -> p c r", c=KC), ACT.Copy)\
                   .then_inc(turn_copied, 1)

            def copy_z(n):
                bank = tile_of("z", n)
                act.wait_ge(first_done, n + 1)
                act.activation(keep.hT[:, :, n * R:(n + 1) * R], bank[:, 0:KC * R].rearrange("p (c r) -> p c r", c=KC), ACT.Copy)\
                   .then_inc(turn_copied, 1)

            def copy_norm(n):
                bank = tile_of("norm", n)
                if n:
                    act.wait_ge(second_done, n)
                for c in range(KC):
                    x = act.activation(normT[:, c, :], bank[:, c * R:(c + 1) * R], ACT.Relu, bias=be_col[:, c:c + 1],
                                       scale=g_col[:, c:c + 1])
                x.then_inc(turn_copied, 1)

            def square_root(n, k):
                act.wait_ge(var_ready, 2 * n + k + 1)
                act.activation(root[:, k:k + 1], var[:, k:k + 1], ACT.Sqrt).then_inc(root_ready, 1)

            def squares(n):
                act.wait_ge(first_ready, n + 1)
                if n:
                    act.wait_ge(squared, n)
                act.activation(square[:, :], first[:, :], ACT.Square, scale=D ** -0.5, accum_out=sumsq[:, :])\
                   .then_inc(squared, 1)

            def exponentials(n):
                act.wait_ge(top_ready, n + 1)
                if n:
                    act.wait_ge(expo_ready, n)
                act.activation(expo[:, :], scores[:, :], ACT.Exp, bias=neg_top[:, 0:1], accum_out=total[:, :])\
                   .then_inc(expo_ready, 1)

            act.wait_ge(loaded, 7 * 16)
            copy_att(0)
            for n in range(T + 1):
                if n < T:
                    squares(n)
                    square_root(n, 0)
                if n:
                    copy_z(n - 1)
                if n < T:
                    copy_norm(n)
                if n:
                    exponentials(n - 1)
                if n + 1 < T:
                    copy_att(n + 1)
                if n < T:
                    square_root(n, 1)

        @block.tensor
        def _(pe):
            def turn(what, n, of, produced):
                pe.wait_ge(produced, n + 1)
                k = turn_no[what, n]
                if k >= 2:
                    pe.wait_ge(turn_copied, k - 1)
                for c in range(KC):
                    mm = pe.transpose(pT[k % 2][:, c * R:(c + 1) * R], of[:, c * P:(c + 1) * P], keep.ident[0:R, 0:R])
                mm.then_inc(turn_done, 1)

            def first_of_h(n):
                if n >= 2:
                    pe.wait_ge(first_ready, n - 1)
                for c in range(KC):
                    pe.matmul(pF[n % 2][0:R, :], keep.hT[:, c, n * R:(n + 1) * R], w1[:, KC + c, :], start=(c == 0), stop=False)

            def first_of_att(n):
                pe.wait_ge(turn_copied, turn_no["att", n] + 1)
                for c in range(KC):
                    mm = pe.matmul(pF[n % 2][0:R, :], attT[:, c, :], w1[:, c, :], start=False, stop=(c == KC - 1))
                mm.then_inc(first_done, 1)

            def second(n):
                pe.wait_ge(turn_copied, turn_no["norm", n] + 1)
                if n:
                    pe.wait_ge(second_taken, n)
                for c in range(KC):
                    mm = pe.matmul(pY[0:R, :], normT[:, c, :], w2[:, c, :], start=(c == 0), stop=(c == KC - 1))
                mm.then_inc(second_done, 1)

            def score(n):
                pe.wait_ge(turn_copied, turn_no["z", n] + 1)
                if n:
                    pe.wait_ge(coefT_ready, n)
                for c in range(KC):
                    mm = pe.matmul(pR[0:R, 0:EXPERTS], keep.hT[:, c, n * R:(n + 1) * R], ws[:, c, :],
                                   start=(c == 0), stop=(c == KC - 1))
                mm.then_inc(routed, 1)

            def turn_coef(n):
                pe.wait_ge(coef_ready, n + 1)
                pe.transpose(pR[0:EXPERTS, 0:R], coef[:, :], keep.ident[0:R, 0:R]).then_inc(coef_turned, 1)

            def second_bias(n):
                pe.wait_ge(coefT_ready, n + 1)
                if n:
                    pe.wait_ge(bias_taken, n)
                pe.matmul(pB[0:R, :], coefT[:, :], eb2[:, :], start=True, stop=True).then_inc(bias_done, 1)

            pe.wait_ge(ready, 2 * KC)
            pe.wait_ge(loaded, 7 * 16)
            turn("att", 0, att[0], att_ready)
            first_of_h(0)
            for n in range(T + 1):
                if n < T:
                    first_of_att(n)
                if n:
                    turn("z", n - 1, z, z_ready)
                if n + 1 < T:
                    first_of_h(n + 1)
                if n:
                    score(n - 1)
                if n < T:
                    turn("norm", n, normed, normed_ready)
                if n + 1 < T:
                    turn("att", n + 1, att[(n + 1) % 2], att_ready)
                if n:
                    turn_coef(n - 1)
                if n < T:
                    second(n)
                if n:
                    second_bias(n - 1)


def experts(nc, w, keep, out):
    with ExitStack() as ctx:
        m = Memory(nc, ctx, "ffn")
        R = NODE_ROWS
        GROUPS = [(0, 4), (4, 4), (8, 2)]
        w1 = [m.sb(f"w1_{s}", [P, KC, FF]) for s in range(2)]
        w2 = [m.sb(f"w2_{s}", [P, FC, D]) for s in range(2)]
        b1 = [m.sb(f"b1_{s}", [P, FC]) for s in range(2)]
        coef = [m.sb(f"coef{s}", [R, NODE_TILES]) for s in range(2)]
        hid = [m.sb(f"hid{b}", [P, FC, 4 * R]) for b in range(2)]
        pH = [m.ps(f"pH{b}") for b in range(2)]
        pY = [m.ps(f"pY{b}") for b in range(3)]
        w_in = [m.sem(f"w_in{s}") for s in range(2)]
        coef_ready = m.sem("coef_ready")
        hid_done = m.sem("hid_done")
        hid_ready = m.sem("hid_ready")
        out_done = m.sem("out_done")
        added = m.sem("added")
        stored = m.sem("stored")
        NG = len(GROUPS)
        block = ctx.enter_context(nc.Block())

        @block.sync
        def _(sp):
            with sp.Fori(0, EXPERTS // 2) as i:
                for s in range(2):
                    e = bass.ds(2 * i + s, 1)
                    sp.wait_ge(out_done, 2 * i * NODE_TILES)
                    sp.dma_start(w1[s][:, :, :], w["W1"][e, :, :].rearrange("a (r p) n -> p (a r) n", p=P)).then_inc(w_in[s], 16)
                    sp.dma_start(w2[s][:, :, :], w["W2"][e, :, :].rearrange("a (r p) n -> p (a r) n", p=P)).then_inc(w_in[s], 16)
                    sp.dma_start(b1[s][:, :], w["b1"][e, :].rearrange("a (c p) -> p (a c)", p=P),
                                 allow_slow_non_contiguous=True).then_inc(w_in[s], 16)
            sp.wait_ge(added, EXPERTS * NODE_TILES)
            sp.dma_start(out.rearrange("(t p) n -> p t n", p=R), keep.x[:, :, :]).then_inc(stored, 16)
            sp.wait_ge(stored, 16)

        @block.scalar
        def _(act):
            with act.Fori(0, EXPERTS // 2) as i:
                for s in range(2):
                    for g, (t0, n) in enumerate(GROUPS):
                        k = (2 * i + s) * NG + g
                        if g == 2:
                            act.wait_ge(out_done, (2 * i + s) * NODE_TILES + 4)
                        else:
                            act.wait_ge(out_done, (2 * i + s) * NODE_TILES)
                        for f in range(FC):
                            act.wait_ge(hid_done, k * FC + f + 1)
                            act.activation(hid[g % 2][:, f, 0:n * R], pH[f][:, 0:n * R], ACT.Gelu, bias=b1[s][:, f:f + 1])\
                               .then_inc(hid_ready, 1)

        @block.vector
        def _(dve):
            with dve.Fori(0, EXPERTS // 2) as i:
                for s in range(2):
                    e = 2 * i + s
                    dve.tensor_copy(coef[s][:, :].unsqueeze(1), keep.coef[:, bass.ds(e, 1), :]).then_inc(coef_ready, 1)
                    dve.wait_ge(coef_ready, e + 1)
                    dve.wait_ge(added, e * NODE_TILES)
                    for t in range(NODE_TILES):
                        dve.wait_ge(out_done, e * NODE_TILES + t + 1)
                        dve.scalar_tensor_tensor(out=keep.x[:, t, :], in0=pY[t % 3][0:R, :], scalar=coef[s][:, t:t + 1],
                                                 in1=keep.x[:, t, :], op0=ALU.mult, op1=ALU.add).then_inc(added, 1)

        @block.tensor
        def _(pe):
            with pe.Fori(0, EXPERTS // 2) as i:
                for s in range(2):
                    e = 2 * i + s
                    pe.wait_ge(w_in[s], 48 * (i + 1))

                    def hidden(g):
                        t0, n = GROUPS[g]
                        for f in range(FC):
                            pe.wait_ge(hid_ready, (e * NG + g) * FC)
                            for c in range(KC):
                                mm = pe.matmul(pH[f][:, 0:n * R], w1[s][:, c, f * P:(f + 1) * P],
                                               keep.hT[:, c, t0 * R:(t0 + n) * R], start=(c == 0), stop=(c == KC - 1))
                            mm.then_inc(hid_done, 1)

                    def output(g):
                        t0, n = GROUPS[g]
                        pe.wait_ge(hid_ready, (e * NG + g + 1) * FC)
                        for t in range(t0, t0 + n):
                            pe.wait_ge(added, e * NODE_TILES + max(t - 2, 0))
                            for f in range(FC):
                                mm = pe.matmul(pY[t % 3][0:R, :], hid[g % 2][:, f, (t - t0) * R:(t - t0 + 1) * R],
                                               w2[s][:, f, :], start=(f == 0), stop=(f == FC - 1))
                            mm.then_inc(out_done, 1)

                    for g in range(NG):
                        hidden(g)
                        output(g)


class Tables:

    def __init__(self, nc):
        def table(name, shape):
            return nc.dram_tensor(name, shape, F32, kind="Internal").ap()

        self.dst_rows = table("dst_rows", [EDGE_TILES, P])
        self.table = [table(f"first_layer_{x}", [NODES, D]) for x in "kv"]
        self.query = table("query", [NODES, Q_W])
        self.h = table("h", [NODES, D])
        self.logits = table("logits", [PLACES, L_W])
        self.expo = table("expo", [PLACES, HEADS])
        self.sums = [table(f"sums{t}", [SUM_ROWS, SUM_W]) for t in range(SUM_TABLES)]


class Keep:

    def __init__(self, m):
        self.ident = m.sb("ident", [P, P])
        self.x = m.sb("x", [NODE_ROWS, NODE_TILES, D])
        self.hT = m.sb("hT", [P, KC, NODES])
        self.coef = m.sb("coef", [NODE_ROWS, EXPERTS, NODE_TILES])
        self.src_i = m.sb("src_i", [P, EDGE_TILES], I32)
        self.dst_i = m.sb("dst_i", [P, EDGE_TILES], I32)
        self.dst_f = m.sb("dst_f", [P, EDGE_TILES])
        self.sum_i = m.sb("sum_i", [P, EDGE_TILES], I32)
        self.place_i = m.sb("place_i", [P, EDGE_TILES], I32)
        self.in_rank = m.sb("in_rank", [P, EDGE_TILES])
        self.w1e = {x: m.sb(f"w1e_{x}", [P, D]) for x in "kv"}
        self.x_loaded = m.sem("x_loaded")
        self.pool_passed = m.sem("pool_passed")
        self.dve_passed = m.sem("dve_passed")

    def for_nodes(self, m):
        self.w1 = {x: m.sb(f"w1_{x}", [P, 4 if x == "q" else 5, D]) for x in "kvq"}
        self.b1 = {x: m.sb(f"b1_{x}", [P, D]) for x in "kvq"}
        self.be_q = m.sb("be_q", [P, KC])
        self.g_col_q = m.sb("g_col_q", [P, KC])
        self.b2q = m.sb("b2q", [P, D])
        self.b2k = m.sb("b2k", [P, D])


def build(nc, w, out):
    dram = Tables(nc)
    with ExitStack() as ctx:
        keep = Keep(Memory(nc, ctx, "keep"))
        with ExitStack() as early:
            keep.for_nodes(Memory(nc, early, "early"))
            prepare_weights(nc, w, keep, dram)
            node_tables(nc, w, keep, dram)
        rank_edges(nc, keep)
        edge_phase(nc, w, keep, dram, values=False)
        segment_softmax(nc, keep, dram)
        edge_phase(nc, w, keep, dram, values=True)
        node_output(nc, w, keep, dram)
        experts(nc, w, keep, out)


_GNN = [f"{x}_{y}" for x in ("hk", "hv", "hq", "no") for y in ("W1", "b1", "g", "be", "W2", "b2")]
_FFN = ["Ws", "bs", "W1", "b1", "W2", "b2"]
_NAMES = {"x": "x", "src": "src", "dst": "dst", "edge_attr_128": "edge_attr_128",
          **{f"L0_gnn_{x}": x for x in _GNN}, **{f"L0_ffn_{x}": x for x in _FFN}}


def kernel(**inputs):
    import numpy as _np
    import concourse.bacc as _bacc
    from concourse import mybir as _mybir
    from concourse.bass_utils import run_bass_kernel_spmd as _run

    nc = _bacc.Bacc("TRN2", target_bir_lowering=False, num_devices=1)
    arrays, w = {}, {}
    for name, short in _NAMES.items():
        a = _np.ascontiguousarray(inputs[name])
        arrays[f"in_{name}"] = a
        w[short] = nc.dram_tensor(f"in_{name}", a.shape, _mybir.dt.from_np(a.dtype), kind="ExternalInput").ap()
    out = nc.dram_tensor("out_0", (NODES, D), _mybir.dt.float32, kind="ExternalOutput").ap()
    build(nc, w, out)
    r = _run(nc, [arrays], core_ids=[0])
    return r.results[0]["out_0"]
```

```python
from contextlib import ExitStack

import concourse.bass as bass
from concourse import mybir

ALU = mybir.AluOpType
ACT = mybir.ActivationFunctionType
AX = mybir.AxisListType
F32 = mybir.dt.float32
F32R = mybir.dt.float32r
BF16 = mybir.dt.bfloat16
I32 = mybir.dt.int32

P = 128
NODES, D = 1250, 512
KC = D // P
NODE_ROWS = 125
NODE_TILES = NODES // NODE_ROWS
EDGES, EF = 20000, 128
EDGE_ROWS = 125
PADS = P - EDGE_ROWS
EDGE_TILES = EDGES // EDGE_ROWS
SUPER = 4
SUPERS = EDGE_TILES // SUPER
PLACES = EDGE_TILES * P
SPAN = PLACES // P
HEADS = 16
HEAD = D // HEADS
HALF = EDGE_TILES // 2
EXPERTS, FF = 8, 256
FC = FF // P
EPS = 1e-5
NEG = -1.0e38

Q_W = D + HEADS
L_W = HEADS + 4
SUM_W = D + HEADS
SUM_ROWS = 11 * P
SUM_TABLES = 4

assert NODE_TILES * NODE_ROWS == NODES and EDGE_TILES * EDGE_ROWS == EDGES and SUPERS * SUPER == EDGE_TILES
assert SUM_ROWS >= NODES + P


class Chain:

    def __init__(self, eng, sem, base=0):
        self.eng, self.sem, self.base, self.n = eng, sem, base, 0

    def __call__(self, instruction):
        self.n += 1
        instruction.then_inc(self.sem, 1)
        self.eng.wait_ge(self.sem, self.base + self.n)


class Memory:

    def __init__(self, nc, ctx, prefix):
        self.nc, self.ctx, self.prefix, self.sems = nc, ctx, prefix, []
        ctx.callback(self.release)

    def release(self):
        if self.sems:
            self.nc.clear_and_free_semaphores(self.sems)
            self.nc.all_engine_barrier()

    def sb(self, name, shape, dtype=F32):
        return self.ctx.enter_context(self.nc.sbuf_tensor(f"{self.prefix}_{name}", shape, dtype))

    def ps(self, name, shape=(P, D)):
        return self.ctx.enter_context(self.nc.psum_tensor(f"{self.prefix}_{name}", list(shape), F32))

    def sem(self, name):
        self.sems.append(self.nc.alloc_semaphore(name=f"{self.prefix}_{name}"))
        return self.sems[-1]


def row_bc(vector):
    return vector.partition_broadcast(P)


def col(vector):
    return vector.rearrange("(c p) -> p c", p=P)


def reciprocal_root(dve, link, var, root, out, tmp):
    link(dve.reciprocal(out, root))
    link(dve.tensor_tensor(tmp, out, out, ALU.mult))
    link(dve.tensor_tensor(tmp, tmp, var, ALU.mult))
    link(dve.tensor_scalar(tmp, tmp, -0.5, 1.5, ALU.mult, ALU.add))
    link(dve.tensor_tensor(out, out, tmp, ALU.mult))


def wait_here(eng, passed):
    eng.sem_inc(passed, 1)


def prepare_weights(nc, w, keep, dram):
    with ExitStack() as ctx:
        m = Memory(nc, ctx, "prep")
        whole = {x: m.sb(f"w1_{x}", [P, 4 if x == "q" else 5, D]) for x in "kvq"}
        less_mean = {x: m.sb(f"less_mean_{x}", [P, KC + 2]) for x in "kvq"}
        rows_i = m.sb("rows_i", [HALF, 2, 2, EDGE_ROWS], I32)
        rows = m.sb("rows", [HALF, 2, 2, P])
        pad_i = m.sb("pad_i", [HALF, 2, P], I32)
        flag = m.sb("flag", [P, EDGE_TILES])
        fill = m.sb("fill", [P, EDGE_TILES])
        stats = m.sb("stats", [NODE_ROWS, NODE_TILES, 6])
        var = m.sb("var", [NODE_ROWS, NODE_TILES])
        root = m.sb("root", [NODE_ROWS, NODE_TILES])
        tmp = m.sb("tmp", [NODE_ROWS, NODE_TILES])
        pI = m.ps("pI")

        scratch = m.sb("scratch", [P, D])
        var_ready = m.sem("var_ready")
        root_ready = m.sem("root_ready")
        summed = m.sem("summed")
        mean_ready = m.sem("mean_ready")
        centred = m.sem("centred")
        loaded = {x: m.sem(f"loaded_{x}") for x in "kvq"}
        small = m.sem("small_loaded")
        idx_loaded = m.sem("idx_loaded")
        consts = m.sem("consts")
        pool_own = m.sem("pool_own")
        dve_own = m.sem("dve_own")
        rows_ready = m.sem("rows_ready")
        rows_turned = m.sem("rows_turned")
        stored = m.sem("stored")
        nets = "qkv"

        block = ctx.enter_context(nc.Block())

        @block.sync
        def _(sp):
            sp.dma_start(keep.x[:, :, :], w["x"].rearrange("(t p) n -> p t n", p=NODE_ROWS)).then_inc(keep.x_loaded, 16)
            for x in nets:
                sp.dma_start(whole[x][:, :, :], w[f"h{x}_W1"].rearrange("(r p) n -> p r n", p=P)).then_inc(loaded[x], 16)
            sp.wait_ge(rows_ready, 2)
            for half in range(2):
                sp.dma_start(dram.dst_rows[half * HALF:(half + 1) * HALF, :], rows[:, half, 1, :]).then_inc(stored, 16)
            sp.wait_ge(stored, 32)

        @block.scalar
        def _(act):
            for half in range(2):
                for i, name in enumerate(("src", "dst")):
                    act.dma_start(rows_i[:, half, i, :],
                                  w[name].rearrange("(h t p) -> h t p", h=2, p=EDGE_ROWS)[half]).then_inc(idx_loaded, 16)
            for x in nets:
                act.dma_start(keep.b1[x][:, :], row_bc(w[f"h{x}_b1"])).then_inc(small, 16)
            act.dma_start(keep.be_q[:, :], col(w["hq_be"]), allow_slow_non_contiguous=True).then_inc(small, 16)
            act.dma_start(keep.g_col_q[:, :], col(w["hq_g"]), allow_slow_non_contiguous=True).then_inc(small, 16)
            act.dma_start(keep.b2q[:, :], row_bc(w["hq_b2"])).then_inc(small, 16)
            act.dma_start(keep.b2k[:, :], row_bc(w["hk_b2"])).then_inc(small, 16)
            act.wait_ge(small, 7 * 16)
            for n, x in enumerate("kv"):
                act.wait_ge(loaded[x], 16)
                rows_of = [whole[x][:, r, :] for r in range(KC + 1)] + [keep.b1[x][:, :]]
                for r, row in enumerate(rows_of):
                    if n or r:
                        act.wait_ge(summed, n * len(rows_of) + r)
                    act.activation(scratch[:, :], row, ACT.Copy, accum_out=less_mean[x][:, r:r + 1]).then_inc(summed, 1)
                act.wait_ge(summed, (n + 1) * len(rows_of))
                act.activation(less_mean[x][:, :], less_mean[x][:, :], ACT.Copy, scale=-1.0 / D).then_inc(mean_ready, 1)
                if n == 0:
                    act.wait_ge(var_ready, 1)
                    act.activation(root[:, :], var[:, :], ACT.Sqrt).then_inc(root_ready, 1)
            act.wait_ge(mean_ready, 2)
            centre = [(whole["v"][:, r, :], keep.w1_hi["v"][:, r, :], "v", r) for r in range(KC)]
            for x in "vk":
                centre += [(whole[x][:, KC, :], keep.w1e[x][:, :], x, KC), (keep.b1[x][:, :], keep.b1[x][:, :], x, KC + 1)]
            for row, to, x, r in centre:
                act.activation(to, row, ACT.Identity, bias=less_mean[x][:, r:r + 1]).then_inc(centred, 1)

        @block.gpsimd
        def _(pool):
            pool.memset(keep.ident[:, :], 0.0).then_inc(pool_own, 1)
            pool.wait_ge(pool_own, 1)
            pool.affine_select(out=keep.ident[:, :], in_=keep.ident[:, :], compare_op=ALU.not_equal, fill=1.0,
                               base=0, pattern=[[-1, P]], channel_multiplier=1).then_inc(consts, 1)
            for half in range(2):
                pool.iota(pad_i[:, half, :], [[1, P]], base=NODES - EDGE_ROWS + PADS * HALF * half,
                          channel_multiplier=PADS).then_inc(consts, 1)
            pool.iota(keep.place_i[:, :], [[PADS, EDGE_TILES]], base=EDGES - EDGE_ROWS, channel_multiplier=1).then_inc(consts, 1)

        @block.vector
        def _(dve):
            link = Chain(dve, dve_own)

            def centre_first(net):
                for c in range(KC):
                    x = dve.tensor_scalar(keep.w1_hi[net][:, c, :], whole[net][:, c, :], less_mean[net][:, c:c + 1], None, ALU.add)
                link(x)

            def split_rest(net):
                for c in range(KC):
                    dve.scalar_tensor_tensor(out=keep.w1_lo[net][:, c, :], in0=whole[net][:, c, :],
                                             scalar=less_mean[net][:, c:c + 1], in1=keep.w1_hi[net][:, c, :].bitcast(F32),
                                             op0=ALU.add, op1=ALU.subtract)

            dve.wait_ge(consts, 4)
            dve.wait_ge(idx_loaded, 64)
            link(dve.memset(rows[:, :, 0, :], 0.0))
            link(dve.tensor_copy(rows[:, :, 1, :], pad_i[:, :, :]))
            for i in range(2):
                dve.tensor_copy(rows[:, :, i, 0:EDGE_ROWS], rows_i[:, :, i, :]).then_inc(rows_ready, 1)
            dve.wait_ge(keep.x_loaded, 16)
            for n in range(NODE_TILES):
                x = dve.bn_stats(stats[:, n, :], keep.x[:, n, :])
            link(x)
            for n in range(NODE_TILES):
                x = dve.bn_aggr(keep.x_mv[:, n, :], stats[:, n, :])
            link(x)
            dve.tensor_scalar(var[:, :], keep.x_mv[:, :, 1], EPS, None, ALU.add).then_inc(var_ready, 1)
            dve.wait_ge(small, 7 * 16)
            dve.wait_ge(loaded["q"], 16)
            mean = less_mean["q"]
            link(dve.tensor_reduce(mean[:, 0:KC], whole["q"][:, :, :], AX.X, ALU.add))
            link(dve.tensor_reduce(mean[:, KC:KC + 1], keep.b1["q"][:, :], AX.X, ALU.add))
            link(dve.tensor_scalar(mean[:, 0:KC + 1], mean[:, 0:KC + 1], -1.0 / D, None, ALU.mult))
            centre_first("q")
            link(dve.tensor_scalar(keep.b1["q"][:, :], keep.b1["q"][:, :], mean[:, KC:KC + 1], None, ALU.add))
            split_rest("q")
            dve.wait_ge(root_ready, 1)
            reciprocal_root(dve, link, var[:, :], root[:, :], keep.x_rstd[:, :], tmp[:, :])
            dve.wait_ge(mean_ready, 1)
            centre_first("k")
            split_rest("k")
            dve.wait_ge(centred, KC)
            split_rest("v")
            dve.wait_ge(rows_turned, 1)
            turned_rows = pI[:, 0:4 * HALF].rearrange("p (i h t) -> p i h t", i=2, h=2)
            link(dve.tensor_copy(keep.src_i[:, :].rearrange("p (h t) -> p h t", h=2), turned_rows[:, 0, :, :]))
            link(dve.tensor_copy(keep.dst_f[:, :].rearrange("p (h t) -> p h t", h=2), turned_rows[:, 1, :, :]))
            link(dve.tensor_scalar(flag[:, :], keep.dst_f[:, :], float(NODES), None, ALU.is_lt))
            link(dve.tensor_tensor(fill[:, :], flag[:, :], keep.dst_f[:, :], ALU.mult))
            link(dve.tensor_copy(keep.dst_i[:, :], fill[:, :]))

        @block.tensor
        def _(pe):
            pe.wait_ge(consts, 4)
            pe.wait_ge(rows_ready, 2)
            for i in range(2):
                for half in range(2):
                    k = 2 * i + half
                    mm = pe.transpose(pI[:, k * HALF:(k + 1) * HALF], rows[:, half, i, :], keep.ident[0:HALF, 0:HALF])
            mm.then_inc(rows_turned, 1)


class Ranks:
    LOW = 32
    HIGH = -(-NODES // LOW)
    BANK = D // LOW
    GROUPS = EDGE_TILES // BANK
    TURN = 4
    TURNS = BANK // TURN
    LOAD = 4
    LOADS = 3
    ONE_HOTS = [(0, 1, 2), (3, 4, 5), (6, 7, 8), (9,), (), (), (), (), (), ()]
    COUNTS = [(), (0, 1, 2), (3, 4, 5), (6, 7, 8), (9,), (), (), (), (), ()]
    SCAN, BASE = 4, 5
    NONE = ((), (), ())
    LOOKUPS = [NONE] * 6 + [((0,), (1,), ()), ((2,), (3,), (4,)), ((5,), (6,), ()), ((7,), (8,), (9,))]
    IN_TILE = [NONE] * 6 + [((0,), (1,), ()), ((2,), (3,), (4,)), ((5,), (6,), ()), ((7,), (8,), (9,))]

    def __init__(self, m, keep, dram):
        HIGH, LOW = self.HIGH, self.LOW
        self.keep, self.dram = keep, dram
        self.count_i = m.sb("count_i", [P, HIGH + 1], I32)
        self.bound = m.sb("bound", [P, HIGH + 1])
        self.low_no = m.sb("low_no", [P, LOW])
        self.before = m.sb("before", [HIGH, HIGH])
        self.earlier = m.sb("earlier", [P, P])
        self.ident_b = m.sb("ident_b", [P, P], BF16)
        self.reached = m.sb("reached", [P, self.BANK, HIGH + 1])
        self.rest = m.sb("rest", [P, self.BANK])
        self.low_part = m.sb("low_part", [P, self.BANK])
        self.high = m.sb("high", [P, EDGE_TILES, HIGH], BF16)
        self.low = m.sb("low", [P, EDGE_TILES, LOW], BF16)
        self.counts = m.sb("counts", [HIGH, LOW, EDGE_TILES], BF16)
        self.base = m.sb("base", [HIGH, LOW * EDGE_TILES + 1])
        self.total = m.sb("total", [HIGH, 1])
        self.start = m.sb("start", [HIGH, 1])
        self.turned = [m.sb(f"turned{b}", [HIGH, self.TURN, EDGE_ROWS]) for b in range(2)]
        self.picked = m.sb("picked", [P, self.BANK, LOW])
        self.found = m.sb("found", [P, EDGE_TILES])
        self.drow = [m.sb(f"drow{b}", [P, self.LOAD, P]) for b in range(self.LOADS)]
        self.same = m.sb("same", [P, self.LOAD, P])
        self.fill_i = m.sb("fill_i", [P, EDGE_TILES], I32)
        self.fill = m.sb("fill", [P, EDGE_TILES])
        self.leader = m.sb("leader", [P, EDGE_TILES])
        self.pB = [m.ps(f"bank{b}") for b in range(2)]
        self.pL = m.ps("looked")
        self.own = m.sem("ranks_own")
        self.consts = m.sem("ranks_consts")
        self.pool_own = m.sem("ranks_pool_own")
        self.one_hots_ready = m.sem("one_hots_ready")
        self.counted = m.sem("counted")
        self.counts_ready = m.sem("counts_ready")
        self.total_ready = m.sem("total_ready")
        self.start_done = m.sem("start_done")
        self.base_ready = m.sem("base_ready")
        self.turn_done = m.sem("turn_done")
        self.turn_ready = m.sem("turn_ready")
        self.looked = m.sem("looked")
        self.read = m.sem("read")
        self.compared = m.sem("compared")
        self.drow_in = [m.sem(f"drow_in{b}") for b in range(self.LOADS)]


    def pool_work(self, pool):
        HIGH, LOAD = self.HIGH, self.LOAD
        pool.iota(self.count_i[:, :], [[1, HIGH + 1]], base=0, channel_multiplier=0).then_inc(self.consts, 1)
        pool.iota(self.fill_i[:, :], [[0, EDGE_TILES]], base=NODES, channel_multiplier=1).then_inc(self.consts, 1)
        pool.memset(self.before[:, :], 1.0).then_inc(self.pool_own, 1)
        pool.memset(self.earlier[:, :], 1.0).then_inc(self.pool_own, 1)
        pool.wait_ge(self.pool_own, 2)
        pool.affine_select(out=self.before[:, :], in_=self.before[:, :], compare_op=ALU.is_gt, fill=0.0,
                           base=0, pattern=[[1, HIGH]], channel_multiplier=-1).then_inc(self.consts, 1)
        pool.affine_select(out=self.earlier[:, :], in_=self.earlier[:, :], compare_op=ALU.is_gt, fill=0.0,
                           base=0, pattern=[[-1, P]], channel_multiplier=1).then_inc(self.consts, 1)
        for k in range(EDGE_TILES // LOAD):
            b = k % self.LOADS
            if k >= self.LOADS:
                pool.wait_ge(self.compared, k - self.LOADS + 1)
            src = self.dram.dst_rows[LOAD * k:LOAD * (k + 1), :].rearrange("t p -> (t p)").partition_broadcast(P)
            pool.dma_start(self.drow[b][:, :, :].rearrange("p t e -> p (t e)"), src).then_inc(self.drow_in[b], 16)


    def prepare(self, dve):
        self.link = Chain(dve, self.own)
        link = self.link
        dve.wait_ge(self.consts, 4)
        link(dve.tensor_copy(self.low_no[:, :], self.count_i[:, 0:self.LOW]))
        link(dve.tensor_copy(self.bound[:, :], self.count_i[:, :]))
        link(dve.tensor_scalar(self.bound[:, :], self.bound[:, :], float(self.LOW), None, ALU.mult))
        link(dve.tensor_copy(self.ident_b[:, :], self.keep.ident[:, :]))
        link(dve.tensor_copy(self.fill[:, :], self.fill_i[:, :]))

    def group(self, g):
        return slice(g * self.BANK, (g + 1) * self.BANK)

    def one_hots(self, dve, g):
        link, tiles, HIGH, LOW = self.link, self.group(g), self.HIGH, self.LOW
        dst = self.keep.dst_f[:, tiles]
        link(dve.tensor_tensor(self.reached[:, :, :], dst.unsqueeze(2).to_broadcast([P, self.BANK, HIGH + 1]),
                               self.bound[:, :].unsqueeze(1).to_broadcast([P, self.BANK, HIGH + 1]), ALU.is_ge))
        dve.tensor_tensor(self.high[:, tiles, :], self.reached[:, :, 0:HIGH], self.reached[:, :, 1:HIGH + 1], ALU.subtract)\
           .then_inc(self.one_hots_ready, 1)
        link(dve.tensor_reduce(self.rest[:, :], self.reached[:, :, 1:HIGH + 1], AX.X, ALU.add))
        link(dve.scalar_tensor_tensor(out=self.low_part[:, :], in0=self.rest[:, :], scalar=-float(LOW), in1=dst,
                                      op0=ALU.mult, op1=ALU.add))
        dve.tensor_tensor(self.low[:, tiles, :], self.low_part[:, :].unsqueeze(2).to_broadcast([P, self.BANK, LOW]),
                          self.low_no[:, :].unsqueeze(1).to_broadcast([P, self.BANK, LOW]), ALU.is_equal)\
           .then_inc(self.one_hots_ready, 1)
        dve.wait_ge(self.one_hots_ready, 2 * (g + 1))

    def scan(self, dve):
        link = self.link
        dve.wait_ge(self.counts_ready, self.GROUPS)
        flat = self.counts[:, :, :].rearrange("h l t -> h (l t)")
        link(dve.memset(self.base[:, 0:1], 0.0))
        link(dve.tensor_tensor_scan(self.base[:, 1:], flat, flat, 0.0, ALU.add, ALU.max))
        dve.tensor_copy(self.total[:, :], self.base[:, self.LOW * EDGE_TILES:]).then_inc(self.total_ready, 1)

    def add_start(self, dve):
        link = self.link
        dve.wait_ge(self.start_done, 1)
        dve.wait_ge(self.total_ready, 1)
        link(dve.tensor_copy(self.start[:, :], self.pL[0:self.HIGH, 0:1]))
        dve.tensor_scalar(self.base[:, :], self.base[:, :], self.start[:, 0:1], None, ALU.add).then_inc(self.base_ready, 1)

    def pick(self, dve, g):
        link, tiles, R = self.link, self.group(g), EDGE_ROWS
        dve.wait_ge(self.looked, self.BANK * (g + 1))
        link(dve.tensor_tensor(self.picked[0:R, :, :], self.pL[0:R, :].rearrange("p (t l) -> p t l", l=self.LOW),
                               self.low[0:R, tiles, :], ALU.mult))
        dve.sem_inc(self.read, 1)
        link(dve.tensor_reduce(self.found[0:R, tiles], self.picked[0:R, :, :], AX.X, ALU.add))

    def in_tile(self, dve, g):
        LOAD = self.LOAD
        for k in range(g * self.BANK // LOAD, (g + 1) * self.BANK // LOAD):
            b = k % self.LOADS
            dve.wait_ge(self.drow_in[b], 16 * (k // self.LOADS + 1))
            if k:
                dve.wait_ge(self.compared, k)
            for t in range(LOAD):
                tile = slice(LOAD * k + t, LOAD * k + t + 1)
                x = dve.scalar_tensor_tensor(out=self.same[:, t, :], in0=self.drow[b][:, t, :], scalar=self.keep.dst_f[:, tile],
                                             in1=self.earlier[:, :], op0=ALU.is_equal, op1=ALU.mult,
                                             accum_out=self.keep.in_rank[:, tile])
            x.then_inc(self.compared, 1)

    def finish(self, dve):
        link, R = self.link, EDGE_ROWS
        in_rank, fill, leader = self.keep.in_rank, self.fill, self.leader
        dve.wait_ge(self.compared, EDGE_TILES // self.LOAD)
        link(dve.tensor_tensor(self.found[0:R, :], self.found[0:R, :], in_rank[0:R, :], ALU.add))
        link(dve.tensor_copy(self.keep.place_i[0:R, :], self.found[0:R, :]))
        link(dve.tensor_scalar(leader[:, :], in_rank[:, :], 0.0, None, ALU.is_equal))
        link(dve.tensor_scalar(self.found[:, :], self.keep.dst_f[:, :], float(NODES), None, ALU.is_lt))
        link(dve.tensor_tensor(leader[:, :], leader[:, :], self.found[:, :], ALU.mult))
        link(dve.tensor_tensor(self.found[:, :], self.keep.dst_f[:, :], fill[:, :], ALU.subtract))
        link(dve.tensor_tensor(self.found[:, :], self.found[:, :], leader[:, :], ALU.mult))
        link(dve.tensor_tensor(self.found[:, :], self.found[:, :], fill[:, :], ALU.add))
        link(dve.tensor_copy(self.keep.sum_i[:, :], self.found[:, :]))


    def copy_counts(self, act, g):
        act.wait_ge(self.counted, g + 1)
        act.activation(self.counts[:, :, self.group(g)].rearrange("h l t -> h t l"),
                       self.pB[g % 2][0:self.HIGH, :].rearrange("h (t l) -> h t l", l=self.LOW), ACT.Copy).then_inc(self.counts_ready, 1)

    def copy_turned(self, act, k):
        act.wait_ge(self.turn_done, k + 1)
        if k >= 2:
            act.wait_ge(self.looked, self.TURN * (k - 1))
        act.activation(self.turned[k % 2][:, :, :].rearrange("h t e -> h (t e)"),
                       self.pB[k % 2][0:self.HIGH, 0:self.TURN * EDGE_ROWS], ACT.Copy).then_inc(self.turn_ready, 1)


    def count(self, pe, g):
        pe.wait_ge(self.one_hots_ready, 2 * (g + 1))
        if g >= 2:
            pe.wait_ge(self.counts_ready, g - 1)
        for k in range(self.BANK):
            t = g * self.BANK + k
            mm = pe.matmul(self.pB[g % 2][0:self.HIGH, k * self.LOW:(k + 1) * self.LOW], self.high[0:EDGE_ROWS, t, :],
                           self.low[0:EDGE_ROWS, t, :], start=True, stop=True)
        mm.then_inc(self.counted, 1)

    def add_totals(self, pe):
        pe.wait_ge(self.total_ready, 1)
        pe.matmul(self.pL[0:self.HIGH, 0:1], self.before[:, :], self.total[:, :], start=True, stop=True).then_inc(self.start_done, 1)

    def turn(self, pe, k):
        if k >= 2:
            pe.wait_ge(self.turn_ready, k - 1)
        else:
            pe.wait_ge(self.counts_ready, self.GROUPS)
        for t in range(self.TURN):
            mm = pe.matmul(self.pB[k % 2][0:self.HIGH, t * EDGE_ROWS:(t + 1) * EDGE_ROWS],
                           self.high[0:EDGE_ROWS, k * self.TURN + t, :], self.ident_b[0:EDGE_ROWS, 0:EDGE_ROWS], start=True, stop=True)
        mm.then_inc(self.turn_done, 1)

    def look_up(self, pe, g):
        pe.wait_ge(self.base_ready, 1)
        if g:
            pe.wait_ge(self.read, g)
        base = self.base[:, 0:self.LOW * EDGE_TILES].rearrange("h (l t) -> h l t", t=EDGE_TILES)
        first = g * self.TURNS
        if g == 0:
            self.turn(pe, 0)
        for k in range(first, first + self.TURNS):
            if k + 1 < self.GROUPS * self.TURNS:
                self.turn(pe, k + 1)
            pe.wait_ge(self.turn_ready, k + 1)
            for t in range(self.TURN):
                at = (k - first) * self.TURN + t
                pe.matmul(self.pL[0:EDGE_ROWS, at * self.LOW:(at + 1) * self.LOW], self.turned[k % 2][:, t, :],
                          base[:, :, k * self.TURN + t], start=True, stop=True).then_inc(self.looked, 1)


def node_tables(nc, w, keep, dram):
    with ExitStack() as ctx:
        m = Memory(nc, ctx, "node")
        R = NODE_ROWS
        T = NODE_TILES
        w2q = m.sb("w2q", [P, KC, D])
        mv, rstd = keep.x_mv, keep.x_rstd
        var_q = m.sb("var_q", [R, 1])
        root_q = m.sb("root_q", [R, 1])
        rstd_q = m.sb("rstd_q", [R, 1])
        tmp_q = m.sb("tmp_q", [R, 1])
        h = [m.sb(f"h{b}", [R, D]) for b in range(2)]
        hT_hi = m.sb("hT_hi", [P, KC, R], F32R)
        hT_lo = m.sb("hT_lo", [P, KC, R], F32R)
        hT = [m.sb(f"hT{b}", [P, KC, R]) for b in range(2)]
        first = m.sb("first", [R, D])
        square = m.sb("square", [R, D])
        sumsq = m.sb("sumsq", [R, 1])
        row = [m.sb(f"row{b}", [R, 2, D]) for b in range(2)]
        q_norm = m.sb("q_norm", [R, D])
        qT = m.sb("qT", [P, KC, R])
        q_row = [m.sb(f"q_row{b}", [R, Q_W]) for b in range(2)]
        q_bias = m.sb("q_bias", [R, D])
        pT = m.ps("pT")
        pF = {net: m.ps(f"pF_{net}") for net in "kvq"}
        pQ = m.ps("pQ")
        ranks = Ranks(m, keep, dram)
        zero = m.sb("zero", [P, SUM_W // 2])
        zero_ready = m.sem("zero_ready")
        zeroed = m.sem("zeroed")
        w2_loaded = m.sem("w2_loaded")
        own = m.sem("dve_own")
        h_ready = m.sem("h_ready")
        h_stored = [m.sem(f"h_stored{b}") for b in range(2)]
        h_turned = m.sem("h_turned")
        hT_hi_ready = m.sem("hT_hi_ready")
        hT_lo_ready = m.sem("hT_lo_ready")
        hT_ready = m.sem("hT_ready")
        hT_stored = [m.sem(f"hT_stored{b}") for b in range(2)]
        done = {net: m.sem(f"first_done_{net}") for net in "kvq"}
        taken = {net: m.sem(f"first_taken_{net}") for net in "kvq"}
        squared = m.sem("squared")
        normed = m.sem("normed")
        var_q_ready = m.sem("var_q_ready")
        root_q_ready = m.sem("root_q_ready")
        rows_stored = [m.sem(f"rows_stored{b}") for b in range(2)]
        q_turned = m.sem("q_turned")
        qT_ready = m.sem("qT_ready")
        q_done = m.sem("q_done")
        q_taken = m.sem("q_taken")
        q_ready = m.sem("q_ready")
        q_stored = [m.sem(f"q_stored{b}") for b in range(2)]

        block = ctx.enter_context(nc.Block())

        @block.sync
        def _(sp):
            sp.dma_start(w2q[:, :, :], w["hq_W2"].rearrange("(r p) n -> p r n", p=P)).then_inc(w2_loaded, 16)

            def store_query(n):
                sp.wait_ge(q_ready, n + 1)
                sp.dma_start(dram.query[n * R:(n + 1) * R, :], q_row[n % 2][:, :]).then_inc(q_stored[n % 2], 16)

            sp.wait_ge(zero_ready, 1)
            for n in range(T):
                rows = slice(n * R, (n + 1) * R)
                sp.wait_ge(h_ready, n + 1)
                sp.dma_start(dram.h[rows, :], h[n % 2][:, :]).then_inc(h_stored[n % 2], 16)
                sp.wait_ge(hT_ready, n + 1)
                sp.dma_start(dram.hT[n], hT[n % 2][:, :, :].rearrange("p c r -> p (c r)")).then_inc(hT_stored[n % 2], 16)
                if n:
                    store_query(n - 1)
                for k, net in enumerate("kv"):
                    sp.wait_ge(taken[net], n + 1)
                    sp.dma_start(dram.table[k][rows, :], row[n % 2][:, k, :]).then_inc(rows_stored[n % 2], 16)
                if n < SUM_TABLES:
                    sp.dma_start(dram.sums[n].rearrange("(p r) (k f) -> p (r k) f", r=SUM_ROWS // P, k=2),
                                 zero[:, :].unsqueeze(1).to_broadcast([P, SUM_ROWS // P * 2, SUM_W // 2])).then_inc(zeroed, 16)
            store_query(T - 1)
            sp.wait_ge(zeroed, SUM_TABLES * 16)
            for b in range(2):
                sp.wait_ge(h_stored[b], T // 2 * 16)
                sp.wait_ge(hT_stored[b], T // 2 * 16)
                sp.wait_ge(rows_stored[b], T // 2 * 32)
                sp.wait_ge(q_stored[b], T // 2 * 16)

        @block.vector
        def _(dve):
            link = Chain(dve, own)
            def normalise(n):
                if n >= 2:
                    dve.wait_ge(h_turned, n - 1)
                    dve.wait_ge(h_stored[n % 2], 16 * (n // 2))
                dve.tensor_scalar(h[n % 2][:, :], keep.x[:, n, :], mv[:, n, 0:1], rstd[:, n:n + 1], ALU.subtract, ALU.mult)\
                   .then_inc(h_ready, 1)

            def split_h(n):
                dve.wait_ge(hT_ready, n + 1)
                dve.tensor_tensor(hT_lo[:, :, :], hT[n % 2][:, :, :], hT_hi[:, :, :].bitcast(F32), ALU.subtract).then_inc(hT_lo_ready, 1)

            def take_query(n):
                dve.wait_ge(done["q"], n + 1)
                if n:
                    dve.wait_ge(normed, n)
                dve.tensor_tensor(first[:, :], pF["q"][0:R, :], keep.b1["q"][0:R, :], ALU.add).then_inc(taken["q"], 1)

            def take_row(n, net):
                dve.wait_ge(done[net], n + 1)
                if n >= 2:
                    dve.wait_ge(rows_stored[n % 2], 32 * (n // 2))
                dve.tensor_tensor(row[n % 2][:, "kv".index(net), :], pF[net][0:R, :], keep.b1[net][0:R, :], ALU.add)\
                   .then_inc(taken[net], 1)

            def normalise_query(n):
                dve.wait_ge(squared, n + 1)
                dve.tensor_scalar(var_q[:, :], sumsq[:, :], EPS, None, ALU.add).then_inc(var_q_ready, 1)
                dve.wait_ge(root_q_ready, n + 1)
                reciprocal_root(dve, link, var_q[:, :], root_q[:, :], rstd_q[:, :], tmp_q[:, :])
                if n:
                    dve.wait_ge(q_turned, n)
                dve.tensor_scalar(q_norm[:, :], first[:, :], rstd_q[:, 0:1], None, ALU.mult).then_inc(normed, 1)

            def finish_query(n):
                to = q_row[n % 2]
                dve.wait_ge(q_done, n + 1)
                if n >= 2:
                    dve.wait_ge(q_stored[n % 2], 16 * (n // 2))
                link(dve.tensor_tensor(to[:, 0:D], pQ[0:R, :], keep.b2q[0:R, :], ALU.add))
                dve.sem_inc(q_taken, 1)
                link(dve.tensor_tensor(q_bias[:, :], to[:, 0:D], keep.b2k[0:R, :], ALU.mult))
                dve.tensor_reduce(to[:, D:Q_W], q_bias[:, :].rearrange("p (h d) -> p h d", h=HEADS), AX.X, ALU.add)\
                   .then_inc(q_ready, 1)

            normalise(0)
            split_h(0)
            ranks.prepare(dve)
            for n in range(T):
                if n + 1 < T:
                    normalise(n + 1)
                take_query(n)
                normalise_query(n)
                take_row(n, "k")
                lookups = Ranks.LOOKUPS[n]
                in_tile = Ranks.IN_TILE[n]

                def take_ranks(k):
                    for g in in_tile[k]:
                        ranks.in_tile(dve, g)
                    for g in lookups[k]:
                        ranks.pick(dve, g)

                take_ranks(0)
                if n:
                    finish_query(n - 1)
                take_ranks(1)
                take_row(n, "v")
                take_ranks(2)
                if n + 1 < T:
                    split_h(n + 1)
                for g in Ranks.ONE_HOTS[n]:
                    ranks.one_hots(dve, g)
                if n == Ranks.SCAN:
                    ranks.scan(dve)
                if n == Ranks.BASE:
                    ranks.add_start(dve)
            finish_query(T - 1)
            ranks.finish(dve)

        @block.gpsimd
        def _(pool):
            pool.memset(zero[:, :], 0.0).then_inc(zero_ready, 1)
            ranks.pool_work(pool)

        @block.scalar
        def _(act):
            def copy_hT(n):
                act.wait_ge(h_turned, n + 1)
                act.activation(hT_hi[:, :, :], pT[:, 0:KC * R].rearrange("p (c r) -> p c r", c=KC), ACT.Copy)\
                   .then_inc(hT_hi_ready, 1)
                if n >= 2:
                    act.wait_ge(hT_stored[n % 2], 16 * (n // 2))
                act.activation(hT[n % 2][:, :, :], pT[:, 0:KC * R].rearrange("p (c r) -> p c r", c=KC), ACT.Copy)\
                   .then_inc(hT_ready, 1)

            def squares(n):
                act.wait_ge(taken["q"], n + 1)
                if n:
                    act.wait_ge(squared, n)
                    act.wait_ge(var_q_ready, n)
                act.activation(square[:, :], first[:, :], ACT.Square, scale=D ** -0.5, accum_out=sumsq[:, :]).then_inc(squared, 1)

            copy_hT(0)
            for n in range(T):
                squares(n)
                act.wait_ge(var_q_ready, n + 1)
                act.activation(root_q[:, :], var_q[:, :], ACT.Sqrt).then_inc(root_q_ready, 1)
                for g in Ranks.COUNTS[n]:
                    ranks.copy_counts(act, g)
                for groups in Ranks.LOOKUPS[n]:
                    for g in groups:
                        for k in range(g * Ranks.TURNS + (g > 0), (g + 1) * Ranks.TURNS + (g + 1 < Ranks.GROUPS)):
                            ranks.copy_turned(act, k)
                if n + 1 < T:
                    copy_hT(n + 1)
                act.wait_ge(q_turned, n + 1)
                if n:
                    act.wait_ge(q_done, n)
                for c in range(KC):
                    q = act.activation(qT[:, c, :], pT[:, c * R:(c + 1) * R], ACT.Relu, bias=keep.be_q[:, c:c + 1],
                                       scale=keep.g_col_q[:, c:c + 1])
                q.then_inc(qT_ready, 1)

        @block.tensor
        def _(pe):
            def turn(to, of):
                for c in range(KC):
                    mm = pe.transpose(to[:, c * R:(c + 1) * R], of[:, c * P:(c + 1) * P], keep.ident[0:R, 0:R])
                return mm

            def turn_h(n):
                pe.wait_ge(h_ready, n + 1)
                if n >= 2:
                    pe.wait_ge(qT_ready, n - 1)
                turn(pT, h[n % 2]).then_inc(h_turned, 1)

            def first_layer(n, net):
                if n:
                    pe.wait_ge(taken[net], n)
                hi, lo = keep.w1_hi[net], keep.w1_lo[net]
                for k, (a, b) in enumerate(((hT_hi, hi), (hT_hi, lo), (hT_lo, hi))):
                    if k == 2 and net == "q":
                        pe.wait_ge(hT_lo_ready, n + 1)
                    for c in range(KC):
                        mm = pe.matmul(pF[net][0:R, :], a[:, c, :], b[:, c, :], start=(k == c == 0), stop=(k == 2 and c == KC - 1))
                return mm

            def second_layer(n):
                pe.wait_ge(qT_ready, n + 1)
                if n:
                    pe.wait_ge(q_taken, n)
                for c in range(KC):
                    mm = pe.matmul(pQ[0:R, :], qT[:, c, :], w2q[:, c, :], start=(c == 0), stop=(c == KC - 1))
                mm.then_inc(q_done, 1)

            turn_h(0)
            for n in range(T):
                lookups = Ranks.LOOKUPS[n]
                pe.wait_ge(hT_hi_ready, n + 1)
                first_layer(n, "q").then_inc(done["q"], 1)
                first_layer(n, "k").then_inc(done["k"], 1)
                for g in lookups[0]:
                    ranks.look_up(pe, g)
                if n:
                    second_layer(n - 1)
                else:
                    pe.wait_ge(w2_loaded, 16)
                for g in lookups[1]:
                    ranks.look_up(pe, g)
                first_layer(n, "v").then_inc(done["v"], 1)
                if n == Ranks.BASE:
                    ranks.add_totals(pe)
                for g in Ranks.COUNTS[n]:
                    ranks.count(pe, g)
                for g in lookups[2]:
                    ranks.look_up(pe, g)
                if n + 1 < T:
                    turn_h(n + 1)
                    pe.wait_ge(hT_ready, n + 2)
                pe.wait_ge(normed, n + 1)
                turn(pT, q_norm).then_inc(q_turned, 1)
            second_layer(T - 1)


def awaits(eng, sem, value):
    if not isinstance(value, int) or value > 0:
        eng.wait_ge(sem, value)


def edge_phase(nc, w, keep, dram, values):
    net = "v" if values else "k"
    n_net = int(values)
    side_w = HEADS if values else Q_W
    with ExitStack() as ctx:
        m = Memory(nc, ctx, f"edge_{net}")
        w2_hi = m.sb("w2_hi", [P, KC, D], F32R)
        w2_lo = m.sb("w2_lo", [P, KC, D], F32R)
        w1_hi = m.sb("w1_hi", [P, D], F32R)
        w1_lo = m.sb("w1_lo", [P, D], F32R)
        g_col = m.sb("g_col", [P, KC])
        be_col = m.sb("be_col", [P, KC])
        w2 = m.sb("w2", [P, KC, D])
        ef = [m.sb(f"ef{s}", [P, SUPER, EF]) for s in range(2)]
        table = [m.sb(f"table{s}", [P, SUPER, D]) for s in range(2)]
        side = [m.sb(f"side{s}", [P, SUPER, side_w]) for s in range(2)]
        src_at = [m.sb(f"src_at{s}", [P, SUPER], I32) for s in range(2)]
        side_at = [m.sb(f"side_at{s}", [P, SUPER], I32) for s in range(2)]
        out_at = [m.sb(f"out_at{s}", [P, SUPER], I32) for s in range(2)]
        efT_hi = [m.sb(f"efT_hi{s}", [EF, SUPER * P], F32R) for s in range(2)]
        efT_lo = [m.sb(f"efT_lo{s}", [EF, SUPER * P], F32R) for s in range(2)]
        first = [m.sb(f"first{t}", [P, D]) for t in range(SUPER)]
        square = m.sb("square", [P, D])
        sumsq = [m.sb(f"sumsq{t}", [P, 1]) for t in range(SUPER)]
        root = [m.sb(f"root{t}", [P, 1]) for t in range(SUPER)]
        rstd = [m.sb(f"rstd{t}", [P, 1]) for t in range(SUPER)]
        eps = m.sb("eps", [P, 1])
        var = m.sb("var", [P, 1])
        inverse = m.sb("inverse", [P, 1])
        error = m.sb("error", [P, 1])
        correction = m.sb("correction", [P, 1])
        hid = m.sb("hid", [P, KC, P])
        hid_hi = [m.sb(f"hid_hi{b}", [P, KC, P], F32R) for b in range(2)]
        hid_lo = [m.sb(f"hid_lo{b}", [P, KC, P], F32R) for b in range(2)]
        if values:
            drow = [m.sb(f"drow{s}", [P, SUPER, P]) for s in range(2)]
            dcol = m.sb("dcol", [P, SUPER])
            equal = [m.sb(f"equal{s}", [P, SUPER, P], F32R) for s in range(2)]
            weighted = m.sb("weighted", [P, SUM_W])
            weighted_hi = [m.sb(f"weighted_hi{b}", [P, SUM_W], F32R) for b in range(2)]
            weighted_lo = [m.sb(f"weighted_lo{b}", [P, SUM_W], F32R) for b in range(2)]
            out = [m.sb(f"out{s}", [P, SUPER, SUM_W]) for s in range(2)]
        else:
            product = m.sb("product", [P, D])
            logit = m.sb("logit", [P, HEADS])
            out = [m.sb(f"out{s}", [P, SUPER, L_W]) for s in range(2)]

        pE = m.ps("pE")
        pF = [m.ps(f"pF{b}") for b in range(2)]
        pH = m.ps("pH")
        pL = [m.ps(f"pL{b}") for b in range(2)]
        if values:
            pS = m.ps("pS")
            pD = m.ps("pD")
            drow_in = [m.sem(f"drow_in{s}") for s in range(2)]
            dcol_ready = m.sem("dcol_ready")
            equal_ready = m.sem("equal_ready")
            weighted_ready = m.sem("weighted_ready")
            weighted_hi_ready = m.sem("weighted_hi_ready")
            weighted_lo_ready = m.sem("weighted_lo_ready")
            sum_done = m.sem("sum_done")
            sum_copied = m.sem("sum_copied")
        else:
            dst_written = m.sem("dst_written")
            out_cleared = m.sem("out_cleared")
            heads_added = m.sem("heads_added")
            logits_ready = m.sem("logits_ready")

        w2_in = m.sem("w2_in")
        cols_in = m.sem("cols_in")
        w2_hi_ready = m.sem("w2_hi_ready")
        w1_hi_ready = m.sem("w1_hi_ready")
        weights_split = m.sem("weights_split")
        cleared = m.sem("cleared")
        ef_in = [m.sem(f"ef_in{s}") for s in range(2)]
        table_in = [m.sem(f"table_in{s}") for s in range(2)]
        side_in = [m.sem(f"side_in{s}") for s in range(2)]
        src_copied = m.sem("src_copied")
        side_copied = m.sem("side_copied")
        out_copied = m.sem("out_copied")
        ef_turned = m.sem("ef_turned")
        efT_hi_ready = m.sem("efT_hi_ready")
        efT_lo_ready = m.sem("efT_lo_ready")
        first_done = m.sem("first_done")
        first_ready = m.sem("first_ready")
        squared = m.sem("squared")
        root_ready = m.sem("root_ready")
        var_ready = m.sem("var_ready")
        inverse_ready = m.sem("inverse_ready")
        error_ready = m.sem("error_ready")
        correction_ready = m.sem("correction_ready")
        rstd_ready = m.sem("rstd_ready")
        normed = m.sem("normed")
        turned = m.sem("turned")
        hid_ready = m.sem("hid_ready")
        hid_hi_ready = m.sem("hid_hi_ready")
        hid_lo_ready = m.sem("hid_lo_ready")
        second_done = m.sem("second_done")
        second_used = m.sem("second_used")
        out_ready = m.sem("out_ready")
        out_done = [m.sem(f"out_done{t}") for t in range(SUPER)]

        PAIRS = SUPERS // 2

        def rolled(eng, start, step, end):
            def pair(i):
                first_pair, last_pair = (isinstance(i, int) and i == k for k in (0, PAIRS - 1))
                for s in range(2):
                    def super_at(n):
                        if first_pair and s + n < 0 or last_pair and s + n > 1:
                            return None
                        return (i + (s + n) // 2, (s + n) % 2)

                    def tile_at(n, t):
                        where = super_at((t + n) // SUPER)
                        return where and (*where, (t + n) % SUPER)

                    start(super_at)
                    for t in range(SUPER):
                        step(t, lambda n: tile_at(n, t), super_at)

            pair(0)
            with eng.Fori(1, PAIRS - 1) as i:
                pair(i)
            pair(PAIRS - 1)
            end()

        def nothing(*_):
            pass

        def each(body, where, *more):
            if where:
                body(*where, *more)

        def number(i, s, t):
            return (2 * i + s) * SUPER + t

        LAST = [(PAIRS - 1, 1, t) for t in range(SUPER)]
        block = ctx.enter_context(nc.Block())

        @block.sync
        def _(sp):
            def load_ef(i, s):
                j = 2 * i + s
                awaits(sp, ef_turned, j - 1)
                sp.dma_start(ef[s][0:EDGE_ROWS, :, :],
                             w["edge_attr_128"][bass.ds(j * (SUPER * EDGE_ROWS), SUPER * EDGE_ROWS), :]
                             .rearrange("(t p) f -> p t f", t=SUPER)).then_inc(ef_in[s], 16)

            def load_drow(i, s):
                j = 2 * i + s
                awaits(sp, equal_ready, SUPER * (j - 1))
                sp.dma_start(drow[s][:, :, :].rearrange("p t e -> p (t e)"),
                             dram.dst_rows[bass.ds(j * SUPER, SUPER), :].rearrange("t p -> (t p)").partition_broadcast(P))\
                  .then_inc(drow_in[s], 16)

            def start(supertile):
                each(load_ef, supertile(2))
                if values:
                    each(load_drow, supertile(2))

            def end():
                for t in range(SUPER):
                    sp.wait_ge(out_done[t], 16 * SUPERS)

            sp.wait_ge(cleared, 3)
            for s in range(2):
                load_ef(0, s)
            sp.dma_start(w2[:, :, :], w[f"h{net}_W2"].rearrange("(r p) n -> p r n", p=P)).then_inc(w2_in, 16)
            sp.dma_start(g_col[:, :], col(w[f"h{net}_g"]), allow_slow_non_contiguous=True).then_inc(cols_in, 16)
            sp.dma_start(be_col[:, :], col(w[f"h{net}_be"]), allow_slow_non_contiguous=True).then_inc(cols_in, 16)
            if values:
                for s in range(2):
                    load_drow(0, s)
            rolled(sp, start, nothing, end)

        @block.gpsimd
        def _(pool):
            def gather_table(i, s):
                j = 2 * i + s
                awaits(pool, first_ready, SUPER * (j - 1))
                wait_here(pool, keep.pool_passed)
                pool.tensor_copy(src_at[s][:, :], keep.src_i[:, bass.ds(j * SUPER, SUPER)]).then_inc(src_copied, 1)
                pool.wait_ge(src_copied, j + 1)
                wait_here(pool, keep.pool_passed)
                for t in range(SUPER):
                    pool.indirect_dma_start(out=table[s][:, t, :], out_offset=None, in_=dram.table[n_net],
                                            in_offset=bass.IndirectOffsetOnAxis(ap=src_at[s][:, t:t + 1], axis=0))\
                        .then_inc(table_in[s], 16)

            def gather_side(i, s):
                j = 2 * i + s
                awaits(pool, weighted_ready if values else out_ready, SUPER * (j - 1))
                wait_here(pool, keep.pool_passed)
                pool.tensor_copy(side_at[s][:, :], (keep.place_i if values else keep.dst_i)[:, bass.ds(j * SUPER, SUPER)])\
                    .then_inc(side_copied, 1)
                pool.wait_ge(side_copied, j + 1)
                wait_here(pool, keep.pool_passed)
                for t in range(SUPER):
                    pool.indirect_dma_start(out=side[s][:, t, :], out_offset=None, in_=dram.expo if values else dram.query,
                                            in_offset=bass.IndirectOffsetOnAxis(ap=side_at[s][:, t:t + 1], axis=0))\
                        .then_inc(side_in[s], 16)

            def scatter(i, s, t):
                j = 2 * i + s
                if t == 0:
                    for u in range(SUPER):
                        awaits(pool, out_done[u], 16 * (j - 1))
                    wait_here(pool, keep.pool_passed)
                    pool.tensor_copy(out_at[s][:, :], (keep.sum_i if values else keep.place_i)[:, bass.ds(j * SUPER, SUPER)])\
                        .then_inc(out_copied, 1)
                    pool.wait_ge(out_copied, j + 1)
                pool.wait_ge(out_ready, number(i, s, t) + 1)
                awaits(pool, out_done[t], 16 * j)
                wait_here(pool, keep.pool_passed)
                where = bass.IndirectOffsetOnAxis(ap=out_at[s][:, t:t + 1], axis=0)
                if values:
                    pool.indirect_dma_start(out=dram.sums[t], out_offset=where, in_=out[s][:, t, :], in_offset=None,
                                            compute_op=ALU.add).then_inc(out_done[t], 16)
                else:
                    pool.indirect_dma_start(out=dram.logits, out_offset=where, in_=out[s][:, t, :],
                                            in_offset=None).then_inc(out_done[t], 16)

            BEHIND = 3 if values else 1

            def start(supertile):
                if supertile(-1):
                    scatter(*supertile(-1), SUPER - BEHIND)
                each(gather_side, supertile(1))
                each(gather_table, supertile(2))
                for t in range(SUPER - BEHIND + 1, SUPER):
                    if supertile(-1):
                        scatter(*supertile(-1), t)
                for t in range(SUPER - BEHIND):
                    scatter(*supertile(0), t)

            def end():
                for t in range(SUPER - BEHIND, SUPER):
                    scatter(*LAST[t])

            for s in range(2):
                pool.memset(ef[s][:, :, :], 0.0).then_inc(cleared, 1)
            gather_table(0, 0)
            gather_table(0, 1)
            gather_side(0, 0)
            rolled(pool, start, nothing, end)

        @block.scalar
        def _(act):
            def split_efT(i, s):
                act.wait_ge(ef_turned, 2 * i + s + 1)
                act.activation(efT_hi[s][:, :], pE[:, :], ACT.Copy).then_inc(efT_hi_ready, 1)

            def squares(i, s, t):
                n = number(i, s, t)
                act.wait_ge(first_ready, n + 1)
                awaits(act, squared, n)
                awaits(act, rstd_ready, n - SUPER + 1)
                act.activation(square[:, :], first[t][:, :], ACT.Square, scale=D ** -0.5, accum_out=sumsq[t][:, :])\
                   .then_inc(squared, 1)
                act.wait_ge(squared, n + 1)
                act.activation(root[t][:, :], sumsq[t][:, :], ACT.Sqrt, bias=eps[:, 0:1]).then_inc(root_ready, 1)

            def hidden(i, s, t):
                n = number(i, s, t)
                act.wait_ge(turned, n + 1)
                awaits(act, hid_lo_ready, n)
                for c in range(KC):
                    r = act.activation(hid[:, c, :], pH[:, c * P:(c + 1) * P], ACT.Relu, bias=be_col[:, c:c + 1],
                                       scale=g_col[:, c:c + 1])
                r.then_inc(hid_ready, 1)
                act.wait_ge(hid_ready, n + 1)
                awaits(act, second_done, n - 1)
                act.activation(hid_hi[t % 2][:, :, :], hid[:, :, :], ACT.Copy).then_inc(hid_hi_ready, 1)

            def split_weighted(i, s, t):
                n = number(i, s, t)
                act.wait_ge(second_used, n + 1)
                act.wait_ge(weighted_ready, n + 1)
                awaits(act, sum_done, n - 1)
                act.activation(weighted_hi[t % 2][:, :], weighted[:, :], ACT.Copy).then_inc(weighted_hi_ready, 1)

            def copy_sum(i, s, t):
                n = number(i, s, t)
                act.wait_ge(sum_done, n + 1)
                awaits(act, out_done[t], 16 * (2 * i + s - 1))
                act.activation(out[s][:, t, 0:D], pS[:, :], ACT.Copy).then_inc(sum_copied, 1)
                act.activation(out[s][:, t, D:SUM_W], pD[:, 0:HEADS], ACT.Copy).then_inc(sum_copied, 1)
                act.wait_ge(sum_copied, 2 * (n + 1))
                act.sem_inc(out_ready, 1)

            def step(t, tile, supertile):
                if values:
                    each(copy_sum, tile(-3))
                each(hidden, tile(1))
                if values:
                    each(split_weighted, tile(-1))
                each(squares, tile(3))
                if t == 2:
                    each(split_efT, supertile(2))

            def end():
                if values:
                    copy_sum(*LAST[1])
                    split_weighted(*LAST[3])
                    copy_sum(*LAST[2])
                    copy_sum(*LAST[3])

            for s in range(2):
                split_efT(0, s)
            act.wait_ge(cleared, 3)
            for t in range(3):
                squares(0, 0, t)
            act.wait_ge(w2_in, 16)
            act.activation(w2_hi[:, :, :], w2[:, :, :], ACT.Copy).then_inc(w2_hi_ready, 1)
            act.wait_ge(cols_in, 32)
            hidden(0, 0, 0)
            rolled(act, nothing, step, end)

        @block.vector
        def _(dve):
            def split_efT(i, s):
                j = 2 * i + s
                dve.wait_ge(efT_hi_ready, j + 1)
                dve.tensor_tensor(efT_lo[s][:, :], pE[:, :], efT_hi[s][:, :], ALU.subtract).then_inc(efT_lo_ready, 1)

            def add_table(i, s, t):
                n = number(i, s, t)
                if t == 0:
                    dve.wait_ge(table_in[s], 64 * (i + 1))
                dve.wait_ge(first_done, n + 1)
                awaits(dve, turned, n - SUPER + 1)
                dve.tensor_tensor(first[t][:, :], pF[t % 2][:, :], table[s][:, t, :], ALU.add).then_inc(first_ready, 1)


            def invert(i, s, t):
                n = number(i, s, t)
                dve.wait_ge(root_ready, n + 1)
                awaits(dve, rstd_ready, n)
                dve.tensor_scalar(var[:, :], sumsq[t][:, :], EPS, None, ALU.add).then_inc(var_ready, 1)
                dve.reciprocal(inverse[:, :], root[t][:, :]).then_inc(inverse_ready, 1)

            def newton_product(i, s, t):
                n = number(i, s, t)
                dve.wait_ge(var_ready, n + 1)
                dve.wait_ge(inverse_ready, n + 1)
                dve.scalar_tensor_tensor(out=error[:, :], in0=inverse[:, :], scalar=var[:, 0:1], in1=inverse[:, :],
                                         op0=ALU.mult, op1=ALU.mult).then_inc(error_ready, 1)

            def newton_factor(i, s, t):
                dve.wait_ge(error_ready, number(i, s, t) + 1)
                dve.tensor_scalar(correction[:, :], error[:, :], -0.5, 1.5, ALU.mult, ALU.add).then_inc(correction_ready, 1)

            def correct(i, s, t):
                n = number(i, s, t)
                dve.wait_ge(correction_ready, n + 1)
                awaits(dve, normed, n - SUPER + 1)
                dve.tensor_tensor(rstd[t][:, :], inverse[:, :], correction[:, :], ALU.mult).then_inc(rstd_ready, 1)

            def normalise(i, s, t):
                n = number(i, s, t)
                dve.wait_ge(rstd_ready, n + 1)
                dve.wait_ge(squared, n + 1)
                dve.tensor_scalar(first[t][:, :], first[t][:, :], rstd[t][:, 0:1], None, ALU.mult).then_inc(normed, 1)

            def split_hidden(i, s, t):
                n = number(i, s, t)
                dve.wait_ge(hid_hi_ready, n + 1)
                awaits(dve, second_done, n - 1)
                dve.tensor_tensor(hid_lo[t % 2][:, :, :], hid[:, :, :], hid_hi[t % 2][:, :, :], ALU.subtract)\
                   .then_inc(hid_lo_ready, 1)

            def compare(i, s, t):
                j = 2 * i + s
                if t == 0:
                    awaits(dve, equal_ready, SUPER * j)
                    dve.tensor_copy(dcol[:, :], keep.dst_f[:, bass.ds(j * SUPER, SUPER)]).then_inc(dcol_ready, 1)
                    dve.wait_ge(dcol_ready, j + 1)
                    dve.wait_ge(drow_in[s], 16 * (i + 1))
                awaits(dve, sum_done, number(i, s, t) - 2 * SUPER + 1)
                dve.tensor_scalar(equal[s][:, t, :], drow[s][:, t, :], dcol[:, t:t + 1], None, ALU.is_equal).then_inc(equal_ready, 1)

            def write_destinations(i, s):
                j = 2 * i + s
                for t in range(SUPER):
                    awaits(dve, out_done[t], 16 * (j - 1))
                dve.tensor_copy(out[s][:, :, HEADS:HEADS + 1].rearrange("p t a -> p (t a)"),
                                keep.dst_f[:, bass.ds(j * SUPER, SUPER)]).then_inc(dst_written, 1)


            def multiply_query(i, s, t):
                n = number(i, s, t)
                dve.wait_ge(second_done, n + 1)
                awaits(dve, heads_added, n)
                if t == 0:
                    dve.wait_ge(side_in[s], 64 * (i + 1))
                dve.tensor_tensor(product[:, :], pL[t % 2][:, :], side[s][:, t, 0:D], ALU.mult).then_inc(second_used, 1)

            def add_heads(i, s, t):
                n = number(i, s, t)
                dve.wait_ge(second_used, n + 1)
                awaits(dve, logits_ready, n)
                dve.tensor_reduce(logit[:, :], product[:, :].rearrange("p (h d) -> p h d", h=HEADS), AX.X, ALU.add)\
                   .then_inc(heads_added, 1)

            def add_bias(i, s, t):
                n = number(i, s, t)
                dve.wait_ge(heads_added, n + 1)
                dve.wait_ge(dst_written, 2 * i + s + 1)
                dve.tensor_tensor(out[s][:, t, 0:HEADS], logit[:, :], side[s][:, t, D:Q_W], ALU.add).then_inc(logits_ready, 1)
                dve.wait_ge(logits_ready, n + 1)
                dve.sem_inc(out_ready, 1)


            def weigh(i, s, t):
                n = number(i, s, t)
                dve.wait_ge(second_done, n + 1)
                awaits(dve, weighted_lo_ready, n)
                if t == 0:
                    dve.wait_ge(side_in[s], 64 * (i + 1))
                heads = side[s][:, t, :].unsqueeze(2).to_broadcast([P, HEADS, HEAD])
                dve.tensor_tensor(weighted[:, 0:D].rearrange("p (h d) -> p h d", h=HEADS),
                                  pL[t % 2][:, :].rearrange("p (h d) -> p h d", h=HEADS), heads, ALU.mult)\
                   .then_inc(second_used, 1)
                dve.tensor_copy(weighted[:, D:SUM_W], side[s][:, t, :]).then_inc(weighted_ready, 1)

            def split_weighted(i, s, t):
                n = number(i, s, t)
                dve.wait_ge(weighted_hi_ready, n + 1)
                awaits(dve, sum_done, n - 1)
                dve.tensor_tensor(weighted_lo[t % 2][:, :], weighted[:, :], weighted_hi[t % 2][:, :], ALU.subtract)\
                   .then_inc(weighted_lo_ready, 1)

            def step(t, tile, supertile):
                each(invert, tile(2))
                each(weigh if values else multiply_query, tile(-1))
                each(newton_product, tile(2))
                if not values:
                    each(add_heads, tile(-1))
                each(newton_factor, tile(2))
                each(add_table, tile(3))
                each(correct, tile(2))
                if not values:
                    each(add_bias, tile(-1))
                each(normalise, tile(2))
                each(split_hidden, tile(1))
                if values:
                    each(split_weighted, tile(-1))
                if t == 3:
                    each(split_efT, supertile(2))
                if values:
                    each(compare, tile(SUPER))
                elif t == 2:
                    each(write_destinations, supertile(1))

            def end():
                if values:
                    weigh(*LAST[3])
                    split_weighted(*LAST[3])
                else:
                    for part in (multiply_query, add_heads, add_bias):
                        part(*LAST[3])

            dve.memset(eps[:, :], EPS).then_inc(cleared, 1)
            dve.tensor_copy(w1_hi[:, :], keep.w1e[net][:, :]).then_inc(w1_hi_ready, 1)
            dve.wait_ge(w1_hi_ready, 1)
            dve.tensor_tensor(w1_lo[:, :], keep.w1e[net][:, :], w1_hi[:, :], ALU.subtract).then_inc(weights_split, 1)
            if not values:
                for s in range(2):
                    dve.memset(out[s][:, :, :], 0.0).then_inc(out_cleared, 1)
                dve.wait_ge(out_cleared, 2)
            for s in range(2):
                split_efT(0, s)
            for t in range(3):
                add_table(0, 0, t)
            for t in range(2):
                for part in (invert, newton_product, newton_factor, correct, normalise):
                    part(0, 0, t)
            dve.wait_ge(w2_hi_ready, 1)
            dve.tensor_tensor(w2_lo[:, :, :], w2[:, :, :], w2_hi[:, :, :], ALU.subtract).then_inc(weights_split, 1)
            split_hidden(0, 0, 0)
            if values:
                for t in range(SUPER):
                    compare(0, 0, t)
            else:
                write_destinations(0, 0)
            rolled(dve, nothing, step, end)

        @block.tensor
        def _(pe):
            def turn_ef(i, s):
                j = 2 * i + s
                pe.wait_ge(ef_in[s], 16 * (i + 1))
                awaits(pe, efT_lo_ready, j)
                for t in range(SUPER):
                    mm = pe.transpose(pE[:, t * P:(t + 1) * P], ef[s][:, t, :], keep.ident[:, :])
                mm.then_inc(ef_turned, 1)

            def first_layer(i, s, t):
                n = number(i, s, t)
                if t == 0:
                    pe.wait_ge(efT_lo_ready, 2 * i + s + 1)
                awaits(pe, first_ready, n - 1)
                edges = slice(t * P, (t + 1) * P)
                pe.matmul(pF[t % 2][:, :], efT_hi[s][:, edges], w1_hi[:, :], start=True, stop=False)
                pe.matmul(pF[t % 2][:, :], efT_hi[s][:, edges], w1_lo[:, :], start=False, stop=False)
                pe.matmul(pF[t % 2][:, :], efT_lo[s][:, edges], w1_hi[:, :], start=False, stop=True).then_inc(first_done, 1)

            def turn(i, s, t):
                n = number(i, s, t)
                pe.wait_ge(normed, n + 1)
                awaits(pe, hid_ready, n)
                for c in range(KC):
                    feats = slice(c * P, (c + 1) * P)
                    mm = pe.transpose(pH[:, feats], first[t][:, feats], keep.ident[:, :])
                mm.then_inc(turned, 1)

            def second_layer(i, s, t):
                n = number(i, s, t)
                pe.wait_ge(hid_lo_ready, n + 1)
                awaits(pe, second_used, n - 1)
                hi, lo, bank = hid_hi[t % 2], hid_lo[t % 2], pL[t % 2]
                for c in range(KC):
                    pe.matmul(bank[:, :], hi[:, c, :], w2_hi[:, c, :], start=(c == 0), stop=False)
                    pe.matmul(bank[:, :], hi[:, c, :], w2_lo[:, c, :], start=False, stop=False)
                    mm = pe.matmul(bank[:, :], lo[:, c, :], w2_hi[:, c, :], start=False, stop=(c == KC - 1))
                mm.then_inc(second_done, 1)

            def add_rows(i, s, t):
                n = number(i, s, t)
                pe.wait_ge(equal_ready, n + 1)
                pe.wait_ge(weighted_lo_ready, n + 1)
                awaits(pe, sum_copied, 2 * n)
                for cols, bank in ((slice(0, D), pS[:, :]), (slice(D, SUM_W), pD[:, 0:HEADS])):
                    pe.matmul(bank, equal[s][:, t, :], weighted_hi[t % 2][:, cols], start=True, stop=False)
                    mm = pe.matmul(bank, equal[s][:, t, :], weighted_lo[t % 2][:, cols], start=False, stop=True)
                mm.then_inc(sum_done, 1)

            def step(t, tile, supertile):
                each(first_layer, tile(3))
                each(turn, tile(1))
                second_layer(*tile(0))
                if values:
                    each(add_rows, tile(-2))
                if t == 1:
                    each(turn_ef, supertile(2))

            def end():
                if values:
                    add_rows(*LAST[2])
                    add_rows(*LAST[3])

            for s in range(2):
                turn_ef(0, s)
            pe.wait_ge(weights_split, 1)
            for t in range(3):
                first_layer(0, 0, t)
            turn(0, 0, 0)
            pe.wait_ge(weights_split, 2)
            rolled(pe, nothing, step, end)


def segment_softmax(nc, w, keep, late, dram):
    with ExitStack() as ctx:
        m = Memory(nc, ctx, "soft")
        place = m.sb("place", [P, SPAN, L_W])
        dest = m.sb("dest", [P, SPAN])
        apart = m.sb("apart", [P, SPAN])
        ahead = m.sb("ahead", [P, SPAN])
        lead = m.sb("lead", [P, SPAN])
        trail = m.sb("trail", [P, SPAN])
        fwd = m.sb("fwd", [P, HEADS, SPAN])
        best = m.sb("best", [P, HEADS, SPAN])
        expo = m.sb("expo", [P, SPAN, HEADS])
        ends = m.sb("ends", [P, 4, HEADS])
        endsT = m.sb("endsT", [HEADS, 4, P])
        whole = m.sb("whole", [HEADS, P])
        joined = m.sb("joined", [HEADS, P])
        joined_b = m.sb("joined_b", [HEADS, P])
        through = m.sb("through", [HEADS, P])
        carry = m.sb("carry", [HEADS, 2, P])
        scanned = m.sb("scanned", [HEADS, 2, P])
        carry_in = m.sb("carry_in", [P, 2, HEADS])
        pA = m.ps("pA")
        pB = m.ps("pB")
        loaded = m.sem("loaded")
        own = m.sem("own")
        ends_ready = m.sem("ends_ready")
        turned = m.sem("turned")
        carry_ready = m.sem("carry_ready")
        carried = m.sem("carried")
        less = m.sem("less")
        expo_ready = m.sem("expo_ready")
        stored = m.sem("stored")
        scratch = m.sb("scratch", [P, D])
        mean = m.sb("mean", [P, 2 * KC + 1])
        centring_in = m.sem("centring_in")
        late_in = m.sem("late_in")
        summed = m.sem("summed")
        mean_ready = m.sem("mean_ready")
        centred = m.sem("centred")
        block = ctx.enter_context(nc.Block())

        @block.sync
        def _(sp):
            sp.dma_start(place[:, :, :], dram.logits.rearrange("(p j) f -> p j f", p=P)).then_inc(loaded, 16)
            sp.dma_start(late.w1[:, :, :], w["no_W1"].rearrange("(r p) n -> p r n", p=P)).then_inc(centring_in, 16)
            sp.dma_start(late.b1[:, :], row_bc(w["no_b1"])).then_inc(centring_in, 16)
            for to, of in ((late.b2v[:, :], row_bc(w["hv_b2"])),
                           (late.w2[:, :, :], w["no_W2"].rearrange("(r p) n -> p r n", p=P)),
                           (late.ws[:, :, :], w["Ws"].rearrange("(r p) n -> p r n", p=P)),
                           (late.bs[:, :], row_bc(w["bs"])),
                           (late.b2[:, :], row_bc(w["no_b2"])),
                           (late.g_col[:, :], col(w["no_g"])),
                           (late.be_col[:, :], col(w["no_be"])),
                           (late.eb2[:, :], w["b2"])):
                sp.dma_start(to, of, allow_slow_non_contiguous=True).then_inc(late_in, 16)
            sp.wait_ge(late_in, 8 * 16)
            sp.wait_ge(expo_ready, 1)
            sp.dma_start(dram.expo.rearrange("(p j) f -> p j f", p=P), expo[:, :, :]).then_inc(stored, 16)
            sp.wait_ge(stored, 16)

        @block.scalar
        def _(act):
            act.wait_ge(centring_in, 32)
            vectors = [late.w1[:, r, :] for r in range(2 * KC)] + [late.b1[:, :]]
            for r, vector in enumerate(vectors):
                if r:
                    act.wait_ge(summed, r)
                act.activation(scratch[:, :], vector, ACT.Copy, accum_out=mean[:, r:r + 1]).then_inc(summed, 1)
            act.wait_ge(summed, len(vectors))
            act.activation(mean[:, :], mean[:, :], ACT.Copy, scale=-1.0 / D).then_inc(mean_ready, 1)
            act.wait_ge(mean_ready, 1)
            for r, vector in enumerate(vectors):
                act.activation(vector, vector, ACT.Identity, bias=mean[:, r:r + 1]).then_inc(centred, 1)
            act.wait_ge(less, 1)
            act.activation(expo[:, :, :], expo[:, :, :], ACT.Exp, scale=HEAD ** -0.5).then_inc(expo_ready, 1)

        @block.vector
        def _(dve):
            link = Chain(dve, own)
            dve.wait_ge(loaded, 16)
            link(dve.tensor_copy(dest[:, :].unsqueeze(2), place[:, :, HEADS:HEADS + 1]))
            link(dve.memset(apart[:, :], NEG))
            link(dve.memset(ahead[:, :], NEG))
            link(dve.tensor_tensor(apart[:, 1:SPAN], dest[:, 1:SPAN], dest[:, 0:SPAN - 1], ALU.not_equal))
            link(dve.tensor_scalar(apart[:, 1:SPAN], apart[:, 1:SPAN], NEG, None, ALU.mult))
            link(dve.tensor_copy(ahead[:, 0:SPAN - 1], apart[:, 1:SPAN]))
            link(dve.tensor_scalar(lead[:, :], dest[:, :], dest[:, 0:1], NEG, ALU.not_equal, ALU.mult))
            link(dve.tensor_scalar(trail[:, :], dest[:, :], dest[:, SPAN - 1:SPAN], NEG, ALU.not_equal, ALU.mult))
            for h in range(HEADS):
                s = dve.tensor_tensor_scan(fwd[:, h, :], apart[:, :], place[:, :, h:h + 1].rearrange("p j a -> p (j a)"),
                                           NEG, ALU.add, ALU.max)
            link(s)
            for h in range(HEADS):
                s = dve.tensor_tensor_scan(best[:, h, ::-1], ahead[:, ::-1], fwd[:, h, ::-1], NEG, ALU.add, ALU.max)
            link(s)
            link(dve.tensor_copy(ends[:, 0, :].unsqueeze(2), best[:, :, 0:1]))
            link(dve.tensor_copy(ends[:, 1, :].unsqueeze(2), best[:, :, SPAN - 1:SPAN]))
            link(dve.tensor_copy(ends[:, 2, :], dest[:, 0:1].to_broadcast([P, HEADS])))
            dve.tensor_copy(ends[:, 3, :], dest[:, SPAN - 1:SPAN].to_broadcast([P, HEADS])).then_inc(ends_ready, 1)
            dve.wait_ge(turned, 1)
            link(dve.tensor_copy(endsT[:, :, :].rearrange("h k p -> h (k p)"), pA[0:HEADS, :]))
            first, last = endsT[:, 2, :], endsT[:, 3, :]
            link(dve.memset(joined[:, :], NEG))
            link(dve.memset(joined_b[:, :], NEG))
            link(dve.tensor_tensor(whole[:, :], first, last, ALU.not_equal))
            link(dve.tensor_scalar(whole[:, :], whole[:, :], NEG, None, ALU.mult))
            link(dve.tensor_tensor(joined[:, 1:P], first[:, 1:P], last[:, 0:P - 1], ALU.not_equal))
            link(dve.tensor_scalar(joined[:, 1:P], joined[:, 1:P], NEG, None, ALU.mult))
            link(dve.tensor_copy(joined_b[:, 0:P - 1], joined[:, 1:P]))
            link(dve.memset(carry[:, :, :], NEG))
            link(dve.tensor_tensor(through[:, :], whole[:, :], joined[:, :], ALU.min))
            link(dve.tensor_tensor_scan(scanned[:, 0, :], through[:, :], endsT[:, 1, :], NEG, ALU.add, ALU.max))
            link(dve.tensor_tensor(through[:, :], whole[:, :], joined_b[:, :], ALU.min))
            link(dve.tensor_tensor_scan(scanned[:, 1, ::-1], through[:, ::-1], endsT[:, 0, ::-1], NEG, ALU.add, ALU.max))
            link(dve.tensor_tensor(carry[:, 0, 1:P], scanned[:, 0, 0:P - 1], joined[:, 1:P], ALU.add))
            dve.tensor_tensor(carry[:, 1, 0:P - 1], scanned[:, 1, 1:P], joined_b[:, 0:P - 1], ALU.add).then_inc(carry_ready, 1)
            dve.wait_ge(carried, 1)
            link(dve.tensor_copy(carry_in[:, :, :].rearrange("p k h -> p (k h)"), pB[:, 0:2 * HEADS]))
            for k, mask in enumerate((lead, trail)):
                for h in range(HEADS):
                    s = dve.scalar_tensor_tensor(out=best[:, h, :], in0=mask[:, :], scalar=carry_in[:, k, h:h + 1],
                                                 in1=best[:, h, :], op0=ALU.add, op1=ALU.max)
                link(s)
            dve.tensor_tensor(expo[:, :, :], place[:, :, 0:HEADS], best[:, :, :].rearrange("p h j -> p j h"), ALU.subtract)\
               .then_inc(less, 1)

        @block.tensor
        def _(pe):
            pe.wait_ge(ends_ready, 1)
            for k in range(4):
                mm = pe.transpose(pA[0:HEADS, k * P:(k + 1) * P], ends[:, k, :], keep.ident[:, :])
            mm.then_inc(turned, 1)
            pe.wait_ge(carry_ready, 1)
            for k in range(2):
                mm = pe.transpose(pB[:, k * HEADS:(k + 1) * HEADS], carry[:, k, :], keep.ident[0:HEADS, 0:HEADS])
            mm.then_inc(carried, 1)


def node_output(nc, w, keep, late, dram):
    with ExitStack() as ctx:
        m = Memory(nc, ctx, "outp")
        R = NODE_ROWS
        T = NODE_TILES
        w1, b1, b2v, w2, ws, bs, b2, g_col, be_col, eb2 = (
            late.w1, late.b1, late.b2v, late.w2, late.ws, late.bs, late.b2, late.g_col, late.be_col, late.eb2)
        order_i = m.sb("order_i", [P, EXPERTS], I32)
        order = m.sb("order", [P, EXPERTS])
        sums = [m.sb(f"sums{b}", [R, SUM_TABLES, SUM_W]) for b in range(2)]
        h = [m.sb(f"h{b}", [R, D]) for b in range(2)]
        hT = [m.sb(f"hT{b}", [P, KC, R]) for b in range(2)]
        den = m.sb("den", [R, HEADS])
        some = m.sb("some", [R, HEADS])
        att = [m.sb(f"att{b}", [R, D]) for b in range(2)]
        bias_v = m.sb("bias_v", [R, D])
        attT = m.sb("attT", [P, KC, R])
        first = m.sb("first", [R, D])
        square = m.sb("square", [R, D])
        sumsq = m.sb("sumsq", [R, 1])
        var = m.sb("var", [R, 2])
        root = m.sb("root", [R, 2])
        rstd = m.sb("rstd", [R, 2])
        tmp = m.sb("tmp", [R, 2])
        normed = m.sb("normed", [R, D])
        normT = m.sb("normT", [P, KC, R])
        x1 = [m.sb(f"x1_{b}", [R, D]) for b in range(2)]
        stats = m.sb("stats", [R, 6])
        mv = m.sb("mv", [R, 2])
        z = m.sb("z", [P, D])
        scores = m.sb("scores", [R, EXPERTS])
        top = m.sb("top", [R, 1])
        neg_top = m.sb("neg_top", [R, 1])
        chosen = m.sb("chosen", [R, EXPERTS])
        expo = m.sb("expo", [R, EXPERTS])
        total = m.sb("total", [R, 1])
        coef = m.sb("coef", [R, EXPERTS])
        coefT = m.sb("coefT", [EXPERTS, R])
        pT = [m.ps(f"pT{b}") for b in range(2)]
        pF = [m.ps(f"pF{b}") for b in range(2)]
        pY = m.ps("pY")
        pR = m.ps("pR")
        pB = m.ps("pB")

        order_ready = m.sem("order_ready")
        own = m.sem("own")
        sums_in = [m.sem(f"sums_in{b}") for b in range(2)]
        sums_added = m.sem("sums_added")
        den_ready = m.sem("den_ready")
        sums_used = m.sem("sums_used")
        pool_own = m.sem("pool_own")
        h_in = [m.sem(f"h_in{b}") for b in range(2)]
        hT_in = [m.sem(f"hT_in{b}") for b in range(2)]
        residual_ready = m.sem("residual_ready")
        att_ready = m.sem("att_ready")
        turn_done = m.sem("turn_done")
        turn_copied = m.sem("turn_copied")
        first_done = m.sem("first_done")
        first_ready = m.sem("first_ready")
        squared = m.sem("squared")
        var_ready = m.sem("var_ready")
        root_ready = m.sem("root_ready")
        normed_ready = m.sem("normed_ready")
        second_done = m.sem("second_done")
        second_taken = m.sem("second_taken")
        z_ready = m.sem("z_ready")
        zT_lo_ready = m.sem("zT_lo_ready")
        routed = m.sem("routed")
        top_ready = m.sem("top_ready")
        expo_ready = m.sem("expo_ready")
        coef_ready = m.sem("coef_ready")
        coef_turned = m.sem("coef_turned")
        coefT_ready = m.sem("coefT_ready")
        bias_done = m.sem("bias_done")
        bias_taken = m.sem("bias_taken")

        turns = [("att", 0)]
        for n in range(T + 1):
            turns += [(what, k) for what, k in (("z", n - 1), ("norm", n), ("att", n + 1))
                      if 0 <= k < T and (what != "norm" or n < T)]
        turn_no = {what: k for k, what in enumerate(turns)}
        block = ctx.enter_context(nc.Block())

        @block.sync
        def _(sp):
            def load_sums(n):
                b = n % 2
                if n >= 2:
                    sp.wait_ge(sums_used, n - 1)
                rows = slice(n * R, (n + 1) * R)
                for t in range(SUM_TABLES):
                    sp.dma_start(sums[b][:, t, :], dram.sums[t][rows, :]).then_inc(sums_in[b], 16)
                if n >= 2:
                    sp.wait_ge(first_done, n - 1)
                sp.dma_start(hT[b][:, :, :].rearrange("p c r -> p (c r)"), dram.hT[n]).then_inc(hT_in[b], 16)
                if n >= 2:
                    sp.wait_ge(second_taken, n - 1)
                sp.dma_start(h[b][:, :], dram.h[rows, :]).then_inc(h_in[b], 16)

            load_sums(0)
            load_sums(1)
            sp.dma_start(keep.expert_w1[:, :, :], w["W1"][0].rearrange("(r p) n -> p r n", p=P)).then_inc(keep.expert_in, 16)
            sp.dma_start(keep.expert_w2[:, :, :], w["W2"][0].rearrange("(r p) n -> p r n", p=P)).then_inc(keep.expert_in, 16)
            for n in range(2, T):
                load_sums(n)

        @block.gpsimd
        def _(pool):
            link = Chain(pool, pool_own)

            def add_tables(n):
                s = sums[n % 2]
                pool.wait_ge(sums_in[n % 2], SUM_TABLES * 16 * (n // 2 + 1))
                for t in range(1, SUM_TABLES):
                    link(pool.tensor_tensor(s[:, 0, :], s[:, 0, :], s[:, t, :], ALU.add))
                pool.sem_inc(sums_added, 1)

            def attention(n):
                to = att[n % 2]
                by_head = "p (h d) -> p h d"
                pool.wait_ge(den_ready, n + 1)
                if n >= 2:
                    pool.wait_ge(turn_done, turn_no["att", n - 2] + 1)
                pool.tensor_tensor(bias_v[:, :].rearrange(by_head, h=HEADS), b2v[0:R, :].rearrange(by_head, h=HEADS),
                                   some[:, :].unsqueeze(2).to_broadcast([R, HEADS, HEAD]), ALU.mult)
                link(pool.tensor_tensor(to[:, :].rearrange(by_head, h=HEADS),
                                        sums[n % 2][:, 0, 0:D].rearrange(by_head, h=HEADS),
                                        den[:, :].unsqueeze(2).to_broadcast([R, HEADS, HEAD]), ALU.mult))
                pool.sem_inc(sums_used, 1)
                link(pool.tensor_tensor(to[:, :], to[:, :], bias_v[:, :], ALU.add))
                pool.sem_inc(att_ready, 1)

            def residual(n):
                pool.wait_ge(h_in[n % 2], 16 * (n // 2 + 1))
                link(pool.tensor_tensor(h[n % 2][:, :], h[n % 2][:, :], b2[0:R, :], ALU.add))
                link(pool.tensor_tensor(h[n % 2][:, :], h[n % 2][:, :], keep.x[:, n, :], ALU.add))
                pool.sem_inc(residual_ready, 1)

            pool.iota(order_i[:, :], [[-1, EXPERTS]], base=EXPERTS, channel_multiplier=0).then_inc(order_ready, 1)
            add_tables(0)
            for n in range(T):
                attention(n)
                if n + 1 < T:
                    add_tables(n + 1)
                residual(n)

        @block.vector
        def _(dve):
            link = Chain(dve, own)
            dve.wait_ge(order_ready, 1)
            link(dve.tensor_copy(order[:, :], order_i[:, :]))

            def denominators(n):
                dve.wait_ge(sums_added, n + 1)
                if n:
                    dve.wait_ge(att_ready, n)
                total = sums[n % 2][:, 0, D:SUM_W]
                dve.tensor_scalar(some[:, :], total, 0.0, None, ALU.is_gt)
                link(dve.tensor_scalar(den[:, :], total, 1e-30, None, ALU.max))
                dve.reciprocal(den[:, :], den[:, :]).then_inc(den_ready, 1)

            def normalise_first(n):
                dve.wait_ge(first_done, n + 1)
                dve.tensor_tensor(first[:, :], pF[n % 2][0:R, :], b1[0:R, :], ALU.add).then_inc(first_ready, 1)
                dve.wait_ge(squared, n + 1)
                dve.tensor_scalar(var[:, 0:1], sumsq[:, :], EPS, None, ALU.add).then_inc(var_ready, 1)
                dve.wait_ge(root_ready, 2 * n + 1)
                reciprocal_root(dve, link, var[:, 0:1], root[:, 0:1], rstd[:, 0:1], tmp[:, 0:1])
                if n:
                    dve.wait_ge(turn_done, turn_no["norm", n - 1] + 1)
                link(dve.tensor_scalar(normed[:, :], first[:, :], rstd[:, 0:1], None, ALU.mult))
                dve.sem_inc(normed_ready, 1)

            def residuals(n):
                to = x1[n % 2]
                dve.wait_ge(second_done, n + 1)
                if n >= 2:
                    dve.wait_ge(bias_taken, n - 1)
                dve.wait_ge(residual_ready, n + 1)
                link(dve.tensor_tensor(to[:, :], pY[0:R, :], h[n % 2][:, :], ALU.add))
                dve.sem_inc(second_taken, 1)
                link(dve.bn_stats(stats[:, :], to[:, :]))
                link(dve.bn_aggr(mv[:, :], stats[:, :]))
                dve.tensor_scalar(var[:, 1:2], mv[:, 1:2], EPS, None, ALU.add).then_inc(var_ready, 1)
                dve.wait_ge(root_ready, 2 * n + 2)
                reciprocal_root(dve, link, var[:, 1:2], root[:, 1:2], rstd[:, 1:2], tmp[:, 1:2])
                if n:
                    dve.wait_ge(turn_done, turn_no["z", n - 1] + 1)
                dve.tensor_scalar(z[0:R, :], to[:, :], mv[:, 0:1], rstd[:, 1:2], ALU.subtract, ALU.mult).then_inc(z_ready, 1)

            def route(n):
                dve.wait_ge(routed, n + 1)
                if n:
                    dve.wait_ge(coef_turned, n)
                link(dve.tensor_tensor(scores[:, :], pR[0:R, 0:EXPERTS], bs[0:R, :], ALU.add))
                link(dve.tensor_reduce(top[:, :], scores[:, :], AX.X, ALU.max))
                dve.tensor_scalar(neg_top[:, :], top[:, :], -1.0, None, ALU.mult).then_inc(top_ready, 1)
                link(dve.scalar_tensor_tensor(out=chosen[:, :], in0=scores[:, :], scalar=top[:, 0:1], in1=order[0:R, :],
                                              op0=ALU.is_equal, op1=ALU.mult))
                link(dve.tensor_reduce(top[:, :], chosen[:, :], AX.X, ALU.max))
                link(dve.tensor_scalar(chosen[:, :], chosen[:, :], top[:, 0:1], None, ALU.is_equal))
                dve.wait_ge(expo_ready, n + 1)
                link(dve.reciprocal(total[:, :], total[:, :]))
                link(dve.tensor_scalar(coef[:, :], chosen[:, :], total[:, 0:1], None, ALU.mult))
                dve.sem_inc(coef_ready, 1)
                link(dve.tensor_copy(keep.coef[:, :, n:n + 1], coef[:, :].unsqueeze(2)))

            def add_bias(n):
                dve.wait_ge(bias_done, n + 1)
                dve.tensor_tensor(keep.x[:, n, :], x1[n % 2][:, :], pB[0:R, :], ALU.add).then_inc(bias_taken, 1)

            def split_z(n):
                k = turn_no["z", n]
                dve.wait_ge(turn_copied, k + 1)
                dve.tensor_tensor(keep.zT_lo[:, :, n * P:(n + 1) * P], pT[k % 2][:, :].rearrange("p (c r) -> p c r", c=KC),
                                  keep.zT_hi[:, :, n * P:(n + 1) * P], ALU.subtract).then_inc(zT_lo_ready, 1)

            link(dve.memset(z[:, :], 0.0))
            denominators(0)
            denominators(1)
            for n in range(T + 2):
                if n < T:
                    normalise_first(n)
                if 1 <= n <= T:
                    split_z(n - 1)
                    route(n - 1)
                if n + 2 < T:
                    denominators(n + 2)
                if n >= 2:
                    add_bias(n - 2)
                if n < T:
                    residuals(n)

        @block.scalar
        def _(act):
            def tile_of(what, n):
                act.wait_ge(turn_done, turn_no[what, n] + 1)
                return pT[turn_no[what, n] % 2]

            def copy_att(n):
                bank = tile_of("att", n)
                if n:
                    act.wait_ge(first_done, n)
                act.activation(attT[:, :, :], bank[:, 0:KC * R].rearrange("p (c r) -> p c r", c=KC), ACT.Copy)\
                   .then_inc(turn_copied, 1)

            def copy_z(n):
                bank = tile_of("z", n)
                act.activation(keep.zT_hi[:, :, n * P:(n + 1) * P], bank[:, :].rearrange("p (c r) -> p c r", c=KC), ACT.Copy)\
                   .then_inc(turn_copied, 1)

            def copy_norm(n):
                bank = tile_of("norm", n)
                if n:
                    act.wait_ge(second_done, n)
                for c in range(KC):
                    x = act.activation(normT[:, c, :], bank[:, c * R:(c + 1) * R], ACT.Relu, bias=be_col[:, c:c + 1],
                                       scale=g_col[:, c:c + 1])
                x.then_inc(turn_copied, 1)

            def square_root(n, k):
                act.wait_ge(var_ready, 2 * n + k + 1)
                act.activation(root[:, k:k + 1], var[:, k:k + 1], ACT.Sqrt).then_inc(root_ready, 1)

            def squares(n):
                act.wait_ge(first_ready, n + 1)
                if n:
                    act.wait_ge(squared, n)
                act.activation(square[:, :], first[:, :], ACT.Square, scale=D ** -0.5, accum_out=sumsq[:, :])\
                   .then_inc(squared, 1)

            def exponentials(n):
                act.wait_ge(top_ready, n + 1)
                if n:
                    act.wait_ge(expo_ready, n)
                act.activation(expo[:, :], scores[:, :], ACT.Exp, bias=neg_top[:, 0:1], accum_out=total[:, :])\
                   .then_inc(expo_ready, 1)

            def copy_coefT(n):
                act.wait_ge(coef_turned, n + 1)
                if n:
                    act.wait_ge(bias_done, n)
                act.activation(coefT[:, :], pR[0:EXPERTS, 0:R], ACT.Copy).then_inc(coefT_ready, 1)

            copy_att(0)
            for n in range(T + 1):
                if n < T:
                    squares(n)
                    square_root(n, 0)
                if n:
                    copy_z(n - 1)
                if n < T:
                    copy_norm(n)
                if n:
                    exponentials(n - 1)
                if n + 1 < T:
                    copy_att(n + 1)
                if n:
                    copy_coefT(n - 1)
                if n < T:
                    square_root(n, 1)

        @block.tensor
        def _(pe):
            def turn(what, n, of, produced):
                pe.wait_ge(produced, n + 1)
                k = turn_no[what, n]
                if k >= 2:
                    pe.wait_ge(turn_copied, k - 1)
                    if turns[k - 2][0] == "z":
                        pe.wait_ge(zT_lo_ready, turns[k - 2][1] + 1)
                width = of.shape[0]
                for c in range(KC):
                    mm = pe.transpose(pT[k % 2][:, c * width:(c + 1) * width], of[:, c * P:(c + 1) * P],
                                      keep.ident[0:width, 0:width])
                mm.then_inc(turn_done, 1)

            def first_of_h(n):
                pe.wait_ge(hT_in[n % 2], 16 * (n // 2 + 1))
                if n >= 2:
                    pe.wait_ge(first_ready, n - 1)
                for c in range(KC):
                    pe.matmul(pF[n % 2][0:R, :], hT[n % 2][:, c, :], w1[:, KC + c, :], start=(c == 0), stop=False)

            def first_of_att(n):
                pe.wait_ge(turn_copied, turn_no["att", n] + 1)
                for c in range(KC):
                    mm = pe.matmul(pF[n % 2][0:R, :], attT[:, c, :], w1[:, c, :], start=False, stop=(c == KC - 1))
                mm.then_inc(first_done, 1)

            def second(n):
                pe.wait_ge(turn_copied, turn_no["norm", n] + 1)
                if n:
                    pe.wait_ge(second_taken, n)
                for c in range(KC):
                    mm = pe.matmul(pY[0:R, :], normT[:, c, :], w2[:, c, :], start=(c == 0), stop=(c == KC - 1))
                mm.then_inc(second_done, 1)

            def score(n):
                pe.wait_ge(zT_lo_ready, n + 1)
                if n:
                    pe.wait_ge(coefT_ready, n)
                tokens = slice(n * P, n * P + R)
                for k, part in enumerate((keep.zT_hi, keep.zT_lo)):
                    for c in range(KC):
                        mm = pe.matmul(pR[0:R, 0:EXPERTS], part[:, c, tokens].bitcast(F32), ws[:, c, :],
                                       start=(k == c == 0), stop=(k == 1 and c == KC - 1))
                mm.then_inc(routed, 1)

            def turn_coef(n):
                pe.wait_ge(coef_ready, n + 1)
                pe.transpose(pR[0:EXPERTS, 0:R], coef[:, :], keep.ident[0:R, 0:R]).then_inc(coef_turned, 1)

            def second_bias(n):
                pe.wait_ge(coefT_ready, n + 1)
                if n:
                    pe.wait_ge(bias_taken, n)
                pe.matmul(pB[0:R, :], coefT[:, :], eb2[:, :], start=True, stop=True).then_inc(bias_done, 1)

            first_of_h(0)
            turn("att", 0, att[0], att_ready)
            for n in range(T + 2):
                if n < T:
                    first_of_att(n)
                if n >= 2:
                    second_bias(n - 2)
                if 1 <= n <= T:
                    turn("z", n - 1, z, z_ready)
                if n + 1 < T:
                    first_of_h(n + 1)
                if 1 <= n <= T:
                    score(n - 1)
                if n < T:
                    turn("norm", n, normed, normed_ready)
                if n + 1 < T:
                    turn("att", n + 1, att[(n + 1) % 2], att_ready)
                if n < T:
                    second(n)
                if 1 <= n <= T:
                    turn_coef(n - 1)


def experts(nc, w, keep, out):
    with ExitStack() as ctx:
        m = Memory(nc, ctx, "ffn")
        R = NODE_ROWS
        GROUPS = [(0, 4), (4, 4), (8, 2)]
        WIDEST = 4
        NG = len(GROUPS)
        UNITS = [(e, g) for e in range(EXPERTS) for g in range(NG)]
        w1, w2 = keep.expert_w1, keep.expert_w2
        w1_hi, w1_lo = ([m.sb(f"w1_{x}{s}", [P, KC, FF], F32R) for s in range(2)] for x in ("hi", "lo"))
        w2_hi, w2_lo = ([m.sb(f"w2_{x}{s}", [P, FC, D], F32R) for s in range(2)] for x in ("hi", "lo"))
        b1 = m.sb("b1", [P, EXPERTS, FC])
        hid = m.sb("hid", [P, FC, WIDEST * P])
        hid_hi, hid_lo = ([m.sb(f"hid_{x}{b}", [P, FC, WIDEST * P], F32R) for b in range(2)] for x in ("hi", "lo"))
        pH = [m.ps(f"pH{f}") for f in range(FC)]
        pY = [m.ps(f"pY{b}") for b in range(4)]
        b1_in = m.sem("b1_in")
        w1_in = m.sem("w1_in")
        w2_in = m.sem("w2_in")
        w_hi_ready = m.sem("w_hi_ready")
        w_lo_ready = m.sem("w_lo_ready")
        hid_done = m.sem("hid_done")
        gelu_done = m.sem("gelu_done")
        hid_hi_ready = m.sem("hid_hi_ready")
        hid_lo_ready = m.sem("hid_lo_ready")
        out_done = m.sem("out_done")
        added = m.sem("added")
        stored = m.sem("stored")
        block = ctx.enter_context(nc.Block())

        @block.sync
        def _(sp):
            sp.dma_start(b1[:, :, :], w["b1"].rearrange("e (c p) -> p e c", p=P), allow_slow_non_contiguous=True).then_inc(b1_in, 16)
            for e in range(1, EXPERTS):
                sp.wait_ge(w_lo_ready, 2 * e)
                sp.dma_start(w1[:, :, :], w["W1"][e].rearrange("(r p) n -> p r n", p=P)).then_inc(w1_in, 16)
                sp.dma_start(w2[:, :, :], w["W2"][e].rearrange("(r p) n -> p r n", p=P)).then_inc(w2_in, 16)
            for t in range(NODE_TILES):
                sp.wait_ge(added, (EXPERTS - 1) * NODE_TILES + t + 1)
                sp.dma_start(out[t * R:(t + 1) * R, :], keep.x[:, t, :]).then_inc(stored, 16)
            sp.wait_ge(stored, NODE_TILES * 16)

        @block.scalar
        def _(act):
            def split_expert(e):
                for whole, hi, arrived in ((w1, w1_hi, w1_in), (w2, w2_hi, w2_in)):
                    if e:
                        act.wait_ge(arrived, 16 * e)
                    else:
                        act.wait_ge(keep.expert_in, 32)
                    if e >= 2:
                        act.wait_ge(out_done, (e - 1) * NODE_TILES)
                    act.activation(hi[e % 2][:, :, :], whole[:, :, :], ACT.Copy).then_inc(w_hi_ready, 1)

            split_expert(0)
            act.wait_ge(b1_in, 16)
            for u, (e, g) in enumerate(UNITS):
                n = GROUPS[g][1]
                for f in range(FC):
                    act.wait_ge(hid_done, u * FC + f + 1)
                    if u:
                        act.wait_ge(hid_lo_ready, u)
                    act.activation(hid[:, f, 0:n * P], pH[f][:, 0:n * P], ACT.Gelu, bias=b1[:, e, f:f + 1]).then_inc(gelu_done, 1)
                act.wait_ge(gelu_done, FC * (u + 1))
                if u >= 2:
                    e2, g2 = UNITS[u - 2]
                    act.wait_ge(out_done, e2 * NODE_TILES + sum(GROUPS[g2]))
                act.activation(hid_hi[u % 2][:, :, 0:n * P], hid[:, :, 0:n * P], ACT.Copy).then_inc(hid_hi_ready, 1)
                if g == 0 and e + 1 < EXPERTS:
                    split_expert(e + 1)

        @block.vector
        def _(dve):
            def split_expert(e):
                for k, (whole, hi, lo) in enumerate(((w1, w1_hi, w1_lo), (w2, w2_hi, w2_lo))):
                    dve.wait_ge(w_hi_ready, 2 * e + k + 1)
                    dve.tensor_tensor(lo[e % 2][:, :, :], whole[:, :, :], hi[e % 2][:, :, :], ALU.subtract).then_inc(w_lo_ready, 1)

            def split_hidden(u):
                n = GROUPS[UNITS[u][1]][1]
                dve.wait_ge(hid_hi_ready, u + 1)
                dve.tensor_tensor(hid_lo[u % 2][:, :, 0:n * P], hid[:, :, 0:n * P], hid_hi[u % 2][:, :, 0:n * P], ALU.subtract)\
                   .then_inc(hid_lo_ready, 1)

            split_expert(0)
            split_hidden(0)
            for u, (e, g) in enumerate(UNITS):
                t0, n = GROUPS[g]
                for t in range(t0, t0 + n):
                    k = e * NODE_TILES + t
                    dve.wait_ge(out_done, k + 1)
                    if e:
                        dve.wait_ge(added, k + 1 - NODE_TILES)
                    dve.scalar_tensor_tensor(out=keep.x[:, t, :], in0=pY[k % 4][0:R, :], scalar=keep.coef[:, e, t:t + 1],
                                             in1=keep.x[:, t, :], op0=ALU.mult, op1=ALU.add).then_inc(added, 1)
                    if t == t0 and u + 1 < len(UNITS):
                        split_hidden(u + 1)
                if g == 0 and e + 1 < EXPERTS:
                    split_expert(e + 1)

        @block.tensor
        def _(pe):
            def hidden(u):
                e, g = UNITS[u]
                t0, n = GROUPS[g]
                tokens = slice(t0 * P, (t0 + n) * P)
                if g == 0:
                    pe.wait_ge(w_lo_ready, 2 * e + 2)
                for f in range(FC):
                    if u:
                        pe.wait_ge(gelu_done, (u - 1) * FC + f + 1)
                    feats = slice(f * P, (f + 1) * P)
                    for c in range(KC):
                        for k, (a, b) in enumerate(((w1_hi, keep.zT_hi), (w1_hi, keep.zT_lo), (w1_lo, keep.zT_hi))):
                            mm = pe.matmul(pH[f][:, 0:n * P], a[e % 2][:, c, feats], b[:, c, tokens],
                                           start=(c == k == 0), stop=(c == KC - 1 and k == 2))
                    mm.then_inc(hid_done, 1)

            def output(u):
                e, g = UNITS[u]
                t0, n = GROUPS[g]
                pe.wait_ge(hid_lo_ready, u + 1)
                for t in range(t0, t0 + n):
                    k = e * NODE_TILES + t
                    if k >= 4:
                        pe.wait_ge(added, k - 3)
                    tokens = slice((t - t0) * P, (t - t0 + 1) * P)
                    for f in range(FC):
                        for p, (a, b) in enumerate(((hid_hi, w2_hi), (hid_hi, w2_lo), (hid_lo, w2_hi))):
                            mm = pe.matmul(pY[k % 4][:, :], a[u % 2][:, f, tokens], b[e % 2][:, f, :],
                                           start=(f == p == 0), stop=(f == FC - 1 and p == 2))
                    mm.then_inc(out_done, 1)

            hidden(0)
            for u in range(len(UNITS)):
                if u + 1 < len(UNITS):
                    hidden(u + 1)
                output(u)


class Tables:

    def __init__(self, nc):
        def table(name, shape):
            return nc.dram_tensor(name, shape, F32, kind="Internal").ap()

        self.dst_rows = table("dst_rows", [EDGE_TILES, P])
        self.table = [table(f"first_layer_{x}", [NODES, D]) for x in "kv"]
        self.query = table("query", [NODES, Q_W])
        self.hT = table("hT", [NODE_TILES, P, KC * NODE_ROWS])
        self.h = table("h", [NODES, D])
        self.logits = table("logits", [PLACES, L_W])
        self.expo = table("expo", [PLACES, HEADS])
        self.sums = [table(f"sums{t}", [SUM_ROWS, SUM_W]) for t in range(SUM_TABLES)]


class Keep:

    def __init__(self, m):
        self.ident = m.sb("ident", [P, P])
        self.x = m.sb("x", [NODE_ROWS, NODE_TILES, D])
        self.coef = m.sb("coef", [NODE_ROWS, EXPERTS, NODE_TILES])
        self.src_i = m.sb("src_i", [P, EDGE_TILES], I32)
        self.dst_i = m.sb("dst_i", [P, EDGE_TILES], I32)
        self.dst_f = m.sb("dst_f", [P, EDGE_TILES])
        self.sum_i = m.sb("sum_i", [P, EDGE_TILES], I32)
        self.place_i = m.sb("place_i", [P, EDGE_TILES], I32)
        self.in_rank = m.sb("in_rank", [P, EDGE_TILES])
        self.w1e = {x: m.sb(f"w1e_{x}", [P, D]) for x in "kv"}
        self.x_loaded = m.sem("x_loaded")
        self.pool_passed = m.sem("pool_passed")

    def for_experts(self, m):
        self.zT_hi = m.sb("zT_hi", [P, KC, NODE_TILES * P], F32R)
        self.zT_lo = m.sb("zT_lo", [P, KC, NODE_TILES * P], F32R)
        self.expert_w1 = m.sb("expert_w1", [P, KC, FF])
        self.expert_w2 = m.sb("expert_w2", [P, FC, D])
        self.expert_in = m.sem("expert_in")

    def for_nodes(self, m):
        self.x_mv = m.sb("x_mv", [NODE_ROWS, NODE_TILES, 2])
        self.x_rstd = m.sb("x_rstd", [NODE_ROWS, NODE_TILES])
        self.w1_hi = {x: m.sb(f"w1_hi_{x}", [P, KC, D], F32R) for x in "kvq"}
        self.w1_lo = {x: m.sb(f"w1_lo_{x}", [P, KC, D], F32R) for x in "kvq"}
        self.b1 = {x: m.sb(f"b1_{x}", [P, D]) for x in "kvq"}
        self.be_q = m.sb("be_q", [P, KC])
        self.g_col_q = m.sb("g_col_q", [P, KC])
        self.b2q = m.sb("b2q", [P, D])
        self.b2k = m.sb("b2k", [P, D])


class Late:

    def __init__(self, m):
        self.w1 = m.sb("w1", [P, 2 * KC, D])
        self.b1 = m.sb("b1", [P, D])
        self.w2 = m.sb("w2", [P, KC, D])
        self.b2 = m.sb("b2", [P, D])
        self.b2v = m.sb("b2v", [P, D])
        self.g_col = m.sb("g_col", [P, KC])
        self.be_col = m.sb("be_col", [P, KC])
        self.ws = m.sb("ws", [P, KC, EXPERTS])
        self.bs = m.sb("bs", [P, EXPERTS])
        self.eb2 = m.sb("eb2", [EXPERTS, D])


def build(nc, w, out):
    dram = Tables(nc)
    with ExitStack() as ctx:
        keep = Keep(Memory(nc, ctx, "keep"))
        with ExitStack() as early:
            keep.for_nodes(Memory(nc, early, "early"))
            prepare_weights(nc, w, keep, dram)
            node_tables(nc, w, keep, dram)
        edge_phase(nc, w, keep, dram, values=False)
        late = Late(Memory(nc, ctx, "late"))
        segment_softmax(nc, w, keep, late, dram)
        edge_phase(nc, w, keep, dram, values=True)
        keep.for_experts(Memory(nc, ctx, "tokens"))
        node_output(nc, w, keep, late, dram)
        experts(nc, w, keep, out)


_GNN = [f"{x}_{y}" for x in ("hk", "hv", "hq", "no") for y in ("W1", "b1", "g", "be", "W2", "b2")]
_FFN = ["Ws", "bs", "W1", "b1", "W2", "b2"]
_NAMES = {"x": "x", "src": "src", "dst": "dst", "edge_attr_128": "edge_attr_128",
          **{f"L0_gnn_{x}": x for x in _GNN}, **{f"L0_ffn_{x}": x for x in _FFN}}


def kernel(**inputs):
    import numpy as _np
    import concourse.bacc as _bacc
    from concourse import mybir as _mybir
    from concourse.bass_utils import run_bass_kernel_spmd as _run

    nc = _bacc.Bacc("TRN2", target_bir_lowering=False, num_devices=1)
    arrays, w = {}, {}
    for name, short in _NAMES.items():
        a = _np.ascontiguousarray(inputs[name])
        arrays[f"in_{name}"] = a
        w[short] = nc.dram_tensor(f"in_{name}", a.shape, _mybir.dt.from_np(a.dtype), kind="ExternalInput").ap()
    out = nc.dram_tensor("out_0", (NODES, D), _mybir.dt.float32, kind="ExternalOutput").ap()
    build(nc, w, out)
    r = _run(nc, [arrays], core_ids=[0])
    return r.results[0]["out_0"]
```
